# Optimizing a Trainium2 kernel written in Bass

```python
import numpy as np
import jax
import jax.numpy as jnp

def _softmax(x, axis=-1):
    return jax.nn.softmax(x, axis=axis)

def _gelu(x):
    return jax.nn.gelu(x, approximate=True)

def _silu(x):
    return jax.nn.silu(x)

def _sigmoid(x):
    return jax.nn.sigmoid(x)

def _layernorm(x, axis=-1, eps=1e-05):
    m = jnp.mean(x, axis=axis, keepdims=True)
    v = jnp.var(x, axis=axis, keepdims=True)
    return (x - m) / jnp.sqrt(v + eps)

def _scatter_add(tgt, idx, src, axis=0):
    return tgt.at[idx].add(src)

def _segment_sum(src, seg, n):
    return jax.ops.segment_sum(src, seg, n)
kernel_name = 'mk_seq_preln_d2_jaxref_r8_517178'

def setup_inputs(seed: int=0):
    np.random.seed(seed)
    _w = jnp.asarray

    def _L0_attn_setup():
        import jax, jax.numpy as jnp
        import numpy as np
        from jax import lax
        B, T, H = (4, 256, 128)
        HU = 4 * H
        LAYERS, INDEX = (12, 0)
        K_CLAMP, K_EPS = (60.0, 1e-08)
        LN_EPS = 1e-05

        def _ln(x, g, b):
            m = jnp.mean(x, -1, keepdims=True)
            v = jnp.mean((x - m) ** 2, -1, keepdims=True)
            return (x - m) / jnp.sqrt(v + LN_EPS) * g + b

        def _shift(x):
            return jnp.pad(x[:, :-1], ((0, 0), (1, 0), (0, 0)))

        def _wkv(k, kv, decay, first):

            def step(carry, inp):
                sk, skv = carry
                kt, kvt = inp
                out = (first * kt + sk, first * kvt + skv)
                return ((kt + decay * sk, kvt + decay * skv), out)
            b = k.shape[0]
            init = (jnp.zeros((b, k.shape[2]), k.dtype), jnp.zeros((b, k.shape[2]), k.dtype))
            _, (wk, wkv) = lax.scan(step, init, (jnp.swapaxes(k, 0, 1), jnp.swapaxes(kv, 0, 1)))
            return (jnp.swapaxes(wk, 0, 1), jnp.swapaxes(wkv, 0, 1))
        key = jax.random.key(seed)
        ks = jax.random.split(key, 9)
        s = 0.02
        tr01 = INDEX / (LAYERS - 1)
        tr1pz = 1.0 - INDEX / LAYERS
        i_h = np.arange(H, dtype=np.float64) / H
        i_hu = np.arange(HU, dtype=np.float64)
        decay_speed = -5.0 + 8.0 * (i_hu / (HU - 1)) ** (0.7 + 1.3 * tr01)
        zigzag = ((np.arange(HU) + 1) % 3 - 1) * 0.5
        time_first = np.log(0.3) + zigzag
        f32 = lambda a: jnp.asarray(a, jnp.float32)
        return {'x': jax.random.normal(ks[0], (B, T, H), jnp.float32), 'ln0_g': jnp.ones((H,), jnp.float32), 'ln0_b': jnp.zeros((H,), jnp.float32), 'pre_g': jnp.ones((H,), jnp.float32), 'pre_b': jnp.zeros((H,), jnp.float32), 'post_g': jnp.ones((H,), jnp.float32), 'post_b': jnp.zeros((H,), jnp.float32), 'tm_decay': f32(decay_speed), 'tm_first': f32(time_first), 'tm_mix_k': f32(i_h ** tr1pz), 'tm_mix_v': f32(i_h ** tr1pz + 0.3 * tr01), 'tm_mix_r': f32(i_h ** (0.5 * tr1pz)), 'tm_Wk': jax.random.normal(ks[1], (H, HU), jnp.float32) * s, 'tm_Wv': jax.random.normal(ks[2], (H, HU), jnp.float32) * s, 'tm_Wr': jax.random.normal(ks[3], (H, HU), jnp.float32) * s, 'tm_Wo': jax.random.normal(ks[4], (HU, H), jnp.float32) * s, 'cm_mix_k': f32(i_h ** tr1pz), 'cm_mix_r': f32(i_h ** tr1pz), 'cm_Wk': jax.random.normal(ks[5], (H, HU), jnp.float32) * s, 'cm_Wv': jax.random.normal(ks[6], (HU, H), jnp.float32) * s, 'cm_Wr': jax.random.normal(ks[7], (H, H), jnp.float32) * s}
    _L0_attn_in = _L0_attn_setup()

    def _L0_ffn_setup():
        import jax, jax.numpy as jnp
        import numpy as np
        D_MODEL = 128
        EXPANSION = 4
        D_HIDDEN = D_MODEL * EXPANSION
        NUM_STAGES = int(np.log2(D_HIDDEN))

        def butterfly(y, weights, dim):
            lead = y.shape[:-1]
            for stage in range(weights.shape[0]):
                s = 2 ** stage
                nb = dim // (2 * s)
                yr = y.reshape(*lead, nb, 2, s)
                a = yr[..., 0, :]
                b = yr[..., 1, :]
                w = weights[stage].reshape(nb, s, 2, 2)
                na = w[..., 0, 0] * a + w[..., 0, 1] * b
                nb2 = w[..., 1, 0] * a + w[..., 1, 1] * b
                y = jnp.stack([na, nb2], axis=-2).reshape(*lead, dim)
            return y
        key = jax.random.key(seed)
        ks = jax.random.split(key, 6)
        B, S = (4, 256)
        x = jax.random.normal(ks[0], (B, S, D_MODEL), jnp.float32)
        W_exp = jax.random.normal(ks[1], (D_MODEL, D_HIDDEN), jnp.float32) * 0.02
        b_exp = jnp.zeros((D_HIDDEN,), jnp.float32)
        up_weights = jax.random.normal(ks[2], (NUM_STAGES, D_HIDDEN // 2, 2, 2), jnp.float32) * 0.02
        up_bias = jnp.zeros((D_HIDDEN,), jnp.float32)
        down_weights = jax.random.normal(ks[3], (NUM_STAGES, D_HIDDEN // 2, 2, 2), jnp.float32) * 0.02
        W_con = jax.random.normal(ks[4], (D_HIDDEN, D_MODEL), jnp.float32) * 0.02
        b_con = jnp.zeros((D_MODEL,), jnp.float32)
        down_bias = jnp.zeros((D_MODEL,), jnp.float32)
        return dict(x=x, W_exp=W_exp, b_exp=b_exp, up_weights=up_weights, up_bias=up_bias, down_weights=down_weights, W_con=W_con, b_con=b_con, down_bias=down_bias)
    _L0_ffn_in = _L0_ffn_setup()

    def _L1_attn_setup():
        import jax, jax.numpy as jnp
        import numpy as np
        B, M, D, H, K, V = (4, 256, 128, 16, 64, 64)
        key = jax.random.key(seed)
        ks = jax.random.split(key, 5)
        return {'x': jax.random.normal(ks[0], (B, M, D), dtype=jnp.float32), 'P_q': jax.random.normal(ks[1], (H, D, K), dtype=jnp.float32) * 0.02, 'P_k': jax.random.normal(ks[2], (H, D, K), dtype=jnp.float32) * 0.02, 'P_v': jax.random.normal(ks[3], (H, D, V), dtype=jnp.float32) * 0.02, 'P_o': jax.random.normal(ks[4], (H, D, V), dtype=jnp.float32) * 0.02}
    _L1_attn_in = _L1_attn_setup()

    def _L1_ffn_setup():
        import jax, jax.numpy as jnp
        import numpy as np
        DIM = 128
        DEPTH = 6
        HEADS = 16
        DIM_HEAD = 64
        WINDOW = 32
        INNER = HEADS * DIM_HEAD
        DIM_INNER = int(DIM * 4 * 2 / 3)
        QK_SCALE = 8.0

        def shift_tokens(t):
            a, s = jnp.split(t, 2, -1)
            s = jnp.pad(s, ((0, 0), (1, 0), (0, 0)))[:, :-1]
            return jnp.concatenate([a, s], -1)

        def l2norm(t):
            return t / jnp.maximum(jnp.linalg.norm(t, axis=-1, keepdims=True), 1e-12)

        def rotate_half(x):
            x1, x2 = jnp.split(x, 2, -1)
            return jnp.concatenate([-x2, x1], -1)

        def rotary_tables(n):
            half = jnp.arange(0, DIM_HEAD, 2, dtype=jnp.float32)
            inv_freq = 1.0 / 10000.0 ** (half / DIM_HEAD)
            t = jnp.arange(n, dtype=jnp.float32)
            freqs = t[:, None] * inv_freq[None, :]
            freqs = jnp.concatenate([freqs, freqs], -1)
            base_scale = (half + 0.4 * DIM_HEAD) / (1.4 * DIM_HEAD)
            power = (t - n // 2) / (WINDOW // 2)
            scale = base_scale[None, :] ** power[:, None]
            scale = jnp.concatenate([scale, scale], -1)
            return (freqs, scale)

        def local_attention(q, k, v):
            b, h, n, d = q.shape
            w = WINDOW
            nw = n // w
            bq = q.reshape(b, h, nw, w, d)
            bk = k.reshape(b, h, nw, w, d)
            bv = v.reshape(b, h, nw, w, d)

            def look(t):
                p = jnp.pad(t, ((0, 0), (0, 0), (1, 0), (0, 0), (0, 0)))
                return jnp.concatenate([p[:, :, :nw], p[:, :, 1:]], axis=3)
            bk2, bv2 = (look(bk), look(bv))
            seq = jnp.arange(n).reshape(nw, w)
            seq_p = jnp.pad(seq, ((1, 0), (0, 0)), constant_values=-1)
            jt = jnp.concatenate([seq_p[:nw], seq_p[1:]], axis=1)
            it = seq[:, :, None]
            jb = jt[:, None, :]
            mask = (it < jb) | (it > jb + w) | (jb == -1)
            sim = jnp.einsum('bhwie,bhwje->bhwij', bq, bk2) * QK_SCALE
            sim = jnp.where(mask, -jnp.finfo(sim.dtype).max, sim)
            attn = jax.nn.softmax(sim, -1)
            out = jnp.einsum('bhwij,bhwje->bhwie', attn, bv2)
            return out.reshape(b, h, n, d)

        def attn_layer(x, Wqkv, qs, ksc, Wo):
            b, n, _ = x.shape
            qkv = x @ Wqkv
            q, k, v = jnp.split(qkv, 3, -1)
            sh = lambda t: t.reshape(b, n, HEADS, DIM_HEAD).transpose(0, 2, 1, 3)
            q, k, v = (sh(q), sh(k), sh(v))
            q = l2norm(q) * qs
            k = l2norm(k) * ksc
            freqs, scale = rotary_tables(n)
            cos, sin = (jnp.cos(freqs), jnp.sin(freqs))
            q = q * cos * scale + rotate_half(q) * sin * scale
            inv = 1.0 / scale
            k = k * cos * inv + rotate_half(k) * sin * inv
            out = local_attention(q, k, v)
            out = out.transpose(0, 2, 1, 3).reshape(b, n, INNER)
            return out @ Wo

        def ffn_layer(x, g, bln, W1, b1, W2, b2):
            mu = x.mean(-1, keepdims=True)
            var = ((x - mu) ** 2).mean(-1, keepdims=True)
            xn = (x - mu) / jnp.sqrt(var + 1e-05) * g + bln
            hg = xn @ W1 + b1
            a, gate = jnp.split(hg, 2, -1)
            return a * jax.nn.gelu(gate, approximate=False) @ W2 + b2
        key = jax.random.key(seed)
        ks = jax.random.split(key, 8)
        B, N = (2, 256)
        init = lambda k, shape: jax.random.normal(k, shape, jnp.float32) * 0.02
        return {'x': jax.random.normal(ks[0], (B, N, DIM), jnp.float32), 'Wqkv': init(ks[1], (DEPTH, DIM, 3 * INNER)), 'q_scale': jnp.ones((DEPTH, DIM_HEAD), jnp.float32), 'k_scale': jnp.ones((DEPTH, DIM_HEAD), jnp.float32), 'Wo': init(ks[2], (DEPTH, INNER, DIM)), 'ln_g': jnp.ones((DEPTH, DIM), jnp.float32), 'ln_b': jnp.zeros((DEPTH, DIM), jnp.float32), 'W1': init(ks[3], (DEPTH, DIM, 2 * DIM_INNER)), 'b1': jnp.zeros((DEPTH, 2 * DIM_INNER), jnp.float32), 'W2': init(ks[4], (DEPTH, DIM_INNER, DIM)), 'b2': jnp.zeros((DEPTH, DIM), jnp.float32)}
    _L1_ffn_in = _L1_ffn_setup()
    _d = {'L0_attn_x': _L0_attn_in['x'], 'L0_attn_ln0_g': _L0_attn_in['ln0_g'], 'L0_attn_ln0_b': _L0_attn_in['ln0_b'], 'L0_attn_pre_g': _L0_attn_in['pre_g'], 'L0_attn_pre_b': _L0_attn_in['pre_b'], 'L0_attn_post_g': _L0_attn_in['post_g'], 'L0_attn_post_b': _L0_attn_in['post_b'], 'L0_attn_tm_decay': _L0_attn_in['tm_decay'], 'L0_attn_tm_first': _L0_attn_in['tm_first'], 'L0_attn_tm_mix_k': _L0_attn_in['tm_mix_k'], 'L0_attn_tm_mix_v': _L0_attn_in['tm_mix_v'], 'L0_attn_tm_mix_r': _L0_attn_in['tm_mix_r'], 'L0_attn_tm_Wk': _L0_attn_in['tm_Wk'], 'L0_attn_tm_Wv': _L0_attn_in['tm_Wv'], 'L0_attn_tm_Wr': _L0_attn_in['tm_Wr'], 'L0_attn_tm_Wo': _L0_attn_in['tm_Wo'], 'L0_attn_cm_mix_k': _L0_attn_in['cm_mix_k'], 'L0_attn_cm_mix_r': _L0_attn_in['cm_mix_r'], 'L0_attn_cm_Wk': _L0_attn_in['cm_Wk'], 'L0_attn_cm_Wv': _L0_attn_in['cm_Wv'], 'L0_attn_cm_Wr': _L0_attn_in['cm_Wr'], 'L0_ffn_W_exp': _L0_ffn_in['W_exp'], 'L0_ffn_b_exp': _L0_ffn_in['b_exp'], 'L0_ffn_up_weights': _L0_ffn_in['up_weights'], 'L0_ffn_up_bias': _L0_ffn_in['up_bias'], 'L0_ffn_down_weights': _L0_ffn_in['down_weights'], 'L0_ffn_W_con': _L0_ffn_in['W_con'], 'L0_ffn_b_con': _L0_ffn_in['b_con'], 'L0_ffn_down_bias': _L0_ffn_in['down_bias'], 'L1_attn_P_q': _L1_attn_in['P_q'], 'L1_attn_P_k': _L1_attn_in['P_k'], 'L1_attn_P_v': _L1_attn_in['P_v'], 'L1_attn_P_o': _L1_attn_in['P_o'], 'L1_ffn_Wqkv': _L1_ffn_in['Wqkv'], 'L1_ffn_q_scale': _L1_ffn_in['q_scale'], 'L1_ffn_k_scale': _L1_ffn_in['k_scale'], 'L1_ffn_Wo': _L1_ffn_in['Wo'], 'L1_ffn_ln_g': _L1_ffn_in['ln_g'], 'L1_ffn_ln_b': _L1_ffn_in['ln_b'], 'L1_ffn_W1': _L1_ffn_in['W1'], 'L1_ffn_b1': _L1_ffn_in['b1'], 'L1_ffn_W2': _L1_ffn_in['W2'], 'L1_ffn_b2': _L1_ffn_in['b2']}
    _x0 = _d['L0_attn_x']
    _d['L0_attn_x'] = jax.random.normal(jax.random.fold_in(jax.random.key(seed), 1), (8, 512, 128), dtype=_x0.dtype)
    del _x0
    return _d

def reference(L0_attn_x, L0_attn_ln0_g, L0_attn_ln0_b, L0_attn_pre_g, L0_attn_pre_b, L0_attn_post_g, L0_attn_post_b, L0_attn_tm_decay, L0_attn_tm_first, L0_attn_tm_mix_k, L0_attn_tm_mix_v, L0_attn_tm_mix_r, L0_attn_tm_Wk, L0_attn_tm_Wv, L0_attn_tm_Wr, L0_attn_tm_Wo, L0_attn_cm_mix_k, L0_attn_cm_mix_r, L0_attn_cm_Wk, L0_attn_cm_Wv, L0_attn_cm_Wr, L0_ffn_W_exp, L0_ffn_b_exp, L0_ffn_up_weights, L0_ffn_up_bias, L0_ffn_down_weights, L0_ffn_W_con, L0_ffn_b_con, L0_ffn_down_bias, L1_attn_P_q, L1_attn_P_k, L1_attn_P_v, L1_attn_P_o, L1_ffn_Wqkv, L1_ffn_q_scale, L1_ffn_k_scale, L1_ffn_Wo, L1_ffn_ln_g, L1_ffn_ln_b, L1_ffn_W1, L1_ffn_b1, L1_ffn_W2, L1_ffn_b2):

    def _L0_attn_ref(x, ln0_g, ln0_b, pre_g, pre_b, post_g, post_b, tm_decay, tm_first, tm_mix_k, tm_mix_v, tm_mix_r, tm_Wk, tm_Wv, tm_Wr, tm_Wo, cm_mix_k, cm_mix_r, cm_Wk, cm_Wv, cm_Wr):
        import jax, jax.numpy as jnp
        import numpy as np
        from jax import lax
        B, T, H = (4, 256, 128)
        HU = 4 * H
        LAYERS, INDEX = (12, 0)
        K_CLAMP, K_EPS = (60.0, 1e-08)
        LN_EPS = 1e-05

        def _ln(x, g, b):
            m = jnp.mean(x, -1, keepdims=True)
            v = jnp.mean((x - m) ** 2, -1, keepdims=True)
            return (x - m) / jnp.sqrt(v + LN_EPS) * g + b

        def _shift(x):
            return jnp.pad(x[:, :-1], ((0, 0), (1, 0), (0, 0)))

        def _wkv(k, kv, decay, first):

            def step(carry, inp):
                sk, skv = carry
                kt, kvt = inp
                out = (first * kt + sk, first * kvt + skv)
                return ((kt + decay * sk, kvt + decay * skv), out)
            b = k.shape[0]
            init = (jnp.zeros((b, k.shape[2]), k.dtype), jnp.zeros((b, k.shape[2]), k.dtype))
            _, (wk, wkv) = lax.scan(step, init, (jnp.swapaxes(k, 0, 1), jnp.swapaxes(kv, 0, 1)))
            return (jnp.swapaxes(wk, 0, 1), jnp.swapaxes(wkv, 0, 1))
        if INDEX == 0:
            x = _ln(x, ln0_g, ln0_b)
        xn = _ln(x, pre_g, pre_b)
        xx = _shift(xn)
        xk = xn * tm_mix_k + xx * (1.0 - tm_mix_k)
        xv = xn * tm_mix_v + xx * (1.0 - tm_mix_v)
        xr = xn * tm_mix_r + xx * (1.0 - tm_mix_r)
        k = jnp.exp(jnp.minimum(xk @ tm_Wk, K_CLAMP))
        v = xv @ tm_Wv
        r = xr @ tm_Wr
        kv = k * v
        decay = jnp.exp(-jnp.exp(tm_decay))
        first = jnp.exp(tm_first)
        wk, wkv = _wkv(k, kv, decay, first)
        rwkv = jax.nn.sigmoid(r) * (wkv / (wk + K_EPS))
        x = x + rwkv @ tm_Wo
        xn = _ln(x, post_g, post_b)
        xx = _shift(xn)
        xk = xn * cm_mix_k + xx * (1.0 - cm_mix_k)
        xr = xn * cm_mix_r + xx * (1.0 - cm_mix_r)
        kv = jax.nn.silu(xk @ cm_Wk) @ cm_Wv
        x = x + (jax.nn.sigmoid(xr @ cm_Wr) + kv)
        return x

    def _L0_ffn_ref(x, W_exp, b_exp, up_weights, up_bias, down_weights, W_con, b_con, down_bias):
        import jax, jax.numpy as jnp
        import numpy as np
        D_MODEL = 128
        EXPANSION = 4
        D_HIDDEN = D_MODEL * EXPANSION
        NUM_STAGES = int(np.log2(D_HIDDEN))

        def butterfly(y, weights, dim):
            lead = y.shape[:-1]
            for stage in range(weights.shape[0]):
                s = 2 ** stage
                nb = dim // (2 * s)
                yr = y.reshape(*lead, nb, 2, s)
                a = yr[..., 0, :]
                b = yr[..., 1, :]
                w = weights[stage].reshape(nb, s, 2, 2)
                na = w[..., 0, 0] * a + w[..., 0, 1] * b
                nb2 = w[..., 1, 0] * a + w[..., 1, 1] * b
                y = jnp.stack([na, nb2], axis=-2).reshape(*lead, dim)
            return y
        h = jnp.einsum('bsd,dh->bsh', x, W_exp) + b_exp
        h = butterfly(h, up_weights, D_HIDDEN)
        h = jax.nn.gelu(h + up_bias, approximate=False)
        h = butterfly(h, down_weights, D_HIDDEN)
        y = jnp.einsum('bsh,hd->bsd', h, W_con) + b_con
        return y + down_bias

    def _L1_attn_ref(x, P_q, P_k, P_v, P_o):
        import jax, jax.numpy as jnp
        import numpy as np
        B, M, D, H, K, V = (4, 256, 128, 16, 64, 64)
        Q = jnp.einsum('bmd,hdk->bhmk', x, P_q)
        Kt = jnp.einsum('bmd,hdk->bhmk', x, P_k)
        Vt = jnp.einsum('bmd,hdv->bhmv', x, P_v)
        scale = 1.0 / jnp.sqrt(jnp.asarray(K, dtype=x.dtype))
        logits = jnp.einsum('bhmk,bhnk->bhmn', Q, Kt) * scale
        m = logits.shape[-1]
        causal = jnp.tril(jnp.ones((m, m), dtype=bool))
        logits = jnp.where(causal[None, None], logits, jnp.asarray(-jnp.inf, dtype=logits.dtype))
        weights = jax.nn.softmax(logits, axis=-1)
        o = jnp.einsum('bhmn,bhnv->bhmv', weights, Vt)
        y = jnp.einsum('bhmv,hdv->bmd', o, P_o)
        return y

    def _L1_ffn_ref(x, Wqkv, q_scale, k_scale, Wo, ln_g, ln_b, W1, b1, W2, b2):
        import jax, jax.numpy as jnp
        import numpy as np
        DIM = 128
        DEPTH = 6
        HEADS = 16
        DIM_HEAD = 64
        WINDOW = 32
        INNER = HEADS * DIM_HEAD
        DIM_INNER = int(DIM * 4 * 2 / 3)
        QK_SCALE = 8.0

        def shift_tokens(t):
            a, s = jnp.split(t, 2, -1)
            s = jnp.pad(s, ((0, 0), (1, 0), (0, 0)))[:, :-1]
            return jnp.concatenate([a, s], -1)

        def l2norm(t):
            return t / jnp.maximum(jnp.linalg.norm(t, axis=-1, keepdims=True), 1e-12)

        def rotate_half(x):
            x1, x2 = jnp.split(x, 2, -1)
            return jnp.concatenate([-x2, x1], -1)

        def rotary_tables(n):
            half = jnp.arange(0, DIM_HEAD, 2, dtype=jnp.float32)
            inv_freq = 1.0 / 10000.0 ** (half / DIM_HEAD)
            t = jnp.arange(n, dtype=jnp.float32)
            freqs = t[:, None] * inv_freq[None, :]
            freqs = jnp.concatenate([freqs, freqs], -1)
            base_scale = (half + 0.4 * DIM_HEAD) / (1.4 * DIM_HEAD)
            power = (t - n // 2) / (WINDOW // 2)
            scale = base_scale[None, :] ** power[:, None]
            scale = jnp.concatenate([scale, scale], -1)
            return (freqs, scale)

        def local_attention(q, k, v):
            b, h, n, d = q.shape
            w = WINDOW
            nw = n // w
            bq = q.reshape(b, h, nw, w, d)
            bk = k.reshape(b, h, nw, w, d)
            bv = v.reshape(b, h, nw, w, d)

            def look(t):
                p = jnp.pad(t, ((0, 0), (0, 0), (1, 0), (0, 0), (0, 0)))
                return jnp.concatenate([p[:, :, :nw], p[:, :, 1:]], axis=3)
            bk2, bv2 = (look(bk), look(bv))
            seq = jnp.arange(n).reshape(nw, w)
            seq_p = jnp.pad(seq, ((1, 0), (0, 0)), constant_values=-1)
            jt = jnp.concatenate([seq_p[:nw], seq_p[1:]], axis=1)
            it = seq[:, :, None]
            jb = jt[:, None, :]
            mask = (it < jb) | (it > jb + w) | (jb == -1)
            sim = jnp.einsum('bhwie,bhwje->bhwij', bq, bk2) * QK_SCALE
            sim = jnp.where(mask, -jnp.finfo(sim.dtype).max, sim)
            attn = jax.nn.softmax(sim, -1)
            out = jnp.einsum('bhwij,bhwje->bhwie', attn, bv2)
            return out.reshape(b, h, n, d)

        def attn_layer(x, Wqkv, qs, ksc, Wo):
            b, n, _ = x.shape
            qkv = x @ Wqkv
            q, k, v = jnp.split(qkv, 3, -1)
            sh = lambda t: t.reshape(b, n, HEADS, DIM_HEAD).transpose(0, 2, 1, 3)
            q, k, v = (sh(q), sh(k), sh(v))
            q = l2norm(q) * qs
            k = l2norm(k) * ksc
            freqs, scale = rotary_tables(n)
            cos, sin = (jnp.cos(freqs), jnp.sin(freqs))
            q = q * cos * scale + rotate_half(q) * sin * scale
            inv = 1.0 / scale
            k = k * cos * inv + rotate_half(k) * sin * inv
            out = local_attention(q, k, v)
            out = out.transpose(0, 2, 1, 3).reshape(b, n, INNER)
            return out @ Wo

        def ffn_layer(x, g, bln, W1, b1, W2, b2):
            mu = x.mean(-1, keepdims=True)
            var = ((x - mu) ** 2).mean(-1, keepdims=True)
            xn = (x - mu) / jnp.sqrt(var + 1e-05) * g + bln
            hg = xn @ W1 + b1
            a, gate = jnp.split(hg, 2, -1)
            return a * jax.nn.gelu(gate, approximate=False) @ W2 + b2
        for i in range(DEPTH):
            x = attn_layer(shift_tokens(x), Wqkv[i], q_scale[i], k_scale[i], Wo[i]) + x
            x = ffn_layer(shift_tokens(x), ln_g[i], ln_b[i], W1[i], b1[i], W2[i], b2[i]) + x
        return x
    x = L0_attn_x
    x = x + _L0_attn_ref(_layernorm(x, axis=-1), L0_attn_ln0_g, L0_attn_ln0_b, L0_attn_pre_g, L0_attn_pre_b, L0_attn_post_g, L0_attn_post_b, L0_attn_tm_decay, L0_attn_tm_first, L0_attn_tm_mix_k, L0_attn_tm_mix_v, L0_attn_tm_mix_r, L0_attn_tm_Wk, L0_attn_tm_Wv, L0_attn_tm_Wr, L0_attn_tm_Wo, L0_attn_cm_mix_k, L0_attn_cm_mix_r, L0_attn_cm_Wk, L0_attn_cm_Wv, L0_attn_cm_Wr)
    x = x + _L0_ffn_ref(_layernorm(x, axis=-1), L0_ffn_W_exp, L0_ffn_b_exp, L0_ffn_up_weights, L0_ffn_up_bias, L0_ffn_down_weights, L0_ffn_W_con, L0_ffn_b_con, L0_ffn_down_bias)
    x = x + _L1_attn_ref(_layernorm(x, axis=-1), L1_attn_P_q, L1_attn_P_k, L1_attn_P_v, L1_attn_P_o)
    x = x + _L1_ffn_ref(_layernorm(x, axis=-1), L1_ffn_Wqkv, L1_ffn_q_scale, L1_ffn_k_scale, L1_ffn_Wo, L1_ffn_ln_g, L1_ffn_ln_b, L1_ffn_W1, L1_ffn_b1, L1_ffn_W2, L1_ffn_b2)
    return x

_drawn_inputs = setup_inputs


def setup_inputs(seed=0):
    import zlib

    import numpy as np

    out = dict(_drawn_inputs(seed))
    spreads = {'L0_attn_ln0_g': (1.0, 0.2),
     'L0_attn_ln0_b': (0.0, 0.1),
     'L0_attn_pre_g': (1.0, 0.6),
     'L0_attn_pre_b': (0.0, 0.8),
     'L0_attn_post_g': (1.0, 0.6),
     'L0_attn_post_b': (0.0, 0.8),
     'L0_ffn_b_exp': (0.0, 0.1),
     'L0_ffn_up_bias': (0.0, 0.1),
     'L0_ffn_b_con': (0.0, 0.668),
     'L0_ffn_down_bias': (0.0, 0.585),
     'L1_ffn_q_scale': (1.0, 0.6),
     'L1_ffn_k_scale': (1.0, 0.6),
     'L1_ffn_ln_g': (1.0, 0.6),
     'L1_ffn_ln_b': (0.0, 0.8),
     'L1_ffn_b1': (0.0, 0.8),
     'L1_ffn_b2': (0.0, 0.342)}
    factors = {'L0_attn_tm_decay': 6.408,
     'L0_attn_tm_first': 8.0,
     'L0_attn_tm_mix_k': 8.0,
     'L0_attn_tm_mix_v': 8.0,
     'L0_attn_tm_mix_r': 8.0,
     'L0_attn_tm_Wk': 8.0,
     'L0_attn_tm_Wv': 4.099,
     'L0_attn_tm_Wr': 8.0,
     'L0_attn_tm_Wo': 4.114,
     'L0_attn_cm_mix_k': 4.544,
     'L0_attn_cm_mix_r': 13.021,
     'L0_attn_cm_Wk': 2.7,
     'L0_attn_cm_Wv': 2.68,
     'L1_attn_P_q': 8.0,
     'L1_attn_P_k': 8.0,
     'L1_attn_P_v': 5.91,
     'L1_attn_P_o': 5.743,
     'L1_ffn_W1': 5.638,
     'L1_ffn_W2': 5.521}
    for name, (base, spread) in spreads.items():
        noise = np.random.default_rng([zlib.crc32(name.encode()), seed]).standard_normal(out[name].shape)
        drawn = base * np.exp(spread * noise) if base else spread * noise
        out[name] = jnp.asarray(drawn.astype(out[name].dtype))
    for name, factor in factors.items():
        out[name] = (out[name] * factor).astype(out[name].dtype)
    return out
```

```python
from contextlib import ExitStack

import numpy as np

import concourse.bass as bass
from concourse import mybir
from concourse.alu_op_type import AluOpType as ALU

ACT = mybir.ActivationFunctionType
AX = mybir.AxisListType
F32 = mybir.dt.float32
BF16 = mybir.dt.bfloat16

P = 128
B, T, D = 8, 512, 128
TILES = T // P
NT = B * TILES
BANK = 512
HEADS, DH = 16, 64
PAIRS = HEADS // 2
INNER = HEADS * DH
WIN = 32
LAYERS = 6
GATED = 341
CHUNKS = [(0, 128), (128, 128), (256, GATED - 256)]
LN_EPS = 1e-5
NORM_FLOOR = 1e-24
QK_SCALE = 8.0
MASKED = -1e30
LEAD = WIN
SEQ = T + 1
XW = LEAD + B * SEQ


class Memory:

    def __init__(self, nc, ctx, prefix):
        self.nc, self.ctx, self.prefix, self.sems = nc, ctx, prefix, []
        ctx.callback(self.clear)

    def clear(self):
        for sem in self.sems:
            self.nc.gpsimd.sem_clear(sem)
            self.nc.release_semaphore(sem)

    def sb(self, name, shape, dt=F32):
        return self.ctx.enter_context(self.nc.sbuf_tensor(f"{self.prefix}_{name}", shape, dt))

    def bank(self, name):
        return self.ctx.enter_context(self.nc.psum_tensor(f"{self.prefix}_{name}", [P, BANK], F32))

    def sem(self, name):
        self.sems.append(self.nc.alloc_semaphore(f"{self.prefix}_{name}"))
        return self.sems[-1]


class LayerNorm:

    def __init__(self, mem, shared, tok, feat):
        self.tok, self.feat, self.shared = tok, feat, shared
        self.stats = mem.sb("ln_stats", [P, TILES, 6])
        self.both = mem.sb("ln_both", [P, TILES, 3])
        self.gap = mem.sb("ln_gap", [P, TILES])
        self.gap2, self.gap_eps = mem.sb("ln_gap2", [P, TILES]), mem.sb("ln_gap_eps", [P, TILES])
        self.mean = mem.sb("ln_mean", [P, TILES])
        self.vareps = mem.sb("ln_vareps", [P, TILES])
        self.rstd = mem.sb("ln_rstd", [P, TILES])
        self.hat = mem.sb("ln_hat", [P, TILES, P])
        self.turned = mem.sem("ln_turned")
        self.stats_done = mem.sem("ln_stats_done")
        self.steps = mem.sem("ln_steps")
        self.rstd_done = mem.sem("ln_rstd_done")
        self.hat_done = mem.sem("ln_hat_done")
        self.back = mem.sem("ln_back")

    def turn_in(self, pe, m, src):
        pe.wait_ge(self.hat_done, TILES * m)
        for t in range(TILES):
            turn = pe.transpose(self.tok[:, t * P:(t + 1) * P], src[:, t * P:(t + 1) * P], self.shared.ident[:])
        turn.then_inc(self.turned, 1)

    def statistics(self, dve, m, tok=None):
        if tok is None:
            dve.wait_ge(self.turned, m + 1)
            tok = self.tok[:].rearrange("p (t f) -> p t f", t=TILES)
        dve.wait_ge(self.steps, 6 * m)
        for t in range(TILES):
            dve.bn_stats(self.stats[:, t, :], tok[:, t, :]).then_inc(self.stats_done, 1)
        dve.wait_ge(self.stats_done, TILES * m + TILES)
        even, odd = self.stats[:, :, 0:3], self.stats[:, :, 3:6]
        dve.tensor_tensor(self.gap[:], even[:, :, 1], odd[:, :, 1], ALU.subtract).then_inc(self.steps, 1)
        dve.tensor_tensor(self.both[:], even, odd, ALU.add).then_inc(self.steps, 1)
        dve.wait_ge(self.steps, 6 * m + 1)
        dve.tensor_tensor(self.gap2[:], self.gap[:], self.gap[:], ALU.mult).then_inc(self.steps, 1)
        dve.wait_ge(self.steps, 6 * m + 2)
        dve.wait_ge(self.hat_done, TILES * m)
        dve.tensor_scalar(self.mean[:], self.both[:, :, 1], 0.5, None, ALU.mult).then_inc(self.steps, 1)
        dve.wait_ge(self.steps, 6 * m + 3)
        dve.tensor_scalar(self.gap_eps[:], self.gap2[:], 0.25, LN_EPS, ALU.mult, ALU.add).then_inc(self.steps, 1)
        dve.wait_ge(self.steps, 6 * m + 5)
        dve.wait_ge(self.rstd_done, m)
        dve.scalar_tensor_tensor(self.vareps[:], self.both[:, :, 2], 1.0 / P, self.gap_eps[:],
                                 ALU.mult, ALU.add).then_inc(self.steps, 1)

    def reciprocal_deviation(self, pool, m):
        pool.wait_ge(self.steps, 6 * m + 6)
        pool.wait_ge(self.hat_done, TILES * m)
        pool.tensor_tensor(self.rstd[:], self.vareps[:], self.shared.minus_half[:, 0:TILES],
                           ALU.pow).then_inc(self.rstd_done, 1)

    def normalise(self, dve, m, tok=None, out=None):
        if tok is None:
            tok = self.tok[:].rearrange("p (t f) -> p t f", t=TILES)
        if out is None:
            out = self.hat
        dve.wait_ge(self.rstd_done, m + 1)
        for t in range(TILES):
            dve.tensor_scalar(out[:, t, :], tok[:, t, :], self.mean[:, t:t + 1], self.rstd[:, t:t + 1],
                              ALU.subtract, ALU.mult).then_inc(self.hat_done, 1)

    def turn_back(self, pe, m):
        pe.wait_ge(self.hat_done, TILES * m + TILES)
        for t in range(TILES):
            turn = pe.transpose(self.feat[:, t * P:(t + 1) * P], self.hat[:, t, :], self.shared.ident[:])
        turn.then_inc(self.back, 1)


class Shared:

    def __init__(self, mem):
        self.ident = mem.sb("ident", [P, P])
        self.identb = mem.sb("identb", [P, P], BF16)
        self.minus_half = mem.sb("minus_half", [P, 2 * HEADS])
        self.ones = mem.sb("ones", [P, 1])
        self.w_score = mem.sb("w_score", [P, HEADS, P])
        self.w_value = mem.sb("w_value", [P, HEADS, P])
        self.w_up = mem.sb("w_up", [P, 4 * D])
        self.w_down = mem.sb("w_down", [P, 4, D])
        self.up_bias = mem.sb("up_bias", [P, 4])
        self.down_bias = mem.sb("down_bias", [P, 1])
        self.x0 = mem.sb("x0", [P, XW])
        self.xs = mem.sb("xs", [P, B * T])


def column(tile):
    return tile * P + tile // TILES + (LEAD + 1)


def layers(nc, shared, ins):
    with ExitStack() as ctx:
        mem = Memory(nc, ctx, "lay")
        x0 = shared.x0
        x1 = mem.sb("x1", [P, XW])
        w_qk = mem.sb("w_qk", [P, 2 * INNER])
        w_v = mem.sb("w_v", [P, 2, PAIRS * DH])
        w_o = mem.sb("w_o", [P, PAIRS, P])
        w_1 = mem.sb("w_1", [P, 2 * GATED])
        w_2 = mem.sb("w_2", [P, len(CHUNKS), P])
        vecs = mem.sb("vecs", [P, 9])
        trig = mem.sb("trig", [P, 2, 2, TILES, DH])
        gains = mem.sb("gains", [P, 2, 2, DH])
        cos = mem.sb("cos", [P, 2, TILES, DH])
        sin = mem.sb("sin", [P, 2, TILES, DH])
        mask = mem.sb("mask", [P, TILES, 2 * WIN])
        mask8 = mem.sb("mask8", [P, TILES, PAIRS * 2 * WIN], BF16)
        xt = mem.sb("xt", [P, P])
        xv = mem.sb("xv", [P, WIN + P])
        sq = mem.sb("sq", [P, 2, INNER])
        n2 = mem.sb("n2", [P, 2 * HEADS])
        n2c = mem.sb("n2c", [P, 2 * HEADS])
        rn = mem.sb("rn", [P, 2 * HEADS])
        qkn = mem.sb("qkn", [P, 2, INNER])
        qkr = mem.sb("qkr", [P, 2, INNER])
        qks = mem.sb("qks", [P, 2, INNER])
        qT = mem.sb("qT", [P, PAIRS, P])
        kT = mem.sb("kT", [P, PAIRS, WIN + P])
        probs = mem.sb("probs", [P, PAIRS, 2, 2 * WIN])
        top = mem.sb("top", [P, 2, PAIRS])
        total = mem.sb("total", [P, 2, PAIRS])
        rtotal = mem.sb("rtotal", [P, 2, PAIRS])
        pT = mem.sb("pT", [P, PAIRS, P])
        val = mem.sb("val", [P, TILES, PAIRS * DH])
        att = mem.sb("att", [P, PAIRS, 2, DH])
        aT = mem.sb("aT", [P, PAIRS, P])
        xf = mem.sb("xf", [P, T])
        xn = mem.sb("xn", [P, T])
        gate = mem.sb("gate", [P, len(CHUNKS), T])
        act = mem.sb("act", [P, len(CHUNKS), T])
        qk_ps = [mem.bank(f"qk{j}") for j in range(4)]
        ring = [mem.bank(f"ring{j}") for j in range(4)]
        ln = LayerNorm(mem, shared, ring[0], ring[1])

        s = mem.sem
        const_in = s("const_in")
        qk_in, v_in, o_in, ffn_in, gains_in = s("qk_in"), s("v_in"), s("o_in"), s("ffn_in"), s("gains_in")
        mask_done = s("mask_done")
        kT_clear = s("kT_clear")
        pads_done = s("pads_done")
        x0_first = s("x0_first")
        tables = s("tables")
        xt_ready, xv_ready = s("xt_ready"), s("xv_ready")
        qk_proj = s("qk_proj")
        squared = s("squared")
        norms = s("norms")
        floored, rnorm = s("floored"), s("rnorm")
        normed = s("normed")
        cosed = s("cosed")
        sined_q, sined_k = s("sined_q"), s("sined_k")
        rotated = s("rotated")
        qk_turned = s("qk_turned")
        qT_out, kT_out = s("qT_out"), s("kT_out")
        k_kept = s("k_kept")
        scores = s("scores")
        topped, shifted, summed, inverted = s("topped"), s("shifted"), s("summed"), s("inverted")
        exped = s("exped")
        v_proj, v_out = s("v_proj"), s("v_out")
        p_turned, p_out0, p_out1 = s("p_turned"), s("p_out0"), s("p_out1")
        mixed, att_out = s("mixed"), s("att_out")
        a_turned, aT_out = s("a_turned"), s("aT_out")
        projected, x1_out = s("projected"), s("x1_out")
        xf_ready, xn_ready = s("xf_ready"), s("xn_ready")
        gates, vals = s("gates"), s("vals")
        gelued, gated = s("gelued"), s("gated")
        ffn_out, x0_out = s("ffn_out"), s("x0_out")

        def half_table(w, i, half):
            place = slice(i % TILES, i % TILES + 1) if isinstance(i, int) else bass.ds(i % TILES, 1)
            return sin[:, w, place, 32 * half:32 * half + 32]

        tokens = lambda a, h: a[64 * h:64 * h + 64]
        heads = lambda a: a.rearrange("p (h d) -> p h d", d=DH)
        block = ctx.enter_context(nc.Block())

        @block.sync
        def _(sp):
            sp.dma_start(trig[:], ins["c_trig"]).then_inc(const_in, 16)
            sp.dma_start(mask[:], ins["c_mask"]).then_inc(const_in, 16)
            w_qkv, w_out, w1, w2 = ins["L1_ffn_Wqkv"], ins["L1_ffn_Wo"], ins["L1_ffn_W1"], ins["L1_ffn_W2"]
            with sp.Fori(0, LAYERS) as l:
                one = bass.ds(l, 1)
                sp.wait_ge(tables, 4 * l)
                for side in range(2):
                    for which, name in enumerate(("L1_ffn_q_scale", "L1_ffn_k_scale")):
                        for half in range(2):
                            src = ins[name][one, bass.ds(32 * (half ^ side), 32)]
                            sp.dma_start(gains[:, side, which, 32 * half:32 * half + 32],
                                         src.to_broadcast([P, 32])).then_inc(gains_in, 16)
                sp.wait_ge(qk_proj, 4 * NT * l)
                sp.dma_start(w_qk[:], w_qkv[one, :, 0:2 * INNER].rearrange("o d n -> (o d) n")).then_inc(qk_in, 16)
                sp.wait_ge(v_proj, 4 * NT * l)
                for h in range(2):
                    src = w_qkv[one, :, 2 * INNER:3 * INNER].rearrange("o d (q h v) -> (o d) h q v", h=2, v=DH)
                    sp.dma_start(w_v[:, h, :].rearrange("p (q v) -> p q v", v=DH), src[:, h, :, :]).then_inc(v_in, 16)
                sp.wait_ge(projected, NT * l)
                sp.dma_start(w_o[:], w_out[one].rearrange("o (q p) n -> (o p) q n", p=P)).then_inc(o_in, 16)
                sp.wait_ge(x0_out, B * l)
                sp.dma_start(w_1[:], w1[one].rearrange("o d n -> (o d) n")).then_inc(ffn_in, 16)
                for c, (r0, rows) in enumerate(CHUNKS):
                    sp.dma_start(w_2[0:rows, c, :], w2[one, r0:r0 + rows, :].rearrange("o r n -> (o r) n")).then_inc(ffn_in, 16)
                    for side in range(2):
                        src = ins["L1_ffn_b1"][one, side * GATED + r0:side * GATED + r0 + rows]
                        sp.dma_start(vecs[0:rows, 3 * side + c:3 * side + c + 1], src.rearrange("o r -> r o")).then_inc(ffn_in, 16)
                for c, name in enumerate(("L1_ffn_b2", "L1_ffn_ln_g", "L1_ffn_ln_b")):
                    sp.dma_start(vecs[:, 6 + c:7 + c], ins[name][one, :].rearrange("o r -> r o")).then_inc(ffn_in, 16)

        FFN_LOADS = 1 + 3 * len(CHUNKS) + 3

        @block.tensor
        def _(pe):
            def project_qk(n, banks):
                pe.wait_ge(xt_ready, 2 * n + 2)
                pe.wait_ge(normed, 4 * n)
                for j in banks:
                    pe.matmul(qk_ps[j][:], xt[:], w_qk[:, j * BANK:(j + 1) * BANK], start=True, stop=True).then_inc(qk_proj, 1)

            def turn(n, w, j):
                for q in range(4 * j, 4 * j + 4):
                    turn = pe.transpose(ring[2 * w + j][:, q % 4 * P:q % 4 * P + P],
                                        qkr[:, w, q * P:(q + 1) * P], shared.ident[:])
                turn.then_inc(qk_turned, 1)

            def turn_k(n):
                pe.wait_ge(rotated, 2 * n + 1)
                pe.wait_ge(att_out, 2 * n)
                turn(n, 1, 0)
                turn(n, 1, 1)

            def turn_q(n):
                pe.wait_ge(rotated, 2 * n + 2)
                pe.wait_ge(aT_out, 2 * n)
                turn(n, 0, 1)
                pe.wait_ge(x1_out, n)
                turn(n, 0, 0)

            def score(n, i):
                pe.wait_ge(qT_out, 2 * n + 2)
                pe.wait_ge(kT_out, 2 * n + 2)
                pe.wait_ge(k_kept, n + 1)
                for h in range(2):
                    pe.matmul(ring[h][:], shared.identb[:], mask8[:, bass.ds(i % TILES, 1), :] if not isinstance(i, int)
                              else mask8[:, i % TILES, :], start=True, stop=False, skip_group_check=True)
                    for q in range(PAIRS):
                        for g in range(TILES):
                            mm = pe.matmul(ring[h][WIN * g:WIN * g + WIN, q * 64:q * 64 + 64],
                                           tokens(qT, h)[:, q, WIN * g:WIN * g + WIN],
                                           tokens(kT, h)[:, q, WIN * g:WIN * g + 2 * WIN],
                                           start=False, stop=True, skip_group_check=True)
                    mm.then_inc(scores, 1)

            def project_v(n, windows):
                pe.wait_ge(xv_ready, 2 * n + 2)
                for g in windows:
                    if g < 2:
                        pe.wait_ge(kT_out, 2 * n + g + 1)
                    else:
                        pe.wait_ge(v_out, 4 * n + g - 1)
                    for h in range(2):
                        mm = pe.matmul(ring[2 + g % 2][64 * h:64 * h + 64, :], xv[:, WIN * g:WIN * g + 2 * WIN],
                                       w_v[:, h, :], start=True, stop=True)
                    mm.then_inc(v_proj, 1)

            def turn_probs(n):
                pe.wait_ge(exped, 2 * n + 2)
                for q in range(PAIRS):
                    turn = pe.transpose(ring[q // 4][:, q % 4 * P:q % 4 * P + P],
                                        probs[:, q, :, :].rearrange("p h k -> p (h k)"), shared.ident[:])
                    if q % 4 == 3:
                        turn.then_inc(p_turned, 1)

            def mix(n):
                pe.wait_ge(v_out, 4 * n + 4)
                pe.wait_ge(p_out0, n + 1)
                pe.wait_ge(p_out1, n + 1)
                pe.matmul(ring[2][:, 0:1], shared.identb[:], mask8[:, 0, 0:1], start=True, stop=True, skip_group_check=True)
                for h in range(2):
                    for q in range(PAIRS):
                        for g in range(TILES):
                            mm = pe.matmul(ring[2 + h][WIN * g:WIN * g + WIN, q * DH:q * DH + DH],
                                           tokens(pT, h)[:, q, WIN * g:WIN * g + WIN],
                                           tokens(val, h)[:, g, q * DH:q * DH + DH],
                                           start=True, stop=True, skip_group_check=True)
                    mm.then_inc(mixed, 1)

            def turn_att(n):
                pe.wait_ge(att_out, 2 * n + 2)
                for q in range(PAIRS):
                    turn = pe.transpose(ring[q // 4][:, q % 4 * P:q % 4 * P + P],
                                        att[:, q, :, :].rearrange("p h v -> p (h v)"), shared.ident[:])
                    if q % 4 == 3:
                        turn.then_inc(a_turned, 1)

            def project_out(n):
                pe.wait_ge(aT_out, 2 * n + 2)
                for q in range(PAIRS):
                    mm = pe.matmul(ring[0][:, 0:P], w_o[:, q, :], aT[:, q, :], start=(q == 0), stop=(q == PAIRS - 1))
                mm.then_inc(projected, 1)

            def rest(n, i, ahead):
                project_v(n, (0, 1))
                score(n, i)
                project_v(n, (2, 3))
                if ahead == 2:
                    project_qk(n + 2, (0, 1))
                turn_probs(n)
                if ahead == 2:
                    project_qk(n + 2, (2,))
                mix(n)
                if ahead == 2:
                    project_qk(n + 2, (3,))
                turn_att(n)
                if ahead:
                    turn_k(n + 1)
                project_out(n)
                if ahead:
                    turn_q(n + 1)

            def ffn_up(m):
                pe.wait_ge(xn_ready, m + 1)
                for c, (r0, rows) in enumerate(CHUNKS):
                    g_ps, v_ps = qk_ps[c % 2], qk_ps[2 + c % 2]
                    if c == 2:
                        pe.wait_ge(gelued, 3 * m + 1)
                        pe.wait_ge(gated, 3 * m + 1)
                    elif c == 0:
                        pe.wait_ge(gated, 3 * m)
                    pe.matmul(g_ps[0:rows, :], w_1[:, GATED + r0:GATED + r0 + rows], xn[:], start=True, stop=True).then_inc(gates, 1)
                    pe.matmul(v_ps[0:rows, :], w_1[:, r0:r0 + rows], xn[:], start=True, stop=True).then_inc(vals, 1)

            def ffn_down(m):
                pe.wait_ge(x0_out, m)
                for c, (r0, rows) in enumerate(CHUNKS):
                    pe.wait_ge(gated, 3 * m + c + 1)
                    mm = pe.matmul(ring[2][:], w_2[0:rows, c, :], act[0:rows, c, :], start=(c == 0), stop=(c == 2))
                mm.then_inc(ffn_out, 1)

            with pe.Fori(0, B) as b:
                pe.wait_ge(xf_ready, 2 * b + 2)
                ln.turn_in(pe, b, xf)
                pe.wait_ge(x0_first, b)
                ln.turn_back(pe, b)
            pe.wait_ge(mask_done, TILES)
            pe.wait_ge(x0_first, B)
            with pe.Fori(0, LAYERS) as l:
                pe.wait_ge(qk_in, 16 * l + 16)
                pe.wait_ge(v_in, 32 * l + 32)
                pe.wait_ge(o_in, 16 * l + 16)
                pe.wait_ge(x0_out, B * l)
                tile0 = l * NT
                project_qk(tile0, range(4))
                project_qk(tile0 + 1, range(4))
                turn_k(tile0)
                turn_q(tile0)
                with pe.Fori(0, NT - 2) as i:
                    rest(tile0 + i, i, 2)
                rest(tile0 + NT - 2, NT - 2, 1)
                rest(tile0 + NT - 1, NT - 1, 0)
                pe.wait_ge(ffn_in, 16 * FFN_LOADS * l + 16 * FFN_LOADS)
                pe.wait_ge(x1_out, NT * l + NT)
                first = B * l
                pe.wait_ge(xf_ready, 2 * (first + B) + 2)
                ln.turn_in(pe, first + B, xf)
                ln.turn_back(pe, first + B)
                with pe.Fori(0, B - 1) as b:
                    m = first + b
                    pe.wait_ge(xf_ready, 2 * (m + B) + 4)
                    ln.turn_in(pe, m + B + 1, xf)
                    ffn_up(m)
                    ln.turn_back(pe, m + B + 1)
                    ffn_down(m)
                ffn_up(first + B - 1)
                ffn_down(first + B - 1)

        @block.scalar
        def _(eng):
            def shifted_copy(dst, width, src, col, done):
                eng.copy(dst[0:64, 0:width], src[0:64, bass.ds(col, width)]).then_inc(done, 1)
                eng.copy(dst[64:128, 0:width], src[64:128, bass.ds(col - 1, width)]).then_inc(done, 1)

            def take_qk(n, i):
                eng.wait_ge(qk_proj, 4 * n)
                shifted_copy(xt, P, x0, column(i), xt_ready)

            def square(n, banks):
                for j in banks:
                    eng.wait_ge(qk_proj, 4 * n + j + 1)
                    if j == 0:
                        eng.wait_ge(norms, 2 * n)
                    eng.activation(sq[:, j // 2, j % 2 * BANK:(j % 2 + 1) * BANK], qk_ps[j][:], ACT.Square).then_inc(squared, 1)

            def take_v(n, i):
                eng.wait_ge(v_proj, 4 * n)
                shifted_copy(xv, WIN + P, x0, column(i) - WIN, xv_ready)

            def rest(n, i, ahead):
                eng.wait_ge(scores, 2 * n)
                for j in (1, 0):
                    eng.wait_ge(qk_turned, 4 * n + 4 - j)
                    eng.copy(qT[:, 4 * j:4 * j + 4, :].rearrange("p q t -> p (q t)"), ring[j][:]).then_inc(qT_out, 1)

                def exp(h):
                    eng.wait_ge(shifted, 2 * n + h + 1)
                    eng.activation(probs[:, :, h, :], probs[:, :, h, :], ACT.Exp, scale=QK_SCALE).then_inc(exped, 1)

                def value(g):
                    eng.wait_ge(v_proj, 4 * n + g + 1)
                    if g == 0:
                        eng.wait_ge(mixed, 2 * n)
                    eng.copy(val[:, g, :], ring[2 + g % 2][:]).then_inc(v_out, 1)

                value(0)
                value(1)
                if ahead == 2:
                    take_qk(n + 2, i + 2)
                exp(0)
                value(2)
                exp(1)
                value(3)
                if ahead:
                    take_v(n + 1, i + 1)
                if ahead == 2:
                    square(n + 2, (0, 1))
                eng.wait_ge(p_turned, 2 * n + 2)
                eng.wait_ge(mixed, 2 * n)
                eng.copy(pT[:, 4:8, :].rearrange("p q t -> p (q t)"), ring[1][:]).then_inc(p_out1, 1)
                if ahead == 2:
                    square(n + 2, (2, 3))
                eng.wait_ge(projected, n)
                for j in range(2):
                    eng.wait_ge(a_turned, 2 * n + j + 1)
                    eng.copy(aT[:, 4 * j:4 * j + 4, :].rearrange("p q t -> p (q t)"), ring[j][:]).then_inc(aT_out, 1)

            def take_ffn(m, col):
                eng.wait_ge(ln.turned, m + B)
                shifted_copy(xf, T, x1, col, xf_ready)

            def affine(m):
                eng.wait_ge(ln.back, m + B + 1)
                eng.wait_ge(vals, 3 * m)
                eng.activation(xn[:], ring[1][:], ACT.Identity, bias=vecs[:, 8:9], scale=vecs[:, 7:8]).then_inc(xn_ready, 1)

            def gelu(m):
                for c, (r0, rows) in enumerate(CHUNKS):
                    eng.wait_ge(gates, 3 * m + c + 1)
                    eng.wait_ge(gated, 3 * m)
                    eng.activation(gate[0:rows, c, :], qk_ps[c % 2][0:rows, :], ACT.Gelu,
                                   bias=vecs[0:rows, 3 + c:4 + c]).then_inc(gelued, 1)

            eng.wait_ge(pads_done, 4)
            with eng.Fori(0, B) as b:
                eng.wait_ge(ln.turned, b)
                eng.copy(xf[0:64, :], shared.xs[0:64, bass.ds(b * T, T)]).then_inc(xf_ready, 1)
                eng.copy(xf[64:128, :], shared.xs[64:128, bass.ds(b * T, T)]).then_inc(xf_ready, 1)
                eng.wait_ge(ln.back, b + 1)
                eng.copy(x0[:, bass.ds(b * SEQ + LEAD + 1, T)], ring[1][:]).then_inc(x0_first, 1)
            eng.wait_ge(x0_first, B)
            with eng.Fori(0, LAYERS) as l:
                eng.wait_ge(x0_out, B * l)
                first = l * NT
                take_qk(first, 0)
                take_v(first, 0)
                square(first, range(4))
                take_qk(first + 1, 1)
                square(first + 1, range(4))
                with eng.Fori(0, NT - 2) as i:
                    rest(first + i, i, 2)
                rest(first + NT - 2, NT - 2, 1)
                rest(first + NT - 1, NT - 1, 0)
                eng.wait_ge(x1_out, first + NT)
                eng.wait_ge(ffn_in, 16 * FFN_LOADS * l + 16 * FFN_LOADS)
                m0 = B * l
                take_ffn(m0, LEAD + 1)
                affine(m0)
                with eng.Fori(0, B - 1) as b:
                    take_ffn(m0 + b + 1, b * SEQ + (LEAD + 1 + SEQ))
                    gelu(m0 + b)
                    affine(m0 + b + 1)
                gelu(m0 + B - 1)

        @block.vector
        def _(dve):
            def squared_norms(n, w):
                dve.wait_ge(squared, 4 * n + 2 * w + 2)
                dve.wait_ge(floored, 2 * n)
                part = slice(HEADS * w, HEADS * w + HEADS)
                dve.tensor_reduce(n2[:, part], heads(sq[:, w, :]), AX.X, ALU.add).then_inc(norms, 1)
                dve.wait_ge(norms, 2 * n + w + 1)
                dve.wait_ge(rnorm, 2 * n)
                dve.tensor_scalar(n2c[:, part], n2[:, part], NORM_FLOOR, None, ALU.max).then_inc(floored, 1)

            def scale_to_one(n):
                dve.wait_ge(cosed, 2 * n)
                dve.wait_ge(sined_q, 2 * n)
                dve.wait_ge(sined_k, 2 * n)
                dve.wait_ge(rnorm, 2 * n + 2)
                for j in (2, 3, 0, 1):
                    dve.tensor_tensor(heads(qkn[:, j // 2, j % 2 * BANK:(j % 2 + 1) * BANK]), heads(qk_ps[j][:]),
                                      rn[:, 8 * j:8 * j + 8].unsqueeze(2).to_broadcast([P, 8, DH]),
                                      ALU.mult).then_inc(normed, 1)

            def table(a, w, i):
                row = a[:, w, bass.ds(i % TILES, 1), :] if not isinstance(i, int) else a[:, w, i % TILES:i % TILES + 1, :]
                return row.to_broadcast([P, HEADS, DH])

            def cosine(n, i):
                dve.wait_ge(qk_turned, 4 * n)
                for k, w in enumerate((1, 0)):
                    dve.wait_ge(normed, 4 * n + 2 * k + 2)
                    dve.tensor_tensor(heads(qkr[:, w, :]), heads(qkn[:, w, :]), table(cos, w, i), ALU.mult).then_inc(cosed, 1)

            def sine_q(n, i):
                dve.wait_ge(rotated, 2 * n)
                for half in range(2):
                    dve.tensor_tensor(heads(qks[:, 0, :])[:, :, 32 * half:32 * half + 32],
                                      heads(qkn[:, 0, :])[:, :, 32 - 32 * half:64 - 32 * half],
                                      half_table(0, i, half).to_broadcast([P, HEADS, 32]), ALU.mult).then_inc(sined_q, 1)

            def keys(n):
                dve.wait_ge(scores, 2 * n)
                dve.wait_ge(kT_out, 2 * n)
                dve.tensor_copy(kT[:, :, 0:WIN], kT[:, :, P:P + WIN]).then_inc(k_kept, 1)
                dve.wait_ge(k_kept, n + 1)
                for j in range(2):
                    dve.wait_ge(qk_turned, 4 * n + j + 1)
                    dve.tensor_copy(kT[:, 4 * j:4 * j + 4, WIN:WIN + P],
                                    ring[2 + j][:].rearrange("p (q t) -> p q t", t=P)).then_inc(kT_out, 1)

            def rest(n, i, ahead):
                if ahead:
                    scale_to_one(n + 1)
                dve.wait_ge(shifted, 2 * n)
                dve.wait_ge(p_turned, 2 * n)
                dve.wait_ge(summed, 2 * n)
                for h in range(2):
                    dve.wait_ge(scores, 2 * n + h + 1)
                    dve.tensor_reduce(top[:, h, :], heads(ring[h][:]), AX.X, ALU.max).then_inc(topped, 1)
                    dve.wait_ge(topped, 2 * n + h + 1)
                    dve.tensor_tensor(probs[:, :, h, :], heads(ring[h][:]),
                                      top[:, h, :].unsqueeze(2).to_broadcast([P, PAIRS, 2 * WIN]),
                                      ALU.subtract).then_inc(shifted, 1)
                if ahead:
                    cosine(n + 1, i + 1)
                dve.wait_ge(p_turned, 2 * n + 1)
                dve.wait_ge(mixed, 2 * n)
                dve.tensor_copy(pT[:, 0:4, :].rearrange("p q t -> p (q t)"), ring[0][:]).then_inc(p_out0, 1)
                if ahead:
                    sine_q(n + 1, i + 1)
                dve.wait_ge(inverted, n)
                for h in range(2):
                    dve.wait_ge(exped, 2 * n + h + 1)
                    dve.tensor_reduce(total[:, h, :], probs[:, :, h, :], AX.X, ALU.add).then_inc(summed, 1)
                dve.wait_ge(summed, 2 * n + 2)
                dve.wait_ge(att_out, 2 * n)
                dve.reciprocal(rtotal[:].rearrange("p h q -> p (h q)"), total[:].rearrange("p h q -> p (h q)")).then_inc(inverted, 1)
                if ahead == 2:
                    squared_norms(n + 2, 0)
                dve.wait_ge(inverted, n + 1)
                dve.wait_ge(a_turned, 2 * n)
                for h in range(2):
                    dve.wait_ge(mixed, 2 * n + h + 1)
                    dve.tensor_tensor(att[:, :, h, :], heads(ring[2 + h][:]),
                                      rtotal[:, h, :].unsqueeze(2).to_broadcast([P, PAIRS, DH]),
                                      ALU.mult).then_inc(att_out, 1)
                if ahead == 2:
                    squared_norms(n + 2, 1)
                if ahead:
                    keys(n + 1)
                dve.wait_ge(projected, n + 1)
                at = column(i)
                dve.tensor_tensor(x1[:, bass.ds(at, P)], ring[0][:, 0:P], x0[:, bass.ds(at, P)], ALU.add).then_inc(x1_out, 1)

            def gated_product(m):
                dve.wait_ge(ffn_out, m)
                for c, (r0, rows) in enumerate(CHUNKS):
                    dve.wait_ge(vals, 3 * m + c + 1)
                    dve.wait_ge(gelued, 3 * m + c + 1)
                    dve.scalar_tensor_tensor(act[0:rows, c, :], qk_ps[2 + c % 2][0:rows, :], vecs[0:rows, c:c + 1],
                                             gate[0:rows, c, :], ALU.add, ALU.mult).then_inc(gated, 1)

            def ffn_add(m, col):
                dve.wait_ge(ffn_out, m + 1)
                dve.scalar_tensor_tensor(x0[:, bass.ds(col, T)], ring[2][:], vecs[:, 6:7], x1[:, bass.ds(col, T)],
                                         ALU.add, ALU.add).then_inc(x0_out, 1)

            for a in (x0, x1):
                dve.memset(a[:, 0:LEAD], 0.0).then_inc(pads_done, 1)
                dve.memset(a[:, LEAD:].rearrange("p (b t) -> p b t", t=SEQ)[:, :, 0:1], 0.0).then_inc(pads_done, 1)
            dve.memset(kT[:], 0.0).then_inc(kT_clear, 1)
            dve.wait_ge(kT_clear, 1)
            with dve.Fori(0, B) as b:
                ln.statistics(dve, b)
                dve.wait_ge(ln.back, b)
                ln.normalise(dve, b)
            dve.wait_ge(const_in, 32)
            with dve.Fori(0, LAYERS) as l:
                first = l * NT
                dve.wait_ge(gains_in, 16 * 8 * l + 16 * 8)
                dve.wait_ge(rotated, 2 * first)
                dve.wait_ge(cosed, 2 * first)
                dve.wait_ge(sined_q, 2 * first)
                for side, tab in enumerate((cos, sin)):
                    for w in range(2):
                        dve.tensor_tensor(tab[:, w, :, :], trig[:, side, w, :, :],
                                          gains[:, side, w, :].unsqueeze(1).to_broadcast([P, TILES, DH]),
                                          ALU.mult).then_inc(tables, 1)
                dve.wait_ge(tables, 4 * l + 4)
                for w in range(2):
                    squared_norms(first, w)
                scale_to_one(first)
                cosine(first, 0)
                sine_q(first, 0)
                for w in range(2):
                    squared_norms(first + 1, w)
                keys(first)
                with dve.Fori(0, NT - 2) as i:
                    rest(first + i, i, 2)
                rest(first + NT - 2, NT - 2, 1)
                rest(first + NT - 1, NT - 1, 0)
                dve.wait_ge(ffn_in, 16 * FFN_LOADS * l + 16 * FFN_LOADS)
                m0 = B * l
                ln.statistics(dve, m0 + B)
                dve.wait_ge(ln.back, m0 + B)
                ln.normalise(dve, m0 + B)
                with dve.Fori(0, B - 1) as b:
                    m = m0 + b
                    ln.statistics(dve, m + B + 1)
                    dve.wait_ge(ln.back, m + B + 1)
                    ln.normalise(dve, m + B + 1)
                    gated_product(m)
                    ffn_add(m, b * SEQ + (LEAD + 1))
                gated_product(m0 + B - 1)
                ffn_add(m0 + B - 1, (B - 1) * SEQ + (LEAD + 1))

        @block.gpsimd
        def _(pool):
            def reciprocal_norms(n, w):
                part = slice(HEADS * w, HEADS * w + HEADS)
                pool.wait_ge(floored, 2 * n + w + 1)
                pool.wait_ge(normed, 4 * n)
                pool.tensor_tensor(rn[:, part], n2c[:, part], shared.minus_half[:, part], ALU.pow).then_inc(rnorm, 1)

            def rotate(n, i):
                pool.wait_ge(rotated, 2 * n)
                pool.wait_ge(normed, 4 * n + 2)
                for half in range(2):
                    pool.tensor_tensor(heads(qks[:, 1, :])[:, :, 32 * half:32 * half + 32],
                                       heads(qkn[:, 1, :])[:, :, 32 - 32 * half:64 - 32 * half],
                                       half_table(1, i, half).to_broadcast([P, HEADS, 32]), ALU.mult).then_inc(sined_k, 1)
                pool.wait_ge(cosed, 2 * n + 1)
                pool.wait_ge(sined_k, 2 * n + 2)
                pool.tensor_tensor(qkr[:, 1, :], qkr[:, 1, :], qks[:, 1, :], ALU.add).then_inc(rotated, 1)
                pool.wait_ge(cosed, 2 * n + 2)
                pool.wait_ge(sined_q, 2 * n + 2)
                pool.tensor_tensor(qkr[:, 0, :], qkr[:, 0, :], qks[:, 0, :], ALU.add).then_inc(rotated, 1)

            pool.wait_ge(const_in, 32)
            for t in range(TILES):
                pool.tensor_copy(mask8[:, t, :].rearrange("p (h k) -> p h k", h=PAIRS),
                                 mask[:, t:t + 1, :].to_broadcast([P, PAIRS, 2 * WIN])).then_inc(mask_done, 1)
            with pool.Fori(0, B) as b:
                ln.reciprocal_deviation(pool, b)
            with pool.Fori(0, LAYERS) as l:
                first = l * NT
                pool.wait_ge(tables, 4 * l + 4)
                for w in range(2):
                    reciprocal_norms(first, w)
                rotate(first, 0)
                for w in range(2):
                    reciprocal_norms(first + 1, w)
                with pool.Fori(0, NT - 2) as i:
                    rotate(first + i + 1, i + 1)
                    for w in range(2):
                        reciprocal_norms(first + i + 2, w)
                rotate(first + NT - 1, NT - 1)
                with pool.Fori(0, B) as b:
                    ln.reciprocal_deviation(pool, B * l + b + B)


def fold_heads(nc, shared, ins):
    with ExitStack() as ctx:
        mem = Memory(nc, ctx, "fold")
        names = ("L1_attn_P_q", "L1_attn_P_k", "L1_attn_P_v", "L1_attn_P_o")
        raw = mem.sb("raw", [P, 4, HEADS, DH])
        turned_w = mem.sb("turned", [P, 4, PAIRS, P])
        ps = [mem.bank(f"ps{k}") for k in range(4)]
        prod = [mem.bank(f"prod{k}") for k in range(4)]
        loaded, turned, taken, folded, kept = (mem.sem(n) for n in ("loaded", "turned", "taken", "folded", "kept"))
        block = ctx.enter_context(nc.Block())

        @block.sync
        def _(sp):
            for w, name in enumerate(names):
                sp.dma_start(raw[:, w, :, :], ins[name].rearrange("h d k -> d h k")).then_inc(loaded, 16)

        @block.tensor
        def _(pe):
            pe.wait_ge(loaded, 16 * 4)
            for w in range(4):
                for half in range(2):
                    n = 2 * w + half
                    if n >= 4:
                        pe.wait_ge(taken, n - 3)
                    for q in range(4):
                        first = 8 * half + 2 * q
                        turn = pe.transpose(ps[n % 4][:, q * P:(q + 1) * P],
                                            raw[:, w, first:first + 2, :].rearrange("p h k -> p (h k)"), shared.ident[:])
                    turn.then_inc(turned, 1)
            pe.wait_ge(taken, 8)
            for q in range(PAIRS):
                for h in range(2):
                    if q >= 2:
                        pe.wait_ge(kept, 4 * (q - 1))
                    rows = slice(64 * h, 64 * h + 64)
                    for w in range(2):
                        mm = pe.matmul(prod[2 * (q % 2) + h][:, w * P:(w + 1) * P],
                                       turned_w[rows, 2 * w, q, :], turned_w[rows, 2 * w + 1, q, :],
                                       start=True, stop=True, skip_group_check=True)
                    mm.then_inc(folded, 1)

        @block.vector
        def _(dve):
            for n in range(8):
                dve.wait_ge(turned, n + 1)
                dve.tensor_copy(turned_w[:, n // 2, 4 * (n % 2):4 * (n % 2) + 4, :].rearrange("p q d -> p (q d)"),
                                ps[n % 4][:]).then_inc(taken, 1)
            for n in range(HEADS):
                dve.wait_ge(folded, n + 1)
                for w, dst in enumerate((shared.w_score, shared.w_value)):
                    dve.tensor_copy(dst[:, n, :], prod[n % 4][:, w * P:(w + 1) * P]).then_inc(kept, 1)


def causal(nc, shared, ins):
    with ExitStack() as ctx:
        mem = Memory(nc, ctx, "cau")
        scale = float(DH) ** -0.5
        diag_in, diag = mem.sb("diag_in", [P, P]), mem.sb("diag", [P, P], BF16)
        xf = mem.sb("xf", [P, T])
        xn = mem.sb("xn", [P, T])
        w_head = mem.sb("w_head", [P, P])
        xa = mem.sb("xa", [P, T])
        u = mem.sb("u", [P, TILES, P])
        probs = mem.sb("probs", [P, TILES, T])
        pT = mem.sb("pT", [P, TILES, T])
        top = mem.sb("top", [P, TILES])
        bias = mem.sb("bias", [P, TILES])
        total = mem.sb("total", [P, TILES])
        rtotal = mem.sb("rtotal", [P, TILES])
        y = mem.sb("y", [P, TILES, P])
        sc = [mem.bank(f"scores{k}") for k in range(3)]
        tr = [mem.bank(f"turn{k}") for k in range(3)]
        out_ps, in_ps = mem.bank("out"), mem.bank("in")
        ln = LayerNorm(mem, shared, out_ps, in_ps)
        ROW = {3: (0, 0), 0: (1, 0), 2: (1, P), 1: (2, 0)}
        COL = {0: (0, 0), 1: (1, 0), 3: (1, 3 * P), 2: (2, 0)}
        BANK_ROWS = [[3], [0, 2], [1]]
        BANK_COLS = [[0], [1, 3], [2]]

        s = mem.sem
        const_in, diag_done = s("const_in"), s("diag_done")
        xf_ready, xn_ready = s("xf_ready"), s("xn_ready")
        w_ready = s("w_ready")
        xa_done, xa_out = s("xa_done"), s("xa_out")
        u_done, u_out = s("u_done"), s("u_out")
        scored = s("scored")
        topped, biased = s("topped"), s("biased")
        exped = s("exped")
        inverted = s("inverted")
        p_turned = s("p_turned")
        pT0_out, pT12_out = s("pT0_out"), s("pT12_out")
        mixed, added = s("mixed"), s("added")
        cleared = s("cleared")
        y_turned, xs_out = s("y_turned"), s("xs_out")
        block = ctx.enter_context(nc.Block())

        @block.sync
        def _(sp):
            sp.dma_start(diag_in[:], ins["c_diag"]).then_inc(const_in, 16)

        @block.tensor
        def _(pe):
            def query(m, values):
                pe.wait_ge(w_ready, m + 1)
                pe.wait_ge(u_out, values)
                pe.matmul(in_ps[:], w_head[:], xn[:], start=True, stop=True).then_inc(xa_done, 1)

            def score(m):
                pe.wait_ge(xa_out, m + 1)
                pe.wait_ge(exped, 4 * m)
                for k, rows in enumerate(BANK_ROWS):
                    for i in rows:
                        c0, keys = ROW[i][1], (i + 1) * P
                        pe.matmul(sc[k][:, c0:c0 + keys], xa[:, i * P:(i + 1) * P], xn[:, 0:keys],
                                  start=True, stop=False, skip_group_check=True)
                        mm = pe.matmul(sc[k][:, c0 + i * P:c0 + keys], shared.identb[:], diag[:],
                                       start=False, stop=True, skip_group_check=True)
                    mm.then_inc(scored, 1)

            def turn(m):
                pe.wait_ge(exped, 4 * m + 4)
                pe.wait_ge(pT0_out, m)
                pe.wait_ge(pT12_out, 3 * m)
                for k, cols in enumerate(BANK_COLS):
                    for j in cols:
                        for i in range(j, TILES):
                            c0 = COL[j][1] + (i - j) * P
                            tp = pe.transpose(tr[k][:, c0:c0 + P], probs[:, i, j * P:(j + 1) * P], shared.ident[:])
                    tp.then_inc(p_turned, 1)

            def value(m, h):
                for t in range(TILES):
                    w = shared.w_value[:, h, :] if isinstance(h, int) else \
                        shared.w_value[:, bass.ds(h, 1), :].rearrange("p o d -> p (o d)")
                    mm = pe.matmul(in_ps[:, t * P:(t + 1) * P], xn[:, t * P:(t + 1) * P], w,
                                   start=True, stop=True, skip_group_check=True)
                mm.then_inc(u_done, 1)

            def mix(m):
                pe.wait_ge(u_out, m + 1)
                pe.wait_ge(pT0_out, m + 1)
                pe.wait_ge(pT12_out, 3 * m + 3)
                pe.wait_ge(added, 4 * m)
                for i in range(TILES):
                    for j in range(i + 1):
                        mm = pe.matmul(out_ps[:, i * P:(i + 1) * P], pT[:, j, i * P:(i + 1) * P], u[:, j, :],
                                       start=(j == 0), stop=(j == i), skip_group_check=True)
                mm.then_inc(mixed, 1)

            pe.wait_ge(diag_done, 1)
            with pe.Fori(0, B) as b:
                pe.wait_ge(xf_ready, b + 1)
                pe.wait_ge(xs_out, b)
                ln.turn_in(pe, b, xf)
                pe.wait_ge(u_out, HEADS * b)
                ln.turn_back(pe, b)
                pe.wait_ge(xn_ready, b + 1)
                m0 = HEADS * b
                query(m0, m0)
                score(m0)
                with pe.Fori(0, HEADS - 1) as h:
                    query(m0 + h + 1, m0 + h)
                    turn(m0 + h)
                    pe.wait_ge(xa_out, m0 + h + 2)
                    value(m0 + h, h)
                    score(m0 + h + 1)
                    mix(m0 + h)
                turn(m0 + HEADS - 1)
                value(m0 + HEADS - 1, HEADS - 1)
                mix(m0 + HEADS - 1)
                pe.wait_ge(added, 4 * m0 + 4 * HEADS)
                for t in range(TILES):
                    tp = pe.transpose(out_ps[:, t * P:(t + 1) * P], y[:, t, :], shared.ident[:])
                tp.then_inc(y_turned, 1)

        @block.scalar
        def _(act):
            def query_out(m):
                act.wait_ge(xa_done, m + 1)
                act.wait_ge(scored, 3 * m)
                act.copy(xa[:], in_ps[:]).then_inc(xa_out, 1)

            def exponentials(m):
                act.wait_ge(biased, m + 1)
                act.wait_ge(p_turned, 3 * m)
                act.wait_ge(inverted, m)
                for k in range(3):
                    for i in BANK_ROWS[k]:
                        c0, keys = ROW[i][1], (i + 1) * P
                        act.activation(probs[:, i, 0:keys], sc[k][:, c0:c0 + keys], ACT.Exp, bias=bias[:, i:i + 1],
                                       scale=scale, accum_out=total[:, i:i + 1]).then_inc(exped, 1)

            def values_out(m):
                act.wait_ge(p_turned, 3 * m + 1)
                act.wait_ge(mixed, m)
                act.copy(pT[:, 0, :], tr[0][:]).then_inc(pT0_out, 1)
                act.wait_ge(u_done, m + 1)
                act.copy(u[:].rearrange("p t d -> p (t d)"), in_ps[:]).then_inc(u_out, 1)

            with act.Fori(0, B) as b:
                act.wait_ge(ln.turned, b)
                act.copy(xf[:], shared.xs[:, bass.ds(b * T, T)]).then_inc(xf_ready, 1)
                act.wait_ge(ln.back, b + 1)
                act.wait_ge(u_done, HEADS * b)
                act.wait_ge(scored, 3 * HEADS * b)
                act.copy(xn[:], in_ps[:]).then_inc(xn_ready, 1)
                m0 = HEADS * b
                query_out(m0)
                exponentials(m0)
                with act.Fori(0, HEADS - 1) as h:
                    query_out(m0 + h + 1)
                    values_out(m0 + h)
                    exponentials(m0 + h + 1)
                values_out(m0 + HEADS - 1)

        @block.vector
        def _(dve):
            def maxima(m):
                dve.wait_ge(biased, m)
                for k in range(3):
                    dve.wait_ge(scored, 3 * m + k + 1)
                    for i in BANK_ROWS[k]:
                        c0, keys = ROW[i][1], (i + 1) * P
                        dve.tensor_reduce(top[:, i:i + 1], sc[k][:, c0:c0 + keys], AX.X, ALU.max).then_inc(topped, 1)
                dve.wait_ge(topped, 4 * m + 4)
                dve.wait_ge(exped, 4 * m)
                dve.tensor_scalar(bias[:], top[:], -scale, None, ALU.mult).then_inc(biased, 1)

            def invert(m):
                dve.wait_ge(exped, 4 * m + 4)
                dve.wait_ge(added, 4 * m)
                dve.reciprocal(rtotal[:], total[:]).then_inc(inverted, 1)

            def turned_out(m):
                dve.wait_ge(mixed, m)
                dve.wait_ge(p_turned, 3 * m + 2)
                dve.tensor_copy(pT[:, 1, P:T], tr[1][:, 0:3 * P]).then_inc(pT12_out, 1)
                dve.tensor_copy(pT[:, 3, 3 * P:T], tr[1][:, 3 * P:T]).then_inc(pT12_out, 1)
                dve.wait_ge(p_turned, 3 * m + 3)
                dve.tensor_copy(pT[:, 2, 2 * P:T], tr[2][:, 0:2 * P]).then_inc(pT12_out, 1)

            def add(m):
                dve.wait_ge(mixed, m + 1)
                dve.wait_ge(inverted, m + 1)
                dve.wait_ge(added, 4 * m)
                for t in range(TILES):
                    dve.scalar_tensor_tensor(y[:, t, :], out_ps[:, t * P:(t + 1) * P], rtotal[:, t:t + 1], y[:, t, :],
                                             ALU.mult, ALU.add).then_inc(added, 1)

            dve.wait_ge(const_in, 16)
            dve.tensor_copy(diag[:], diag_in[:]).then_inc(diag_done, 1)
            with dve.Fori(0, B) as b:
                ln.statistics(dve, b)
                dve.wait_ge(ln.back, b)
                ln.normalise(dve, b)
                dve.wait_ge(y_turned, b)
                dve.memset(y[:], 0.0).then_inc(cleared, 1)
                dve.wait_ge(cleared, b + 1)
                m0 = HEADS * b
                maxima(m0)
                invert(m0)
                with dve.Fori(0, HEADS - 1) as h:
                    turned_out(m0 + h)
                    maxima(m0 + h + 1)
                    add(m0 + h)
                    invert(m0 + h + 1)
                turned_out(m0 + HEADS - 1)
                add(m0 + HEADS - 1)
                dve.wait_ge(y_turned, b + 1)
                dve.tensor_tensor(shared.xs[:, bass.ds(b * T, T)], shared.xs[:, bass.ds(b * T, T)], out_ps[:],
                                  ALU.add).then_inc(xs_out, 1)

        @block.gpsimd
        def _(pool):
            with pool.Fori(0, B) as b:
                ln.reciprocal_deviation(pool, b)
                with pool.Fori(0, HEADS) as h:
                    pool.wait_ge(xa_done, HEADS * b + h)
                    pool.tensor_copy(w_head[:], shared.w_score[:, bass.ds(h, 1), :].rearrange("p o d -> p (o d)")).then_inc(w_ready, 1)


STAGES = 9
HIDDEN = 4 * D
HCH = HIDDEN // P


def fold_butterflies(nc, shared, ins):
    with ExitStack() as ctx:
        mem = Memory(nc, ctx, "fly")
        w_up = mem.sb("w_up", [P, STAGES, HIDDEN // 2, 2, 2])
        w_down = mem.sb("w_down", [P, STAGES, HIDDEN // 2, 2, 2])
        up = mem.sb("up", [P, 2, HIDDEN])
        up_same, up_cross = mem.sb("up_same", [P, 2, HIDDEN]), mem.sb("up_cross", [P, 2, HIDDEN])
        w_con = mem.sb("w_con", [P, HCH, P])
        down = mem.sb("down", [P, 1, HIDDEN])
        dn_same, dn_cross = mem.sb("dn_same", [P, 1, HIDDEN]), mem.sb("dn_cross", [P, 1, HIDDEN])
        bias_in = mem.sb("bias_in", [P, HCH + 2])
        con_ps, turn_ps, bias_ps = mem.bank("con"), mem.bank("turn"), mem.bank("bias")
        s = mem.sem
        up_in, down_in, bias_loaded = s("up_in"), s("down_in"), s("bias_loaded")
        cleared, con_turned, con_out = s("cleared"), s("con_turned"), s("con_out")
        up_parts, up_steps, dn_parts, dn_steps = s("up_parts"), s("up_steps"), s("dn_parts"), s("dn_steps")
        turned, bias_turned, done = s("turned"), s("bias_turned"), s("done")
        block = ctx.enter_context(nc.Block())

        def butterfly(eng, cur, same, cross, w, order, transposed, parts, steps):
            blocks = cur.shape[1]
            for n, stage in enumerate(order):
                st = 2 ** stage
                pair = lambda a, half: a[:].rearrange("p k (n two s) -> p k n two s", two=2, s=st)[:, :, :, half, :]

                def weight(o, i):
                    v = w[:, stage, :, o, i].rearrange("p (k n s) -> p k n s", k=1, s=st)
                    return v.to_broadcast([P, blocks, HIDDEN // 2 // st, st])

                eng.wait_ge(steps, n)
                for o in range(2):
                    i = 1 - o
                    eng.tensor_tensor(pair(same, o), pair(cur, o), weight(o, o), ALU.mult).then_inc(parts, 1)
                    eng.tensor_tensor(pair(cross, o), pair(cur, i), weight(*((i, o) if transposed else (o, i))),
                                      ALU.mult).then_inc(parts, 1)
                eng.wait_ge(parts, 4 * n + 4)
                eng.tensor_tensor(cur[:], same[:], cross[:], ALU.add).then_inc(steps, 1)

        @block.sync
        def _(sp):
            sp.dma_start(w_con[:], ins["L0_ffn_W_con"].rearrange("(c p) d -> p c d", p=P)).then_inc(down_in, 16)
            sp.wait_ge(cleared, 1)
            sp.dma_start(up[:, 0, :], ins["L0_ffn_W_exp"]).then_inc(up_in, 16)
            sp.dma_start(up[0:1, 1, :], ins["L0_ffn_b_exp"].rearrange("(o h) -> o h", o=1)).then_inc(up_in, 16)
            for w, name, done_ in ((w_up, "L0_ffn_up_weights", up_in), (w_down, "L0_ffn_down_weights", down_in)):
                src = ins[name].rearrange("(q s) k a b -> q (s k a b)", q=1)
                sp.dma_start(w[:].rearrange("p s k a b -> p (s k a b)"), src.to_broadcast([P, STAGES * 2 * HIDDEN])).then_inc(done_, 16)
            sp.dma_start(bias_in[:, 0:HCH], ins["L0_ffn_up_bias"].rearrange("(c p) -> p c", p=P), allow_slow_non_contiguous=True).then_inc(bias_loaded, 16)
            for k, name in enumerate(("L0_ffn_b_con", "L0_ffn_down_bias")):
                sp.dma_start(bias_in[:, HCH + k:HCH + k + 1], ins[name].rearrange("(p o) -> p o", o=1)).then_inc(bias_loaded, 16)

        @block.tensor
        def _(pe):
            pe.wait_ge(down_in, 32)
            for c in range(HCH):
                turn = pe.transpose(con_ps[:, c * P:(c + 1) * P], w_con[:, c, :], shared.ident[:])
            turn.then_inc(con_turned, 1)
            pe.wait_ge(up_steps, STAGES)
            for c in range(HCH):
                mm = pe.matmul(bias_ps[:, c:c + 1], up[0:1, 1, c * P:(c + 1) * P], shared.ident[0:1, 0:1],
                               start=True, stop=True, skip_group_check=True)
            mm.then_inc(bias_turned, 1)
            pe.wait_ge(dn_steps, STAGES)
            for c in range(HCH):
                turn = pe.transpose(turn_ps[:, c * P:(c + 1) * P], down[:, 0, c * P:(c + 1) * P], shared.ident[:])
            turn.then_inc(turned, 1)

        @block.scalar
        def _(act):
            act.wait_ge(con_turned, 1)
            act.copy(down[:, 0, :], con_ps[:]).then_inc(con_out, 1)
            act.wait_ge(turned, 1)
            act.copy(shared.w_down[:].rearrange("p c d -> p (c d)"), turn_ps[:]).then_inc(done, 1)
            act.wait_ge(up_steps, STAGES)
            act.copy(shared.w_up[:], up[:, 0, :]).then_inc(done, 1)

        @block.vector
        def _(dve):
            dve.memset(up[:], 0.0).then_inc(cleared, 1)
            dve.wait_ge(up_in, 16 * 3)
            butterfly(dve, up, up_same, up_cross, w_up, range(STAGES), False, up_parts, up_steps)
            dve.wait_ge(bias_loaded, 16 * 3)
            dve.wait_ge(bias_turned, 1)
            dve.tensor_tensor(shared.up_bias[:], bias_ps[:, 0:HCH], bias_in[:, 0:HCH], ALU.add).then_inc(done, 1)
            dve.tensor_tensor(shared.down_bias[:], bias_in[:, HCH:HCH + 1], bias_in[:, HCH + 1:HCH + 2], ALU.add).then_inc(done, 1)

        @block.gpsimd
        def _(pool):
            pool.wait_ge(down_in, 32)
            pool.wait_ge(con_out, 1)
            butterfly(pool, down, dn_same, dn_cross, w_down, range(STAGES - 1, -1, -1), True, dn_parts, dn_steps)


def rwkv_ffn(nc, shared, ins):
    with ExitStack() as ctx:
        mem = Memory(nc, ctx, "rwkv")
        K_CLAMP, K_EPS = 60.0, 1e-8
        w_kvr = mem.sb("w_kvr", [P, 3, HIDDEN])
        w_o = mem.sb("w_o", [P, HCH, P])
        c_k, c_v, c_r = mem.sb("c_k", [P, HIDDEN]), mem.sb("c_v", [P, HCH, P]), mem.sb("c_r", [P, P])
        row_g, row_b = mem.sb("row_g", [P, 1, P]), mem.sb("row_b", [P, 1, P])
        VEC = ("pre_g", "pre_b", "post_g", "post_b", "tm_mix_k", "tm_mix_v", "tm_mix_r", "cm_mix_k", "cm_mix_r")
        vec = mem.sb("vec", [P, len(VEC)])
        rest = mem.sb("rest", [P, 5])
        time = mem.sb("time", [P, 2, HCH])
        timed = mem.sb("timed", [P, 2, HCH])
        growth = mem.sb("growth", [P, HCH])
        rows = mem.sb("rows", [P, TILES, P])
        z1, z2, z3 = (mem.sb(n, [P, TILES, P]) for n in ("z1", "z2", "z3"))
        x0T = mem.sb("x0T", [P, T])
        xa = mem.sb("xa", [P, T])
        xb = mem.sb("xb", [P, T])
        xc = mem.sb("xc", [P, T])
        xd = mem.sb("xd", [P, T])
        xh = mem.sb("xh", [P, T])
        xn = mem.sb("xn", [P, 1 + T])
        late = mem.sb("late", [P, 3, T])
        mixed_in = mem.sb("mixed_in", [P, 3, T])
        low = mem.sb("low", [P, 2, T])
        key, kv = mem.sb("key", [P, 2, T]), mem.sb("kv", [P, 2, T])
        gate = mem.sb("gate", [P, 2, T])
        gate1, numer = mem.sb("gate1", [P, T]), mem.sb("numer", [P, T])
        sk, skv = mem.sb("sk", [P, 1 + T]), mem.sb("skv", [P, 1 + T])
        wk, wkv, den, rden = (mem.sb(n, [P, T]) for n in ("wk", "wkv", "den", "rden"))
        out_c = mem.sb("out_c", [P, HCH, T])
        hid = mem.sb("hid", [P, HCH, T])
        sig = mem.sb("sig", [P, T])
        xnf = mem.sb("xnf", [P, T])
        k_ps = [mem.bank(f"k{j}") for j in range(2)]
        v_ps = [mem.bank(f"v{j}") for j in range(2)]
        r_ps = [mem.bank(f"r{j}") for j in range(2)]
        y_ps, t_ps = mem.bank("y"), mem.bank("t")
        lns = LayerNorm(mem, shared, y_ps, r_ps[0])
        mem.prefix = "rwkvf"
        lnf = LayerNorm(mem, shared, t_ps, r_ps[1])
        mem.prefix = "rwkv"

        s = mem.sem
        w_in, x_in = s("w_in"), s("x_in")
        prep = s("prep")
        time_exp = s("time_exp")
        scaled, xa_tok = s("scaled"), s("xa_tok")
        turned3 = s("turned3")
        x0_out, xa_out = s("x0_out"), s("xa_out")
        xn_out = s("xn_out")
        late_done, mix_done = s("late_done"), s("mix_done")
        kvr = s("kvr")
        lowed, keyed, gated, gated1 = s("lowed"), s("keyed"), s("gated"), s("gated1")
        kv_done, scanned, firsts, den_done, rden_done = s("kv_done"), s("scanned"), s("firsts"), s("den_done"), s("rden_done")
        out_done, y_done = s("out_done"), s("y_done")
        xb_done, xc_done, xd_done = s("xb_done"), s("xc_done"), s("xd_done")
        up_done, hid_done = s("up_done"), s("hid_done")
        cr_done, sig_done = s("cr_done"), s("sig_done")
        numerated = s("numerated")
        half_done, xnf_out, xs_out = s("half_done"), s("xnf_out"), s("xs_out")
        WLOADS = 3 + 1 + 3 + 2 + len(VEC) + 2
        block = ctx.enter_context(nc.Block())

        @block.sync
        def _(sp):
            name = lambda n: ins["L0_attn_" + n]
            sp.dma_start(rows[:], ins["L0_attn_x"][0].rearrange("(t p) d -> p t d", p=P)).then_inc(x_in, 16)
            for k, v in enumerate(VEC):
                sp.dma_start(vec[:, k:k + 1], name(v).rearrange("(p o) -> p o", o=1)).then_inc(w_in, 16)
            for k, v in enumerate(("tm_decay", "tm_first")):
                sp.dma_start(time[:, k, :], name(v).rearrange("(c p) -> p c", p=P), allow_slow_non_contiguous=True).then_inc(w_in, 16)
            for dst, v in ((row_g, "ln0_g"), (row_b, "ln0_b")):
                sp.dma_start(dst[:, 0, :], name(v).rearrange("(o d) -> o d", o=1).to_broadcast([P, D])).then_inc(w_in, 16)
            for k, v in enumerate(("tm_Wk", "tm_Wv", "tm_Wr")):
                sp.dma_start(w_kvr[:, k, :], name(v)).then_inc(w_in, 16)
            sp.dma_start(w_o[:], name("tm_Wo").rearrange("(c p) d -> p c d", p=P)).then_inc(w_in, 16)
            sp.dma_start(c_k[:], name("cm_Wk")).then_inc(w_in, 16)
            sp.dma_start(c_v[:], name("cm_Wv").rearrange("(c p) d -> p c d", p=P)).then_inc(w_in, 16)
            sp.dma_start(c_r[:], name("cm_Wr")).then_inc(w_in, 16)
            with sp.Fori(1, B) as b:
                sp.wait_ge(lns.back, b)
                src = ins["L0_attn_x"][bass.ds(b, 1)].rearrange("o (t p) d -> p (o t) d", p=P)
                sp.dma_start(rows[:], src).then_inc(x_in, 16)

        @block.tensor
        def _(pe):
            pe.wait_ge(w_in, 16 * WLOADS)
            with pe.Fori(0, B) as b:
                pe.wait_ge(x_in, 16 * b + 16)
                pe.wait_ge(xs_out, b)
                for t in range(TILES):
                    turn = pe.transpose(k_ps[0][:, t * P:(t + 1) * P], rows[:, t, :], shared.ident[:])
                turn.then_inc(turned3, 1)
                pe.wait_ge(xa_tok, b + 1)
                for t in range(TILES):
                    turn = pe.transpose(v_ps[0][:, t * P:(t + 1) * P], z3[:, t, :], shared.ident[:])
                turn.then_inc(turned3, 1)
                lns_back = 3 * b + 2
                pe.wait_ge(lns.hat_done, TILES * lns_back + TILES)
                for t in range(TILES):
                    turn = pe.transpose(lns.feat[:, t * P:(t + 1) * P], lns.hat[:, t, :], shared.ident[:])
                turn.then_inc(lns.back, 1)
                pe.wait_ge(x0_out, b + 1)
                pe.wait_ge(xa_out, b + 1)
                for c in range(HCH):
                    if c >= 2:
                        pe.wait_ge(lowed, 4 * b + c - 1)
                        pe.wait_ge(kv_done, 4 * b + c - 1)
                        pe.wait_ge(gated, 4 * b + c - 1)
                    for j, bank in enumerate((k_ps, v_ps, r_ps)):
                        if c == 0:
                            pe.wait_ge(mix_done, 5 * b + j + 1)
                        pe.matmul(bank[c % 2][:], w_kvr[:, j, c * P:(c + 1) * P], mixed_in[:, j, :],
                                  start=True, stop=True).then_inc(kvr, 1)
                for c in range(HCH):
                    pe.wait_ge(out_done, 4 * b + c + 1)
                    mm = pe.matmul(y_ps[:], w_o[:, c, :], out_c[:, c, :], start=(c == 0), stop=(c == HCH - 1))
                mm.then_inc(y_done, 1)
                pe.wait_ge(xb_done, b + 1)
                lnf.turn_in(pe, 2 * b, xb)
                lnf.turn_back(pe, 2 * b)
                pe.wait_ge(mix_done, 5 * b + 5)
                pe.matmul(r_ps[0][:], c_r[:], mixed_in[:, 1, :], start=True, stop=True).then_inc(cr_done, 1)
                for c in range(HCH):
                    if c >= 2:
                        pe.wait_ge(hid_done, 8 * b + c - 1)
                    pe.matmul(k_ps[c % 2][:], c_k[:, c * P:(c + 1) * P], mixed_in[:, 0, :], start=True, stop=True).then_inc(up_done, 1)
                for c in range(HCH):
                    pe.wait_ge(hid_done, 8 * b + c + 1)
                    mm = pe.matmul(y_ps[:], c_v[:, c, :], hid[:, c, :], start=(c == 0), stop=(c == HCH - 1))
                mm.then_inc(y_done, 1)
                pe.wait_ge(xd_done, b + 1)
                lnf.turn_in(pe, 2 * b + 1, xd)
                lnf.turn_back(pe, 2 * b + 1)
                pe.wait_ge(xnf_out, b + 1)
                for c in range(HCH):
                    if c >= 2:
                        pe.wait_ge(hid_done, 8 * b + 4 + c - 1)
                    pe.matmul(k_ps[c % 2][:], shared.w_up[:, c * P:(c + 1) * P], xnf[:], start=True, stop=True).then_inc(up_done, 1)
                for c in range(HCH):
                    pe.wait_ge(hid_done, 8 * b + 4 + c + 1)
                    mm = pe.matmul(y_ps[:], shared.w_down[:, c, :], hid[:, c, :], start=(c == 0), stop=(c == HCH - 1))
                mm.then_inc(y_done, 1)

        @block.scalar
        def _(act):
            act.wait_ge(w_in, 16 * WLOADS)
            act.activation(growth[:], time[:, 0, :], ACT.Exp).then_inc(time_exp, 1)
            act.activation(timed[:, 1, :], time[:, 1, :], ACT.Exp).then_inc(time_exp, 1)
            act.wait_ge(time_exp, 2)
            act.activation(timed[:, 0, :], growth[:], ACT.Exp, scale=-1.0).then_inc(time_exp, 1)
            act.wait_ge(prep, 4)
            with act.Fori(0, B) as b:
                act.wait_ge(turned3, 2 * b + 1)
                act.wait_ge(xd_done, b)
                act.copy(x0T[:], k_ps[0][:]).then_inc(x0_out, 1)
                act.wait_ge(turned3, 2 * b + 2)
                act.copy(xa[:], v_ps[0][:]).then_inc(xa_out, 1)

                def spread(n, g, k, count, first, bank):
                    act.activation(xn[:, 1:], bank[:], ACT.Identity, bias=vec[:, g + 1:g + 2], scale=vec[:, g:g + 1]).then_inc(xn_out, 1)
                    act.wait_ge(xn_out, 2 * b + n + 1)
                    for j in range(count):
                        act.activation(late[:, j, :], xn[:, 0:T], ACT.Copy, scale=rest[:, k + j:k + j + 1]).then_inc(late_done, 1)

                act.wait_ge(lns.back, b + 1)
                act.wait_ge(mix_done, 5 * b)
                spread(0, 0, 0, 3, 0, lns.feat)
                for c in range(HCH):
                    act.wait_ge(lowed, 4 * b + c + 1)
                    if c >= 2:
                        act.wait_ge(firsts, 8 * b + 2 * c - 2)
                        act.wait_ge(gated1, 4 * b + c - 1)
                    act.activation(key[:, c % 2, :], low[:, c % 2, :], ACT.Exp).then_inc(keyed, 1)
                    act.wait_ge(kvr, 12 * b + 3 * c + 3)
                    act.activation(gate[:, c % 2, :], r_ps[c % 2][:], ACT.Tanh, scale=0.5).then_inc(gated, 1)
                act.wait_ge(lnf.back, 2 * b + 1)
                spread(1, 2, 3, 2, 3, lnf.feat)
                for c in range(HCH):
                    act.wait_ge(up_done, 8 * b + c + 1)
                    act.activation(hid[:, c, :], k_ps[c % 2][:], ACT.Silu).then_inc(hid_done, 1)
                act.wait_ge(cr_done, b + 1)
                act.activation(sig[:], r_ps[0][:], ACT.Tanh, scale=0.5).then_inc(sig_done, 1)
                act.wait_ge(lnf.back, 2 * b + 2)
                act.copy(xnf[:], lnf.feat[:]).then_inc(xnf_out, 1)
                act.wait_ge(y_done, 3 * b + 2)
                for c in range(HCH):
                    act.wait_ge(up_done, 8 * b + 4 + c + 1)
                    act.activation(hid[:, c, :], k_ps[c % 2][:], ACT.Gelu, bias=shared.up_bias[:, c:c + 1]).then_inc(hid_done, 1)

        @block.vector
        def _(dve):
            for a in (xn, sk, skv):
                dve.memset(a[:, 0:1], 0.0).then_inc(prep, 1)
            dve.wait_ge(w_in, 16 * WLOADS)
            dve.tensor_scalar(rest[:], vec[:, 4:9], -1.0, 1.0, ALU.mult, ALU.add).then_inc(prep, 1)
            dve.wait_ge(prep, 4)
            dve.wait_ge(time_exp, 3)
            with dve.Fori(0, B) as b:
                u = 3 * b
                dve.wait_ge(x_in, 16 * b + 16)
                lns.statistics(dve, u, rows)
                lns.normalise(dve, u, rows, z1)
                dve.wait_ge(lns.hat_done, TILES * u + TILES)
                lns.statistics(dve, u + 1, z1)
                lns.normalise(dve, u + 1, z1, z2)
                dve.wait_ge(lns.hat_done, TILES * u + 2 * TILES)
                dve.wait_ge(turned3, 2 * b)
                dve.tensor_tensor(z1[:], z2[:], row_g[:].to_broadcast([P, TILES, P]), ALU.mult).then_inc(scaled, 1)
                dve.wait_ge(scaled, b + 1)
                dve.tensor_tensor(z3[:], z1[:], row_b[:].to_broadcast([P, TILES, P]), ALU.add).then_inc(xa_tok, 1)
                dve.wait_ge(xa_tok, b + 1)
                lns.statistics(dve, u + 2, z3)
                dve.wait_ge(lns.back, b)
                lns.normalise(dve, u + 2, z3)

                def blend(n, k, count):
                    for j in range(count):
                        dve.wait_ge(late_done, 5 * b + n + j + 1)
                        dve.scalar_tensor_tensor(mixed_in[:, j, :], xn[:, 1:], vec[:, 4 + k + j:5 + k + j], late[:, j, :],
                                                 ALU.mult, ALU.add).then_inc(mix_done, 1)

                dve.wait_ge(up_done, 8 * b)
                blend(0, 0, 3)
                for c in range(HCH):
                    n = 4 * b + c
                    dve.wait_ge(kvr, 12 * b + 3 * c + 1)
                    if c >= 2:
                        dve.wait_ge(keyed, 4 * b + c - 1)
                    dve.tensor_scalar(low[:, c % 2, :], k_ps[c % 2][:], K_CLAMP, None, ALU.min).then_inc(lowed, 1)
                    dve.wait_ge(keyed, n + 1)
                    dve.wait_ge(kvr, 12 * b + 3 * c + 2)
                    dve.wait_ge(firsts, 2 * n)
                    dve.tensor_tensor(kv[:, c % 2, :], key[:, c % 2, :], v_ps[c % 2][:], ALU.mult).then_inc(kv_done, 1)
                    decay = timed[:, 0, c:c + 1].to_broadcast([P, T])
                    dve.tensor_tensor_scan(sk[:, 1:], decay, key[:, c % 2, :], 0.0, ALU.mult, ALU.add).then_inc(scanned, 1)
                    dve.wait_ge(kv_done, n + 1)
                    dve.tensor_tensor_scan(skv[:, 1:], decay, kv[:, c % 2, :], 0.0, ALU.mult, ALU.add).then_inc(scanned, 1)
                    dve.wait_ge(scanned, 2 * n + 1)
                    dve.wait_ge(den_done, n)
                    dve.scalar_tensor_tensor(wk[:], key[:, c % 2, :], timed[:, 1, c:c + 1], sk[:, 0:T],
                                             ALU.mult, ALU.add).then_inc(firsts, 1)
                    dve.wait_ge(scanned, 2 * n + 2)
                    dve.wait_ge(numerated, n)
                    dve.scalar_tensor_tensor(wkv[:], kv[:, c % 2, :], timed[:, 1, c:c + 1], skv[:, 0:T],
                                             ALU.mult, ALU.add).then_inc(firsts, 1)
                    dve.wait_ge(firsts, 2 * n + 1)
                    dve.wait_ge(rden_done, n)
                    dve.tensor_scalar(den[:], wk[:], K_EPS, 2.0, ALU.add, ALU.mult).then_inc(den_done, 1)
                    dve.wait_ge(den_done, n + 1)
                    dve.wait_ge(out_done, n)
                    dve.reciprocal(rden[:], den[:]).then_inc(rden_done, 1)
                dve.wait_ge(y_done, 3 * b + 1)
                dve.tensor_tensor(xb[:], xa[:], y_ps[:], ALU.add).then_inc(xb_done, 1)
                lnf.statistics(dve, 2 * b)
                dve.wait_ge(lnf.back, 2 * b)
                lnf.normalise(dve, 2 * b)
                blend(3, 3, 2)
                dve.wait_ge(y_done, 3 * b + 2)
                dve.wait_ge(sig_done, b + 1)
                dve.scalar_tensor_tensor(xc[:], sig[:], 0.5, xb[:], ALU.mult, ALU.add).then_inc(half_done, 1)
                dve.wait_ge(half_done, 2 * b + 1)
                dve.scalar_tensor_tensor(xh[:], xc[:], 0.5, x0T[:], ALU.add, ALU.add).then_inc(half_done, 1)
                dve.wait_ge(half_done, 2 * b + 2)
                dve.tensor_tensor(xd[:], xh[:], y_ps[:], ALU.add).then_inc(xd_done, 1)
                lnf.statistics(dve, 2 * b + 1)
                dve.wait_ge(lnf.back, 2 * b + 1)
                lnf.normalise(dve, 2 * b + 1)
                dve.wait_ge(y_done, 3 * b + 3)
                dve.scalar_tensor_tensor(shared.xs[:, bass.ds(b * T, T)], y_ps[:], shared.down_bias[:], xd[:],
                                         ALU.add, ALU.add).then_inc(xs_out, 1)

        @block.gpsimd
        def _(pool):
            with pool.Fori(0, B) as b:
                for k in range(3):
                    lns.reciprocal_deviation(pool, 3 * b + k)
                for c in range(HCH):
                    n = 4 * b + c
                    pool.wait_ge(gated, n + 1)
                    pool.wait_ge(numerated, n)
                    pool.tensor_tensor(gate1[:], gate[:, c % 2, :], shared.ones[:].to_broadcast([P, T]), ALU.add).then_inc(gated1, 1)
                    pool.wait_ge(gated1, n + 1)
                    pool.wait_ge(firsts, 2 * n + 2)
                    pool.wait_ge(out_done, n)
                    pool.tensor_tensor(numer[:], wkv[:], gate1[:], ALU.mult).then_inc(numerated, 1)
                    pool.wait_ge(numerated, n + 1)
                    pool.wait_ge(rden_done, n + 1)
                    pool.wait_ge(y_done, 3 * b)
                    pool.tensor_tensor(out_c[:, c, :], numer[:], rden[:], ALU.mult).then_inc(out_done, 1)
                for k in range(2):
                    lnf.reciprocal_deviation(pool, 2 * b + k)


def constants(nc, shared, ins):
    with ExitStack() as ctx:
        mem = Memory(nc, ctx, "const")
        loaded, set_ = mem.sem("loaded"), mem.sem("set")
        block = ctx.enter_context(nc.Block())

        @block.sync
        def _(sp):
            sp.dma_start(shared.ident[:], ins["c_ident"]).then_inc(loaded, 16)

        @block.vector
        def _(dve):
            dve.wait_ge(loaded, 16)
            dve.tensor_copy(shared.identb[:], shared.ident[:]).then_inc(set_, 1)

        @block.gpsimd
        def _(pool):
            for dst, value in ((shared.minus_half, -0.5), (shared.ones, 1.0)):
                pool.memset(dst[:], value).then_inc(set_, 1)
            pool.wait_ge(set_, 3)


def store(nc, shared, out):
    with ExitStack() as ctx:
        mem = Memory(nc, ctx, "out")
        total = [mem.sb(f"total{k}", [P, T]) for k in range(2)]
        rows = [mem.sb(f"rows{k}", [P, TILES, D]) for k in range(2)]
        ps = [mem.bank(f"ps{k}") for k in range(2)]
        added, turned, copied = mem.sem("added"), mem.sem("turned"), mem.sem("copied")
        stored = [mem.sem(f"stored{k}") for k in range(2)]
        block = ctx.enter_context(nc.Block())

        @block.vector
        def _(dve):
            for b in range(B):
                if b >= 2:
                    dve.wait_ge(turned, b - 1)
                at = LEAD + 1 + b * SEQ
                dve.tensor_tensor(total[b % 2][:], shared.xs[:, b * T:(b + 1) * T], shared.x0[:, at:at + T],
                                  ALU.add).then_inc(added, 1)

        @block.tensor
        def _(pe):
            for b in range(B):
                pe.wait_ge(added, b + 1)
                if b >= 2:
                    pe.wait_ge(copied, b - 1)
                for t in range(TILES):
                    turn = pe.transpose(ps[b % 2][:, t * P:(t + 1) * P], total[b % 2][:, t * P:(t + 1) * P], shared.ident[:])
                turn.then_inc(turned, 1)

        @block.scalar
        def _(act):
            for b in range(B):
                act.wait_ge(turned, b + 1)
                if b >= 2:
                    act.wait_ge(stored[b % 2], 16 * (b // 2))
                act.copy(rows[b % 2][:].rearrange("p t d -> p (t d)"), ps[b % 2][:]).then_inc(copied, 1)

        @block.sync
        def _(sp):
            for b in range(B):
                sp.wait_ge(copied, b + 1)
                sp.dma_start(out[b].rearrange("(t p) d -> p t d", p=P), rows[b % 2][:]).then_inc(stored[b % 2], 16)
            for k in range(2):
                sp.wait_ge(stored[k], 16 * (B // 2))


def build(nc, ins, out):
    with ExitStack() as ctx:
        shared = Shared(Memory(nc, ctx, "all"))
        constants(nc, shared, ins)
        fold_butterflies(nc, shared, ins)
        fold_heads(nc, shared, ins)
        rwkv_ffn(nc, shared, ins)
        causal(nc, shared, ins)
        layers(nc, shared, ins)
        store(nc, shared, out)


def _constants():
    ident = np.eye(P, dtype=np.float32)
    p = np.arange(P)[:, None] % WIN
    c = np.arange(2 * WIN)[None, :]
    seen = (c <= p + WIN) & (c >= p)
    mask = np.where(seen, 0.0, MASKED)[:, None, :].repeat(TILES, 1)
    mask[:WIN, 0, :WIN] = MASKED
    diag = np.where(np.arange(P)[None, :] <= np.arange(P)[:, None], 0.0, MASKED)
    half = np.arange(0, DH, 2, dtype=np.float32)
    inv_freq = (1.0 / 10000.0 ** (half / DH)).astype(np.float32)
    t = np.arange(T, dtype=np.float32)
    freqs = np.tile(t[:, None] * inv_freq[None, :], (1, 2)).astype(np.float64)
    base = (half + np.float32(0.4 * DH)) / np.float32(1.4 * DH)
    power = (t - T // 2) / (WIN // 2)
    scale = np.tile(base[None, :].astype(np.float64) ** power[:, None], (1, 2))
    sign = np.where(np.arange(DH) < DH // 2, -1.0, 1.0)
    trig = np.stack([np.stack([np.cos(freqs) * scale, np.cos(freqs) / scale]),
                     np.stack([np.sin(freqs) * scale * sign, np.sin(freqs) / scale * sign])])
    trig = trig.reshape(2, 2, TILES, P, DH).transpose(3, 0, 1, 2, 4)
    return {"c_ident": ident, "c_mask": mask.astype(np.float32), "c_diag": diag.astype(np.float32),
            "c_trig": np.ascontiguousarray(trig, dtype=np.float32)}


def kernel(**inputs):
    import concourse.bacc as bacc
    from concourse.bass_utils import run_bass_kernel_spmd

    nc = bacc.Bacc("TRN2", target_bir_lowering=False, num_devices=1)
    arrays = {name: np.ascontiguousarray(a) for name, a in inputs.items()}
    arrays.update(_constants())
    ins = {name: nc.dram_tensor(name, a.shape, mybir.dt.from_np(a.dtype), kind="ExternalInput").ap()
           for name, a in arrays.items()}
    out = nc.dram_tensor("out", (B, T, D), F32, kind="ExternalOutput").ap()
    build(nc, ins, out)
    return run_bass_kernel_spmd(nc, [arrays], core_ids=[0]).results[0]["out"]
```

```python
from contextlib import ExitStack

import numpy as np

import concourse.bass as bass
from concourse import mybir
from concourse.alu_op_type import AluOpType as ALU

ACT = mybir.ActivationFunctionType
AX = mybir.AxisListType
F32 = mybir.dt.float32
BF16 = mybir.dt.bfloat16

P = 128
B, T, D = 8, 512, 128
TILES = T // P
NT = B * TILES
BANK = 512
HEADS, DH = 16, 64
PAIRS = HEADS // 2
INNER = HEADS * DH
WIN = 32
LAYERS = 6
GATED = 341
CHUNKS = [(0, 128), (128, 128), (256, GATED - 256)]
LN_EPS = 1e-5
NORM_FLOOR = 1e-24
QK_SCALE = 8.0
MASKED = -1e30
LEAD = WIN
SEQ = T + 1
XW = LEAD + B * SEQ


class Memory:

    def __init__(self, nc, ctx, prefix):
        self.nc, self.ctx, self.prefix, self.sems = nc, ctx, prefix, []
        ctx.callback(self.clear)

    def clear(self):
        for sem in self.sems:
            self.nc.gpsimd.sem_clear(sem)
            self.nc.release_semaphore(sem)

    def sb(self, name, shape, dt=F32):
        return self.ctx.enter_context(self.nc.sbuf_tensor(f"{self.prefix}_{name}", shape, dt))

    def bank(self, name):
        return self.ctx.enter_context(self.nc.psum_tensor(f"{self.prefix}_{name}", [P, BANK], F32))

    def sem(self, name):
        self.sems.append(self.nc.alloc_semaphore(f"{self.prefix}_{name}"))
        return self.sems[-1]


class LayerNorm:

    def __init__(self, mem, shared, tok, feat):
        self.tok, self.feat, self.shared = tok, feat, shared
        self.stats = mem.sb("ln_stats", [P, TILES, 6])
        self.both = mem.sb("ln_both", [P, TILES, 3])
        self.gap = mem.sb("ln_gap", [P, TILES])
        self.gap2, self.gap_eps = mem.sb("ln_gap2", [P, TILES]), mem.sb("ln_gap_eps", [P, TILES])
        self.mean = mem.sb("ln_mean", [P, TILES])
        self.vareps = mem.sb("ln_vareps", [P, TILES])
        self.rstd = mem.sb("ln_rstd", [P, TILES])
        self.hat = mem.sb("ln_hat", [P, TILES, P])
        self.turned = mem.sem("ln_turned")
        self.stats_done = mem.sem("ln_stats_done")
        self.steps = mem.sem("ln_steps")
        self.rstd_done = mem.sem("ln_rstd_done")
        self.hat_done = mem.sem("ln_hat_done")
        self.back = mem.sem("ln_back")

    def turn_in(self, pe, m, src):
        pe.wait_ge(self.hat_done, TILES * m)
        for t in range(TILES):
            turn = pe.transpose(self.tok[:, t * P:(t + 1) * P], src[:, t * P:(t + 1) * P], self.shared.ident[:])
        turn.then_inc(self.turned, 1)

    def statistics(self, dve, m, tok=None):
        if tok is None:
            dve.wait_ge(self.turned, m + 1)
            tok = self.tok[:].rearrange("p (t f) -> p t f", t=TILES)
        dve.wait_ge(self.steps, 6 * m)
        for t in range(TILES):
            dve.bn_stats(self.stats[:, t, :], tok[:, t, :]).then_inc(self.stats_done, 1)
        dve.wait_ge(self.stats_done, TILES * m + TILES)
        even, odd = self.stats[:, :, 0:3], self.stats[:, :, 3:6]
        dve.tensor_tensor(self.gap[:], even[:, :, 1], odd[:, :, 1], ALU.subtract).then_inc(self.steps, 1)
        dve.tensor_tensor(self.both[:], even, odd, ALU.add).then_inc(self.steps, 1)
        dve.wait_ge(self.steps, 6 * m + 1)
        dve.tensor_tensor(self.gap2[:], self.gap[:], self.gap[:], ALU.mult).then_inc(self.steps, 1)
        dve.wait_ge(self.steps, 6 * m + 2)
        dve.wait_ge(self.hat_done, TILES * m)
        dve.tensor_scalar(self.mean[:], self.both[:, :, 1], 0.5, None, ALU.mult).then_inc(self.steps, 1)
        dve.wait_ge(self.steps, 6 * m + 3)
        dve.tensor_scalar(self.gap_eps[:], self.gap2[:], 0.25, LN_EPS, ALU.mult, ALU.add).then_inc(self.steps, 1)
        dve.wait_ge(self.steps, 6 * m + 5)
        dve.wait_ge(self.rstd_done, m)
        dve.scalar_tensor_tensor(self.vareps[:], self.both[:, :, 2], 1.0 / P, self.gap_eps[:],
                                 ALU.mult, ALU.add).then_inc(self.steps, 1)

    def reciprocal_deviation(self, pool, m):
        pool.wait_ge(self.steps, 6 * m + 6)
        pool.wait_ge(self.hat_done, TILES * m)
        pool.tensor_tensor(self.rstd[:], self.vareps[:], self.shared.minus_half[:, 0:TILES],
                           ALU.pow).then_inc(self.rstd_done, 1)

    def normalise(self, dve, m, tok=None, out=None):
        if tok is None:
            tok = self.tok[:].rearrange("p (t f) -> p t f", t=TILES)
        if out is None:
            out = self.hat
        dve.wait_ge(self.rstd_done, m + 1)
        for t in range(TILES):
            dve.tensor_scalar(out[:, t, :], tok[:, t, :], self.mean[:, t:t + 1], self.rstd[:, t:t + 1],
                              ALU.subtract, ALU.mult).then_inc(self.hat_done, 1)

    def turn_back(self, pe, m):
        pe.wait_ge(self.hat_done, TILES * m + TILES)
        for t in range(TILES):
            turn = pe.transpose(self.feat[:, t * P:(t + 1) * P], self.hat[:, t, :], self.shared.ident[:])
        turn.then_inc(self.back, 1)


class Shared:

    def __init__(self, mem):
        self.ident = mem.sb("ident", [P, P])
        self.identb = mem.sb("identb", [P, P], BF16)
        self.minus_half = mem.sb("minus_half", [P, 2 * HEADS])
        self.ones = mem.sb("ones", [P, 1])
        self.w_score = mem.sb("w_score", [P, HEADS, P])
        self.w_value = mem.sb("w_value", [P, HEADS, P])
        self.w_up = mem.sb("w_up", [P, 4 * D])
        self.w_down = mem.sb("w_down", [P, 4, D])
        self.up_bias = mem.sb("up_bias", [P, 4])
        self.down_bias = mem.sb("down_bias", [P, 1])
        self.x0 = mem.sb("x0", [P, XW])
        self.xs = mem.sb("xs", [P, B * T])


def column(tile):
    return tile * P + tile // TILES + (LEAD + 1)


def layers(nc, shared, ins):
    with ExitStack() as ctx:
        mem = Memory(nc, ctx, "lay")
        x0 = shared.x0
        x1 = mem.sb("x1", [P, XW])
        w_qk = mem.sb("w_qk", [P, 2 * INNER])
        w_v = mem.sb("w_v", [P, 2, PAIRS * DH])
        w_o = mem.sb("w_o", [P, PAIRS, P])
        w_1 = mem.sb("w_1", [P, 2 * GATED])
        w_2 = mem.sb("w_2", [P, len(CHUNKS), P])
        vecs = mem.sb("vecs", [P, 9])
        trig = mem.sb("trig", [P, 2, 2, TILES, DH])
        gains = mem.sb("gains", [P, 2, 2, DH])
        cos = mem.sb("cos", [P, 2, TILES, DH])
        sin = mem.sb("sin", [P, 2, TILES, DH])
        mask = mem.sb("mask", [P, TILES, 2 * WIN])
        mask8 = mem.sb("mask8", [P, TILES, PAIRS * 2 * WIN], BF16)
        xt = mem.sb("xt", [P, P])
        xv = mem.sb("xv", [P, P])
        sq = mem.sb("sq", [P, 2, INNER])
        n2 = mem.sb("n2", [P, 2 * HEADS])
        n2c = mem.sb("n2c", [P, 2 * HEADS])
        rn = mem.sb("rn", [P, 2 * HEADS])
        qkn = mem.sb("qkn", [P, 2, INNER])
        qkr = mem.sb("qkr", [P, 2, INNER])
        qks = mem.sb("qks", [P, 2, INNER])
        qT = mem.sb("qT", [P, PAIRS, P])
        kT = mem.sb("kT", [P, PAIRS, WIN + P])
        probs = mem.sb("probs", [P, PAIRS, 2, 2 * WIN])
        top = mem.sb("top", [P, 2, PAIRS])
        total = mem.sb("total", [P, 2, PAIRS])
        rtotal = mem.sb("rtotal", [P, 2, PAIRS])
        pT = mem.sb("pT", [P, PAIRS, P])
        val = mem.sb("val", [P, TILES + 1, PAIRS * DH])
        att = mem.sb("att", [P, PAIRS, 2, DH])
        aT = mem.sb("aT", [P, PAIRS, P])
        xf = mem.sb("xf", [P, T])
        xn = mem.sb("xn", [P, T])
        gate = mem.sb("gate", [P, len(CHUNKS), T])
        act = mem.sb("act", [P, len(CHUNKS), T])
        qk_ps = [mem.bank(f"qk{j}") for j in range(4)]
        ring = [mem.bank(f"ring{j}") for j in range(4)]
        ln = LayerNorm(mem, shared, ring[0], ring[1])

        s = mem.sem
        const_in = s("const_in")
        qk_in, v_in, o_in, ffn_in, gains_in = s("qk_in"), s("v_in"), s("o_in"), s("ffn_in"), s("gains_in")
        mask_done = s("mask_done")
        kT_clear = s("kT_clear")
        pads_done = s("pads_done")
        x0_first = s("x0_first")
        tables = s("tables")
        xt_ready, xv_ready = s("xt_ready"), s("xv_ready")
        qk_proj = s("qk_proj")
        squared = s("squared")
        norms = s("norms")
        floored, rnorm = s("floored"), s("rnorm")
        normed = s("normed")
        cosed = s("cosed")
        sined_q, sined_k = s("sined_q"), s("sined_k")
        rotated = s("rotated")
        qk_turned = s("qk_turned")
        qT_out, kT_out = s("qT_out"), s("kT_out")
        k_kept = s("k_kept")
        scores = s("scores")
        topped, shifted, summed, inverted = s("topped"), s("shifted"), s("summed"), s("inverted")
        exped = s("exped")
        v_proj, v_out, v_kept = s("v_proj"), s("v_out"), s("v_kept")
        p_turned, p_out0, p_out1 = s("p_turned"), s("p_out0"), s("p_out1")
        mixed, att_out = s("mixed"), s("att_out")
        a_turned, aT_out = s("a_turned"), s("aT_out")
        projected, x1_out = s("projected"), s("x1_out")
        xf_ready, xn_ready = s("xf_ready"), s("xn_ready")
        gates, vals = s("gates"), s("vals")
        gelued, gated = s("gelued"), s("gated")
        ffn_out, x0_out = s("ffn_out"), s("x0_out")

        def half_table(w, i, half):
            place = slice(i % TILES, i % TILES + 1) if isinstance(i, int) else bass.ds(i % TILES, 1)
            return sin[:, w, place, 32 * half:32 * half + 32]

        tokens = lambda a, h: a[64 * h:64 * h + 64]
        heads = lambda a: a.rearrange("p (h d) -> p h d", d=DH)
        block = ctx.enter_context(nc.Block())

        @block.sync
        def _(sp):
            sp.dma_start(trig[:], ins["c_trig"]).then_inc(const_in, 16)
            sp.dma_start(mask[:], ins["c_mask"]).then_inc(const_in, 16)
            w_qkv, w_out, w1, w2 = ins["L1_ffn_Wqkv"], ins["L1_ffn_Wo"], ins["L1_ffn_W1"], ins["L1_ffn_W2"]
            with sp.Fori(0, LAYERS) as l:
                one = bass.ds(l, 1)
                sp.wait_ge(tables, 4 * l)
                for side in range(2):
                    for which, name in enumerate(("L1_ffn_q_scale", "L1_ffn_k_scale")):
                        for half in range(2):
                            src = ins[name][one, bass.ds(32 * (half ^ side), 32)]
                            sp.dma_start(gains[:, side, which, 32 * half:32 * half + 32],
                                         src.to_broadcast([P, 32])).then_inc(gains_in, 16)
                sp.wait_ge(qk_proj, 4 * NT * l)
                sp.dma_start(w_qk[:], w_qkv[one, :, 0:2 * INNER].rearrange("o d n -> (o d) n")).then_inc(qk_in, 16)
                sp.wait_ge(v_proj, 2 * NT * l)
                for h in range(2):
                    src = w_qkv[one, :, 2 * INNER:3 * INNER].rearrange("o d (q h v) -> (o d) h q v", h=2, v=DH)
                    sp.dma_start(w_v[:, h, :].rearrange("p (q v) -> p q v", v=DH), src[:, h, :, :]).then_inc(v_in, 16)
                sp.wait_ge(projected, NT * l)
                sp.dma_start(w_o[:], w_out[one].rearrange("o (q p) n -> (o p) q n", p=P)).then_inc(o_in, 16)
                sp.wait_ge(x0_out, B * l)
                sp.dma_start(w_1[:], w1[one].rearrange("o d n -> (o d) n")).then_inc(ffn_in, 16)
                for c, (r0, rows) in enumerate(CHUNKS):
                    sp.dma_start(w_2[0:rows, c, :], w2[one, r0:r0 + rows, :].rearrange("o r n -> (o r) n")).then_inc(ffn_in, 16)
                    for side in range(2):
                        src = ins["L1_ffn_b1"][one, side * GATED + r0:side * GATED + r0 + rows]
                        sp.dma_start(vecs[0:rows, 3 * side + c:3 * side + c + 1], src.rearrange("o r -> r o")).then_inc(ffn_in, 16)
                for c, name in enumerate(("L1_ffn_b2", "L1_ffn_ln_g", "L1_ffn_ln_b")):
                    sp.dma_start(vecs[:, 6 + c:7 + c], ins[name][one, :].rearrange("o r -> r o")).then_inc(ffn_in, 16)

        FFN_LOADS = 1 + 3 * len(CHUNKS) + 3

        @block.tensor
        def _(pe):
            def project_qk(n, banks):
                pe.wait_ge(xt_ready, 2 * n + 2)
                pe.wait_ge(normed, 4 * n)
                for j in banks:
                    pe.matmul(qk_ps[j][:], xt[:], w_qk[:, j * BANK:(j + 1) * BANK], start=True, stop=True).then_inc(qk_proj, 1)

            def turn(n, w, j):
                for q in range(4 * j, 4 * j + 4):
                    turn = pe.transpose(ring[2 * w + j][:, q % 4 * P:q % 4 * P + P],
                                        qkr[:, w, q * P:(q + 1) * P], shared.ident[:])
                turn.then_inc(qk_turned, 1)

            def turn_k(n, j, att_halves):
                pe.wait_ge(rotated, 2 * n + 1)
                pe.wait_ge(att_out, att_halves)
                turn(n, 1, j)

            def project_v(n, h):
                pe.wait_ge(xv_ready, 2 * n + 2)
                pe.wait_ge(kT_out, 2 * n + h + 1)
                pe.matmul(ring[2 + h][:], xv[:], w_v[:, h, :], start=True, stop=True).then_inc(v_proj, 1)

            def turn_q_project_v(n):
                pe.wait_ge(rotated, 2 * n + 2)
                pe.wait_ge(aT_out, 2 * n)
                turn(n, 0, 1)
                project_v(n, 0)
                pe.wait_ge(x1_out, n)
                turn(n, 0, 0)
                project_v(n, 1)

            def score(n, i):
                pe.wait_ge(qT_out, 2 * n + 2)
                pe.wait_ge(kT_out, 2 * n + 2)
                pe.wait_ge(k_kept, n + 1)
                for h in range(2):
                    pe.matmul(ring[h][:], shared.identb[:], mask8[:, bass.ds(i % TILES, 1), :] if not isinstance(i, int)
                              else mask8[:, i % TILES, :], start=True, stop=False, skip_group_check=True)
                    for q in range(PAIRS):
                        for g in range(TILES):
                            mm = pe.matmul(ring[h][WIN * g:WIN * g + WIN, q * 64:q * 64 + 64],
                                           tokens(qT, h)[:, q, WIN * g:WIN * g + WIN],
                                           tokens(kT, h)[:, q, WIN * g:WIN * g + 2 * WIN],
                                           start=False, stop=True, skip_group_check=True)
                    mm.then_inc(scores, 1)

            def turn_probs(n):
                pe.wait_ge(exped, 2 * n + 2)
                for q in range(PAIRS):
                    turn = pe.transpose(ring[q // 4][:, q % 4 * P:q % 4 * P + P],
                                        probs[:, q, :, :].rearrange("p h k -> p (h k)"), shared.ident[:])
                    if q % 4 == 3:
                        turn.then_inc(p_turned, 1)

            def mix(n):
                pe.wait_ge(v_out, 12 * n + 12)
                pe.wait_ge(p_out0, n + 1)
                pe.wait_ge(p_out1, n + 1)
                pe.matmul(ring[2][:, 0:1], shared.identb[:], mask8[:, 0, 0:1], start=True, stop=True, skip_group_check=True)
                for h in range(2):
                    for q in range(PAIRS):
                        for g in range(TILES):
                            mm = pe.matmul(ring[2 + h][WIN * g:WIN * g + WIN, q * DH:q * DH + DH],
                                           tokens(pT, h)[:, q, WIN * g:WIN * g + WIN],
                                           tokens(val, h)[:, g, q * DH:q * DH + DH],
                                           start=True, stop=True, skip_group_check=True)
                    mm.then_inc(mixed, 1)

            def turn_att(n):
                pe.wait_ge(att_out, 2 * n + 2)
                for q in range(PAIRS):
                    turn = pe.transpose(ring[q // 4][:, q % 4 * P:q % 4 * P + P],
                                        att[:, q, :, :].rearrange("p h v -> p (h v)"), shared.ident[:])
                    if q % 4 == 3:
                        turn.then_inc(a_turned, 1)

            def project_out(n):
                pe.wait_ge(aT_out, 2 * n + 2)
                for q in range(PAIRS):
                    mm = pe.matmul(ring[0][:, 0:P], w_o[:, q, :], aT[:, q, :], start=(q == 0), stop=(q == PAIRS - 1))
                mm.then_inc(projected, 1)

            def rest(n, i, ahead):
                score(n, i)
                if ahead == 2:
                    project_qk(n + 2, (0, 1, 2))
                turn_probs(n)
                if ahead == 2:
                    project_qk(n + 2, (3,))
                mix(n)
                if ahead:
                    turn_k(n + 1, 0, 2 * n + 1)
                turn_att(n)
                if ahead:
                    turn_k(n + 1, 1, 2 * n + 2)
                project_out(n)
                if ahead:
                    turn_q_project_v(n + 1)

            def ffn_up(m):
                pe.wait_ge(xn_ready, m + 1)
                for c, (r0, rows) in enumerate(CHUNKS):
                    g_ps, v_ps = qk_ps[c % 2], qk_ps[2 + c % 2]
                    if c == 2:
                        pe.wait_ge(gelued, 3 * m + 1)
                        pe.wait_ge(gated, 3 * m + 1)
                    elif c == 0:
                        pe.wait_ge(gated, 3 * m)
                    pe.matmul(g_ps[0:rows, :], w_1[:, GATED + r0:GATED + r0 + rows], xn[:], start=True, stop=True).then_inc(gates, 1)
                    pe.matmul(v_ps[0:rows, :], w_1[:, r0:r0 + rows], xn[:], start=True, stop=True).then_inc(vals, 1)

            def ffn_down(m):
                pe.wait_ge(x0_out, m)
                for c, (r0, rows) in enumerate(CHUNKS):
                    pe.wait_ge(gated, 3 * m + c + 1)
                    mm = pe.matmul(ring[2][:], w_2[0:rows, c, :], act[0:rows, c, :], start=(c == 0), stop=(c == 2))
                mm.then_inc(ffn_out, 1)

            with pe.Fori(0, B) as b:
                pe.wait_ge(xf_ready, 2 * b + 2)
                ln.turn_in(pe, b, xf)
                pe.wait_ge(x0_first, b)
                ln.turn_back(pe, b)
            pe.wait_ge(mask_done, TILES)
            pe.wait_ge(x0_first, B)
            with pe.Fori(0, LAYERS) as l:
                pe.wait_ge(qk_in, 16 * l + 16)
                pe.wait_ge(v_in, 32 * l + 32)
                pe.wait_ge(o_in, 16 * l + 16)
                pe.wait_ge(x0_out, B * l)
                tile0 = l * NT
                project_qk(tile0, range(4))
                project_qk(tile0 + 1, range(4))
                for j in range(2):
                    turn_k(tile0, j, 2 * tile0)
                turn_q_project_v(tile0)
                with pe.Fori(0, NT - 2) as i:
                    rest(tile0 + i, i, 2)
                rest(tile0 + NT - 2, NT - 2, 1)
                rest(tile0 + NT - 1, NT - 1, 0)
                pe.wait_ge(ffn_in, 16 * FFN_LOADS * l + 16 * FFN_LOADS)
                pe.wait_ge(x1_out, NT * l + NT)
                first = B * l
                pe.wait_ge(xf_ready, 2 * (first + B) + 2)
                ln.turn_in(pe, first + B, xf)
                ln.turn_back(pe, first + B)
                with pe.Fori(0, B - 1) as b:
                    m = first + b
                    pe.wait_ge(xf_ready, 2 * (m + B) + 4)
                    ln.turn_in(pe, m + B + 1, xf)
                    ffn_up(m)
                    ln.turn_back(pe, m + B + 1)
                    ffn_down(m)
                ffn_up(first + B - 1)
                ffn_down(first + B - 1)

        @block.scalar
        def _(eng):
            def shifted_copy(dst, width, src, col, done):
                eng.copy(dst[0:64, 0:width], src[0:64, bass.ds(col, width)]).then_inc(done, 1)
                eng.copy(dst[64:128, 0:width], src[64:128, bass.ds(col - 1, width)]).then_inc(done, 1)

            def take_qk(n, i):
                eng.wait_ge(qk_proj, 4 * n)
                shifted_copy(xt, P, x0, column(i), xt_ready)

            def square(n, banks):
                for j in banks:
                    eng.wait_ge(qk_proj, 4 * n + j + 1)
                    if j == 0:
                        eng.wait_ge(norms, 2 * n)
                    eng.activation(sq[:, j // 2, j % 2 * BANK:(j % 2 + 1) * BANK], qk_ps[j][:], ACT.Square).then_inc(squared, 1)

            def take_v(n, i):
                eng.wait_ge(v_proj, 2 * n)
                shifted_copy(xv, P, x0, column(i), xv_ready)

            def rest(n, i, ahead):
                eng.wait_ge(scores, 2 * n)
                for j in (1, 0):
                    eng.wait_ge(qk_turned, 4 * n + 4 - j)
                    eng.copy(qT[:, 4 * j:4 * j + 4, :].rearrange("p q t -> p (q t)"), ring[j][:]).then_inc(qT_out, 1)

                def exp(h):
                    eng.wait_ge(shifted, 2 * n + h + 1)
                    eng.activation(probs[:, :, h, :], probs[:, :, h, :], ACT.Exp, scale=QK_SCALE).then_inc(exped, 1)

                def value(h, g, to, rows, source):
                    to += 64 * h
                    eng.copy(val[to:to + rows, g, :], ring[2 + h][source:source + rows, :]).then_inc(v_out, 1)

                if ahead == 2:
                    take_qk(n + 2, i + 2)
                eng.wait_ge(mixed, 2 * n)
                eng.wait_ge(v_out, 12 * n)
                eng.copy(val[:, 0, :], val[:, TILES, :]).then_inc(v_kept, 1)
                eng.wait_ge(v_kept, n + 1)
                for h in range(2):
                    eng.wait_ge(v_proj, 2 * n + h + 1)
                    value(h, 1, 0, 64, 0)
                    if h == 1:
                        exp(0)
                    value(h, 3, 0, 64, 64)
                    value(h, 2, 0, 32, 32)
                    value(h, 2, 32, 32, 64)
                    if h == 1:
                        exp(1)
                    value(h, 0, 32, 32, 0)
                    value(h, TILES, 0, 32, 96)
                if ahead:
                    take_v(n + 1, i + 1)
                if ahead == 2:
                    square(n + 2, (0, 1))
                eng.wait_ge(p_turned, 2 * n + 2)
                eng.wait_ge(mixed, 2 * n)
                eng.copy(pT[:, 4:8, :].rearrange("p q t -> p (q t)"), ring[1][:]).then_inc(p_out1, 1)
                if ahead == 2:
                    square(n + 2, (2, 3))
                eng.wait_ge(projected, n)
                for j in range(2):
                    eng.wait_ge(a_turned, 2 * n + j + 1)
                    eng.copy(aT[:, 4 * j:4 * j + 4, :].rearrange("p q t -> p (q t)"), ring[j][:]).then_inc(aT_out, 1)

            def affine(m):
                eng.wait_ge(ln.back, m + B + 1)
                eng.wait_ge(vals, 3 * m)
                eng.activation(xn[:], ring[1][:], ACT.Identity, bias=vecs[:, 8:9], scale=vecs[:, 7:8]).then_inc(xn_ready, 1)

            def gelu(m):
                for c, (r0, rows) in enumerate(CHUNKS):
                    eng.wait_ge(gates, 3 * m + c + 1)
                    eng.wait_ge(gated, 3 * m)
                    eng.activation(gate[0:rows, c, :], qk_ps[c % 2][0:rows, :], ACT.Gelu,
                                   bias=vecs[0:rows, 3 + c:4 + c]).then_inc(gelued, 1)

            eng.wait_ge(pads_done, 5)
            with eng.Fori(0, B) as b:
                eng.wait_ge(ln.turned, b)
                eng.copy(xf[0:64, :], shared.xs[0:64, bass.ds(b * T, T)]).then_inc(xf_ready, 1)
                eng.copy(xf[64:128, :], shared.xs[64:128, bass.ds(b * T, T)]).then_inc(xf_ready, 1)
                eng.wait_ge(ln.back, b + 1)
                eng.copy(x0[:, bass.ds(b * SEQ + LEAD + 1, T)], ring[1][:]).then_inc(x0_first, 1)
            eng.wait_ge(x0_first, B)
            with eng.Fori(0, LAYERS) as l:
                eng.wait_ge(x0_out, B * l)
                first = l * NT
                take_qk(first, 0)
                take_v(first, 0)
                square(first, range(4))
                take_qk(first + 1, 1)
                square(first + 1, range(4))
                with eng.Fori(0, NT - 2) as i:
                    rest(first + i, i, 2)
                rest(first + NT - 2, NT - 2, 1)
                rest(first + NT - 1, NT - 1, 0)
                eng.wait_ge(x1_out, first + NT)
                eng.wait_ge(ffn_in, 16 * FFN_LOADS * l + 16 * FFN_LOADS)
                m0 = B * l
                affine(m0)
                with eng.Fori(0, B - 1) as b:
                    gelu(m0 + b)
                    affine(m0 + b + 1)
                gelu(m0 + B - 1)

        @block.vector
        def _(dve):
            def squared_norms(n, w):
                dve.wait_ge(squared, 4 * n + 2 * w + 2)
                dve.wait_ge(floored, 2 * n)
                part = slice(HEADS * w, HEADS * w + HEADS)
                dve.tensor_reduce(n2[:, part], heads(sq[:, w, :]), AX.X, ALU.add).then_inc(norms, 1)
                dve.wait_ge(norms, 2 * n + w + 1)
                dve.wait_ge(rnorm, 2 * n)
                dve.tensor_scalar(n2c[:, part], n2[:, part], NORM_FLOOR, None, ALU.max).then_inc(floored, 1)

            def scale_to_one(n):
                dve.wait_ge(cosed, 2 * n)
                dve.wait_ge(sined_q, 2 * n)
                dve.wait_ge(sined_k, 2 * n)
                dve.wait_ge(rnorm, 2 * n + 2)
                for j in (2, 3, 0, 1):
                    dve.tensor_tensor(heads(qkn[:, j // 2, j % 2 * BANK:(j % 2 + 1) * BANK]), heads(qk_ps[j][:]),
                                      rn[:, 8 * j:8 * j + 8].unsqueeze(2).to_broadcast([P, 8, DH]),
                                      ALU.mult).then_inc(normed, 1)

            def table(a, w, i):
                row = a[:, w, bass.ds(i % TILES, 1), :] if not isinstance(i, int) else a[:, w, i % TILES:i % TILES + 1, :]
                return row.to_broadcast([P, HEADS, DH])

            def cosine(n, i):
                dve.wait_ge(qk_turned, 4 * n)
                for k, w in enumerate((1, 0)):
                    dve.wait_ge(normed, 4 * n + 2 * k + 2)
                    dve.tensor_tensor(heads(qkr[:, w, :]), heads(qkn[:, w, :]), table(cos, w, i), ALU.mult).then_inc(cosed, 1)

            def sine_q(n, i):
                dve.wait_ge(rotated, 2 * n)
                for half in range(2):
                    dve.tensor_tensor(heads(qks[:, 0, :])[:, :, 32 * half:32 * half + 32],
                                      heads(qkn[:, 0, :])[:, :, 32 - 32 * half:64 - 32 * half],
                                      half_table(0, i, half).to_broadcast([P, HEADS, 32]), ALU.mult).then_inc(sined_q, 1)

            def keys(n):
                dve.wait_ge(scores, 2 * n)
                dve.wait_ge(kT_out, 2 * n)
                dve.tensor_copy(kT[:, :, 0:WIN], kT[:, :, P:P + WIN]).then_inc(k_kept, 1)
                dve.wait_ge(k_kept, n + 1)
                for j in range(2):
                    dve.wait_ge(qk_turned, 4 * n + j + 1)
                    dve.tensor_copy(kT[:, 4 * j:4 * j + 4, WIN:WIN + P],
                                    ring[2 + j][:].rearrange("p (q t) -> p q t", t=P)).then_inc(kT_out, 1)

            def rest(n, i, ahead):
                if ahead:
                    scale_to_one(n + 1)
                dve.wait_ge(shifted, 2 * n)
                dve.wait_ge(p_turned, 2 * n)
                dve.wait_ge(summed, 2 * n)
                for h in range(2):
                    dve.wait_ge(scores, 2 * n + h + 1)
                    dve.tensor_reduce(top[:, h, :], heads(ring[h][:]), AX.X, ALU.max).then_inc(topped, 1)
                    dve.wait_ge(topped, 2 * n + h + 1)
                    dve.tensor_tensor(probs[:, :, h, :], heads(ring[h][:]),
                                      top[:, h, :].unsqueeze(2).to_broadcast([P, PAIRS, 2 * WIN]),
                                      ALU.subtract).then_inc(shifted, 1)
                if ahead:
                    cosine(n + 1, i + 1)
                dve.wait_ge(p_turned, 2 * n + 1)
                dve.wait_ge(mixed, 2 * n)
                dve.tensor_copy(pT[:, 0:4, :].rearrange("p q t -> p (q t)"), ring[0][:]).then_inc(p_out0, 1)
                if ahead:
                    sine_q(n + 1, i + 1)
                dve.wait_ge(inverted, n)
                for h in range(2):
                    dve.wait_ge(exped, 2 * n + h + 1)
                    dve.tensor_reduce(total[:, h, :], probs[:, :, h, :], AX.X, ALU.add).then_inc(summed, 1)
                dve.wait_ge(summed, 2 * n + 2)
                dve.wait_ge(att_out, 2 * n)
                dve.reciprocal(rtotal[:].rearrange("p h q -> p (h q)"), total[:].rearrange("p h q -> p (h q)")).then_inc(inverted, 1)
                dve.wait_ge(inverted, n + 1)
                dve.wait_ge(a_turned, 2 * n)
                for h in range(2):
                    dve.wait_ge(mixed, 2 * n + h + 1)
                    dve.tensor_tensor(att[:, :, h, :], heads(ring[2 + h][:]),
                                      rtotal[:, h, :].unsqueeze(2).to_broadcast([P, PAIRS, DH]),
                                      ALU.mult).then_inc(att_out, 1)
                if ahead == 2:
                    squared_norms(n + 2, 0)
                    squared_norms(n + 2, 1)
                if ahead:
                    keys(n + 1)
                dve.wait_ge(projected, n + 1)
                at = column(i)
                dve.tensor_tensor(x1[:, bass.ds(at, P)], ring[0][:, 0:P], x0[:, bass.ds(at, P)], ALU.add).then_inc(x1_out, 1)

            def take_ffn(m, b):
                col = b * SEQ + (LEAD + 1)
                dve.wait_ge(ln.turned, m + B)
                dve.tensor_copy(xf[0:64, :], x1[0:64, bass.ds(col, T)]).then_inc(xf_ready, 1)
                dve.tensor_copy(xf[64:128, :], x1[64:128, bass.ds(col - 1, T)]).then_inc(xf_ready, 1)

            def gated_product(m, chunks):
                dve.wait_ge(ffn_out, m)
                for c in chunks:
                    rows = CHUNKS[c][1]
                    dve.wait_ge(vals, 3 * m + c + 1)
                    dve.wait_ge(gelued, 3 * m + c + 1)
                    dve.scalar_tensor_tensor(act[0:rows, c, :], qk_ps[2 + c % 2][0:rows, :], vecs[0:rows, c:c + 1],
                                             gate[0:rows, c, :], ALU.add, ALU.mult).then_inc(gated, 1)

            def ffn_add(m, col):
                dve.wait_ge(ffn_out, m + 1)
                dve.scalar_tensor_tensor(x0[:, bass.ds(col, T)], ring[2][:], vecs[:, 6:7], x1[:, bass.ds(col, T)],
                                         ALU.add, ALU.add).then_inc(x0_out, 1)

            for a in (x0, x1):
                dve.memset(a[:, 0:LEAD], 0.0).then_inc(pads_done, 1)
                dve.memset(a[:, LEAD:].rearrange("p (b t) -> p b t", t=SEQ)[:, :, 0:1], 0.0).then_inc(pads_done, 1)
            dve.memset(val[:], 0.0).then_inc(pads_done, 1)
            dve.memset(kT[:], 0.0).then_inc(kT_clear, 1)
            dve.wait_ge(kT_clear, 1)
            with dve.Fori(0, B) as b:
                ln.statistics(dve, b)
                dve.wait_ge(ln.back, b)
                ln.normalise(dve, b)
            dve.wait_ge(const_in, 32)
            with dve.Fori(0, LAYERS) as l:
                first = l * NT
                dve.wait_ge(gains_in, 16 * 8 * l + 16 * 8)
                dve.wait_ge(rotated, 2 * first)
                dve.wait_ge(cosed, 2 * first)
                dve.wait_ge(sined_q, 2 * first)
                for side, tab in enumerate((cos, sin)):
                    for w in range(2):
                        dve.tensor_tensor(tab[:, w, :, :], trig[:, side, w, :, :],
                                          gains[:, side, w, :].unsqueeze(1).to_broadcast([P, TILES, DH]),
                                          ALU.mult).then_inc(tables, 1)
                dve.wait_ge(tables, 4 * l + 4)
                for w in range(2):
                    squared_norms(first, w)
                scale_to_one(first)
                cosine(first, 0)
                sine_q(first, 0)
                for w in range(2):
                    squared_norms(first + 1, w)
                keys(first)
                with dve.Fori(0, NT - 2) as i:
                    rest(first + i, i, 2)
                rest(first + NT - 2, NT - 2, 1)
                rest(first + NT - 1, NT - 1, 0)
                dve.wait_ge(ffn_in, 16 * FFN_LOADS * l + 16 * FFN_LOADS)
                m0 = B * l
                dve.wait_ge(x1_out, first + NT)
                take_ffn(m0, 0)
                ln.statistics(dve, m0 + B)
                take_ffn(m0 + 1, 1)
                dve.wait_ge(ln.back, m0 + B)
                ln.normalise(dve, m0 + B)

                def ffn(m, b, more):
                    ln.statistics(dve, m + B + 1)
                    gated_product(m, (0, 1))
                    if more:
                        take_ffn(m + 2, b + 2)
                    dve.wait_ge(ln.back, m + B + 1)
                    ln.normalise(dve, m + B + 1)
                    gated_product(m, (2,))
                    ffn_add(m, b * SEQ + (LEAD + 1))

                with dve.Fori(0, B - 2) as b:
                    ffn(m0 + b, b, True)
                ffn(m0 + B - 2, B - 2, False)
                gated_product(m0 + B - 1, range(len(CHUNKS)))
                ffn_add(m0 + B - 1, (B - 1) * SEQ + (LEAD + 1))

        @block.gpsimd
        def _(pool):
            def reciprocal_norms(n, w):
                part = slice(HEADS * w, HEADS * w + HEADS)
                pool.wait_ge(floored, 2 * n + w + 1)
                pool.wait_ge(normed, 4 * n)
                pool.tensor_tensor(rn[:, part], n2c[:, part], shared.minus_half[:, part], ALU.pow).then_inc(rnorm, 1)

            def rotate(n, i):
                pool.wait_ge(rotated, 2 * n)
                pool.wait_ge(normed, 4 * n + 2)
                for half in range(2):
                    pool.tensor_tensor(heads(qks[:, 1, :])[:, :, 32 * half:32 * half + 32],
                                       heads(qkn[:, 1, :])[:, :, 32 - 32 * half:64 - 32 * half],
                                       half_table(1, i, half).to_broadcast([P, HEADS, 32]), ALU.mult).then_inc(sined_k, 1)
                pool.wait_ge(cosed, 2 * n + 1)
                pool.wait_ge(sined_k, 2 * n + 2)
                pool.tensor_tensor(qkr[:, 1, :], qkr[:, 1, :], qks[:, 1, :], ALU.add).then_inc(rotated, 1)
                pool.wait_ge(cosed, 2 * n + 2)
                pool.wait_ge(sined_q, 2 * n + 2)
                pool.tensor_tensor(qkr[:, 0, :], qkr[:, 0, :], qks[:, 0, :], ALU.add).then_inc(rotated, 1)

            pool.wait_ge(const_in, 32)
            for t in range(TILES):
                pool.tensor_copy(mask8[:, t, :].rearrange("p (h k) -> p h k", h=PAIRS),
                                 mask[:, t:t + 1, :].to_broadcast([P, PAIRS, 2 * WIN])).then_inc(mask_done, 1)
            with pool.Fori(0, B) as b:
                ln.reciprocal_deviation(pool, b)
            with pool.Fori(0, LAYERS) as l:
                first = l * NT
                pool.wait_ge(tables, 4 * l + 4)
                for w in range(2):
                    reciprocal_norms(first, w)
                rotate(first, 0)
                for w in range(2):
                    reciprocal_norms(first + 1, w)
                with pool.Fori(0, NT - 2) as i:
                    rotate(first + i + 1, i + 1)
                    for w in range(2):
                        reciprocal_norms(first + i + 2, w)
                rotate(first + NT - 1, NT - 1)
                with pool.Fori(0, B) as b:
                    ln.reciprocal_deviation(pool, B * l + b + B)


def fold_heads(nc, shared, ins):
    with ExitStack() as ctx:
        mem = Memory(nc, ctx, "fold")
        names = ("L1_attn_P_q", "L1_attn_P_k", "L1_attn_P_v", "L1_attn_P_o")
        raw = mem.sb("raw", [P, 4, HEADS, DH])
        turned_w = mem.sb("turned", [P, 4, PAIRS, P])
        ps = [mem.bank(f"ps{k}") for k in range(4)]
        prod = [mem.bank(f"prod{k}") for k in range(4)]
        loaded, turned, taken, folded, kept = (mem.sem(n) for n in ("loaded", "turned", "taken", "folded", "kept"))
        block = ctx.enter_context(nc.Block())

        @block.sync
        def _(sp):
            for w, name in enumerate(names):
                sp.dma_start(raw[:, w, :, :], ins[name].rearrange("h d k -> d h k")).then_inc(loaded, 16)

        @block.tensor
        def _(pe):
            pe.wait_ge(loaded, 16 * 4)
            for w in range(4):
                for half in range(2):
                    n = 2 * w + half
                    if n >= 4:
                        pe.wait_ge(taken, n - 3)
                    for q in range(4):
                        first = 8 * half + 2 * q
                        turn = pe.transpose(ps[n % 4][:, q * P:(q + 1) * P],
                                            raw[:, w, first:first + 2, :].rearrange("p h k -> p (h k)"), shared.ident[:])
                    turn.then_inc(turned, 1)
            pe.wait_ge(taken, 8)
            for q in range(PAIRS):
                for h in range(2):
                    if q >= 2:
                        pe.wait_ge(kept, 4 * (q - 1))
                    rows = slice(64 * h, 64 * h + 64)
                    for w in range(2):
                        mm = pe.matmul(prod[2 * (q % 2) + h][:, w * P:(w + 1) * P],
                                       turned_w[rows, 2 * w, q, :], turned_w[rows, 2 * w + 1, q, :],
                                       start=True, stop=True, skip_group_check=True)
                    mm.then_inc(folded, 1)

        @block.vector
        def _(dve):
            for n in range(8):
                dve.wait_ge(turned, n + 1)
                dve.tensor_copy(turned_w[:, n // 2, 4 * (n % 2):4 * (n % 2) + 4, :].rearrange("p q d -> p (q d)"),
                                ps[n % 4][:]).then_inc(taken, 1)
            for n in range(HEADS):
                dve.wait_ge(folded, n + 1)
                for w, dst in enumerate((shared.w_score, shared.w_value)):
                    dve.tensor_copy(dst[:, n, :], prod[n % 4][:, w * P:(w + 1) * P]).then_inc(kept, 1)


def causal(nc, shared, ins):
    with ExitStack() as ctx:
        mem = Memory(nc, ctx, "cau")
        scale = float(DH) ** -0.5
        diag_in, diag = mem.sb("diag_in", [P, P]), mem.sb("diag", [P, P], BF16)
        xf = mem.sb("xf", [P, T])
        xn = mem.sb("xn", [P, T])
        w_head = mem.sb("w_head", [P, P])
        xa = mem.sb("xa", [P, T])
        u = mem.sb("u", [P, TILES, P])
        probs = mem.sb("probs", [P, TILES, T])
        pT = mem.sb("pT", [P, TILES, T])
        top = mem.sb("top", [P, TILES])
        bias = mem.sb("bias", [P, TILES])
        total = mem.sb("total", [P, TILES])
        rtotal = mem.sb("rtotal", [P, TILES])
        y = mem.sb("y", [P, TILES, P])
        sc = [mem.bank(f"scores{k}") for k in range(3)]
        tr = [mem.bank(f"turn{k}") for k in range(3)]
        out_ps, in_ps = mem.bank("out"), mem.bank("in")
        ln = LayerNorm(mem, shared, out_ps, in_ps)
        ROW = {3: (0, 0), 0: (1, 0), 2: (1, P), 1: (2, 0)}
        COL = {0: (0, 0), 1: (1, 0), 3: (1, 3 * P), 2: (2, 0)}
        BANK_ROWS = [[3], [0, 2], [1]]
        BANK_COLS = [[0], [1, 3], [2]]

        s = mem.sem
        const_in, diag_done = s("const_in"), s("diag_done")
        xf_ready, xn_ready = s("xf_ready"), s("xn_ready")
        w_ready = s("w_ready")
        xa_done, xa_out = s("xa_done"), s("xa_out")
        u_done, u_out = s("u_done"), s("u_out")
        scored = s("scored")
        topped, biased = s("topped"), s("biased")
        exped = s("exped")
        inverted = s("inverted")
        p_turned = s("p_turned")
        pT0_out, pT12_out = s("pT0_out"), s("pT12_out")
        mixed, added = s("mixed"), s("added")
        cleared = s("cleared")
        y_turned, xs_out = s("y_turned"), s("xs_out")
        block = ctx.enter_context(nc.Block())

        @block.sync
        def _(sp):
            sp.dma_start(diag_in[:], ins["c_diag"]).then_inc(const_in, 16)

        @block.tensor
        def _(pe):
            def query(m, values):
                pe.wait_ge(w_ready, m + 1)
                pe.wait_ge(u_out, values)
                pe.matmul(in_ps[:], w_head[:], xn[:], start=True, stop=True).then_inc(xa_done, 1)

            def score(m):
                pe.wait_ge(xa_out, m + 1)
                pe.wait_ge(exped, 4 * m)
                for k, rows in enumerate(BANK_ROWS):
                    for i in rows:
                        c0, keys = ROW[i][1], (i + 1) * P
                        pe.matmul(sc[k][:, c0:c0 + keys], xa[:, i * P:(i + 1) * P], xn[:, 0:keys],
                                  start=True, stop=False, skip_group_check=True)
                        mm = pe.matmul(sc[k][:, c0 + i * P:c0 + keys], shared.identb[:], diag[:],
                                       start=False, stop=True, skip_group_check=True)
                    mm.then_inc(scored, 1)

            def turn(m):
                pe.wait_ge(exped, 4 * m + 4)
                pe.wait_ge(pT0_out, m)
                pe.wait_ge(pT12_out, 3 * m)
                for k, cols in enumerate(BANK_COLS):
                    for j in cols:
                        for i in range(j, TILES):
                            c0 = COL[j][1] + (i - j) * P
                            tp = pe.transpose(tr[k][:, c0:c0 + P], probs[:, i, j * P:(j + 1) * P], shared.ident[:])
                    tp.then_inc(p_turned, 1)

            def value(m, h):
                for t in range(TILES):
                    w = shared.w_value[:, h, :] if isinstance(h, int) else \
                        shared.w_value[:, bass.ds(h, 1), :].rearrange("p o d -> p (o d)")
                    mm = pe.matmul(in_ps[:, t * P:(t + 1) * P], xn[:, t * P:(t + 1) * P], w,
                                   start=True, stop=True, skip_group_check=True)
                mm.then_inc(u_done, 1)

            def mix(m):
                pe.wait_ge(u_out, m + 1)
                pe.wait_ge(pT0_out, m + 1)
                pe.wait_ge(pT12_out, 3 * m + 3)
                pe.wait_ge(added, 4 * m)
                for i in range(TILES):
                    for j in range(i + 1):
                        mm = pe.matmul(out_ps[:, i * P:(i + 1) * P], pT[:, j, i * P:(i + 1) * P], u[:, j, :],
                                       start=(j == 0), stop=(j == i), skip_group_check=True)
                mm.then_inc(mixed, 1)

            pe.wait_ge(diag_done, 1)
            with pe.Fori(0, B) as b:
                pe.wait_ge(xf_ready, b + 1)
                pe.wait_ge(xs_out, b)
                ln.turn_in(pe, b, xf)
                pe.wait_ge(u_out, HEADS * b)
                ln.turn_back(pe, b)
                pe.wait_ge(xn_ready, b + 1)
                m0 = HEADS * b
                query(m0, m0)
                score(m0)
                with pe.Fori(0, HEADS - 1) as h:
                    query(m0 + h + 1, m0 + h)
                    turn(m0 + h)
                    pe.wait_ge(xa_out, m0 + h + 2)
                    value(m0 + h, h)
                    score(m0 + h + 1)
                    mix(m0 + h)
                turn(m0 + HEADS - 1)
                value(m0 + HEADS - 1, HEADS - 1)
                mix(m0 + HEADS - 1)
                pe.wait_ge(added, 4 * m0 + 4 * HEADS)
                for t in range(TILES):
                    tp = pe.transpose(out_ps[:, t * P:(t + 1) * P], y[:, t, :], shared.ident[:])
                tp.then_inc(y_turned, 1)

        @block.scalar
        def _(act):
            def query_out(m):
                act.wait_ge(xa_done, m + 1)
                act.wait_ge(scored, 3 * m)
                act.copy(xa[:], in_ps[:]).then_inc(xa_out, 1)

            def exponentials(m):
                act.wait_ge(biased, m + 1)
                act.wait_ge(p_turned, 3 * m)
                act.wait_ge(inverted, m)
                for k in range(3):
                    for i in BANK_ROWS[k]:
                        c0, keys = ROW[i][1], (i + 1) * P
                        act.activation(probs[:, i, 0:keys], sc[k][:, c0:c0 + keys], ACT.Exp, bias=bias[:, i:i + 1],
                                       scale=scale, accum_out=total[:, i:i + 1]).then_inc(exped, 1)

            def values_out(m):
                act.wait_ge(p_turned, 3 * m + 1)
                act.wait_ge(mixed, m)
                act.copy(pT[:, 0, :], tr[0][:]).then_inc(pT0_out, 1)
                act.wait_ge(u_done, m + 1)
                act.copy(u[:].rearrange("p t d -> p (t d)"), in_ps[:]).then_inc(u_out, 1)

            with act.Fori(0, B) as b:
                act.wait_ge(ln.turned, b)
                act.copy(xf[:], shared.xs[:, bass.ds(b * T, T)]).then_inc(xf_ready, 1)
                act.wait_ge(ln.back, b + 1)
                act.wait_ge(u_done, HEADS * b)
                act.wait_ge(scored, 3 * HEADS * b)
                act.copy(xn[:], in_ps[:]).then_inc(xn_ready, 1)
                m0 = HEADS * b
                query_out(m0)
                exponentials(m0)
                with act.Fori(0, HEADS - 1) as h:
                    query_out(m0 + h + 1)
                    values_out(m0 + h)
                    exponentials(m0 + h + 1)
                values_out(m0 + HEADS - 1)

        @block.vector
        def _(dve):
            def maxima(m):
                dve.wait_ge(biased, m)
                for k in range(3):
                    dve.wait_ge(scored, 3 * m + k + 1)
                    for i in BANK_ROWS[k]:
                        c0, keys = ROW[i][1], (i + 1) * P
                        dve.tensor_reduce(top[:, i:i + 1], sc[k][:, c0:c0 + keys], AX.X, ALU.max).then_inc(topped, 1)
                dve.wait_ge(topped, 4 * m + 4)
                dve.wait_ge(exped, 4 * m)
                dve.tensor_scalar(bias[:], top[:], -scale, None, ALU.mult).then_inc(biased, 1)

            def invert(m):
                dve.wait_ge(exped, 4 * m + 4)
                dve.wait_ge(added, 4 * m)
                dve.reciprocal(rtotal[:], total[:]).then_inc(inverted, 1)

            def turned_out(m):
                dve.wait_ge(mixed, m)
                dve.wait_ge(p_turned, 3 * m + 2)
                dve.tensor_copy(pT[:, 1, P:T], tr[1][:, 0:3 * P]).then_inc(pT12_out, 1)
                dve.tensor_copy(pT[:, 3, 3 * P:T], tr[1][:, 3 * P:T]).then_inc(pT12_out, 1)
                dve.wait_ge(p_turned, 3 * m + 3)
                dve.tensor_copy(pT[:, 2, 2 * P:T], tr[2][:, 0:2 * P]).then_inc(pT12_out, 1)

            def add(m):
                dve.wait_ge(mixed, m + 1)
                dve.wait_ge(inverted, m + 1)
                dve.wait_ge(added, 4 * m)
                for t in range(TILES):
                    dve.scalar_tensor_tensor(y[:, t, :], out_ps[:, t * P:(t + 1) * P], rtotal[:, t:t + 1], y[:, t, :],
                                             ALU.mult, ALU.add).then_inc(added, 1)

            dve.wait_ge(const_in, 16)
            dve.tensor_copy(diag[:], diag_in[:]).then_inc(diag_done, 1)
            with dve.Fori(0, B) as b:
                ln.statistics(dve, b)
                dve.wait_ge(ln.back, b)
                ln.normalise(dve, b)
                dve.wait_ge(y_turned, b)
                dve.memset(y[:], 0.0).then_inc(cleared, 1)
                dve.wait_ge(cleared, b + 1)
                m0 = HEADS * b
                maxima(m0)
                invert(m0)
                with dve.Fori(0, HEADS - 1) as h:
                    turned_out(m0 + h)
                    maxima(m0 + h + 1)
                    add(m0 + h)
                    invert(m0 + h + 1)
                turned_out(m0 + HEADS - 1)
                add(m0 + HEADS - 1)
                dve.wait_ge(y_turned, b + 1)
                dve.tensor_tensor(shared.xs[:, bass.ds(b * T, T)], shared.xs[:, bass.ds(b * T, T)], out_ps[:],
                                  ALU.add).then_inc(xs_out, 1)

        @block.gpsimd
        def _(pool):
            with pool.Fori(0, B) as b:
                ln.reciprocal_deviation(pool, b)
                with pool.Fori(0, HEADS) as h:
                    pool.wait_ge(xa_done, HEADS * b + h)
                    pool.tensor_copy(w_head[:], shared.w_score[:, bass.ds(h, 1), :].rearrange("p o d -> p (o d)")).then_inc(w_ready, 1)


STAGES = 9
HIDDEN = 4 * D
HCH = HIDDEN // P


def fold_butterflies(nc, shared, ins):
    with ExitStack() as ctx:
        mem = Memory(nc, ctx, "fly")
        w_up = mem.sb("w_up", [P, STAGES, HIDDEN // 2, 2, 2])
        w_down = mem.sb("w_down", [P, STAGES, HIDDEN // 2, 2, 2])
        up = mem.sb("up", [P, 2, HIDDEN])
        up_same, up_cross = mem.sb("up_same", [P, 2, HIDDEN]), mem.sb("up_cross", [P, 2, HIDDEN])
        w_con = mem.sb("w_con", [P, HCH, P])
        down = mem.sb("down", [P, 1, HIDDEN])
        dn_same, dn_cross = mem.sb("dn_same", [P, 1, HIDDEN]), mem.sb("dn_cross", [P, 1, HIDDEN])
        bias_in = mem.sb("bias_in", [P, HCH + 2])
        con_ps, turn_ps, bias_ps = mem.bank("con"), mem.bank("turn"), mem.bank("bias")
        s = mem.sem
        up_in, down_in, bias_loaded = s("up_in"), s("down_in"), s("bias_loaded")
        cleared, con_turned, con_out = s("cleared"), s("con_turned"), s("con_out")
        up_parts, up_steps, dn_parts, dn_steps = s("up_parts"), s("up_steps"), s("dn_parts"), s("dn_steps")
        turned, bias_turned, done = s("turned"), s("bias_turned"), s("done")
        block = ctx.enter_context(nc.Block())

        def butterfly(eng, cur, same, cross, w, order, transposed, parts, steps):
            blocks = cur.shape[1]
            for n, stage in enumerate(order):
                st = 2 ** stage
                pair = lambda a, half: a[:].rearrange("p k (n two s) -> p k n two s", two=2, s=st)[:, :, :, half, :]

                def weight(o, i):
                    v = w[:, stage, :, o, i].rearrange("p (k n s) -> p k n s", k=1, s=st)
                    return v.to_broadcast([P, blocks, HIDDEN // 2 // st, st])

                eng.wait_ge(steps, n)
                for o in range(2):
                    i = 1 - o
                    eng.tensor_tensor(pair(same, o), pair(cur, o), weight(o, o), ALU.mult).then_inc(parts, 1)
                    eng.tensor_tensor(pair(cross, o), pair(cur, i), weight(*((i, o) if transposed else (o, i))),
                                      ALU.mult).then_inc(parts, 1)
                eng.wait_ge(parts, 4 * n + 4)
                eng.tensor_tensor(cur[:], same[:], cross[:], ALU.add).then_inc(steps, 1)

        @block.sync
        def _(sp):
            sp.dma_start(w_con[:], ins["L0_ffn_W_con"].rearrange("(c p) d -> p c d", p=P)).then_inc(down_in, 16)
            sp.wait_ge(cleared, 1)
            sp.dma_start(up[:, 0, :], ins["L0_ffn_W_exp"]).then_inc(up_in, 16)
            sp.dma_start(up[0:1, 1, :], ins["L0_ffn_b_exp"].rearrange("(o h) -> o h", o=1)).then_inc(up_in, 16)
            for w, name, done_ in ((w_up, "L0_ffn_up_weights", up_in), (w_down, "L0_ffn_down_weights", down_in)):
                src = ins[name].rearrange("(q s) k a b -> q (s k a b)", q=1)
                sp.dma_start(w[:].rearrange("p s k a b -> p (s k a b)"), src.to_broadcast([P, STAGES * 2 * HIDDEN])).then_inc(done_, 16)
            sp.dma_start(bias_in[:, 0:HCH], ins["L0_ffn_up_bias"].rearrange("(c p) -> p c", p=P), allow_slow_non_contiguous=True).then_inc(bias_loaded, 16)
            for k, name in enumerate(("L0_ffn_b_con", "L0_ffn_down_bias")):
                sp.dma_start(bias_in[:, HCH + k:HCH + k + 1], ins[name].rearrange("(p o) -> p o", o=1)).then_inc(bias_loaded, 16)

        @block.tensor
        def _(pe):
            pe.wait_ge(down_in, 32)
            for c in range(HCH):
                turn = pe.transpose(con_ps[:, c * P:(c + 1) * P], w_con[:, c, :], shared.ident[:])
            turn.then_inc(con_turned, 1)
            pe.wait_ge(up_steps, STAGES)
            for c in range(HCH):
                mm = pe.matmul(bias_ps[:, c:c + 1], up[0:1, 1, c * P:(c + 1) * P], shared.ident[0:1, 0:1],
                               start=True, stop=True, skip_group_check=True)
            mm.then_inc(bias_turned, 1)
            pe.wait_ge(dn_steps, STAGES)
            for c in range(HCH):
                turn = pe.transpose(turn_ps[:, c * P:(c + 1) * P], down[:, 0, c * P:(c + 1) * P], shared.ident[:])
            turn.then_inc(turned, 1)

        @block.scalar
        def _(act):
            act.wait_ge(con_turned, 1)
            act.copy(down[:, 0, :], con_ps[:]).then_inc(con_out, 1)
            act.wait_ge(turned, 1)
            act.copy(shared.w_down[:].rearrange("p c d -> p (c d)"), turn_ps[:]).then_inc(done, 1)
            act.wait_ge(up_steps, STAGES)
            act.copy(shared.w_up[:], up[:, 0, :]).then_inc(done, 1)

        @block.vector
        def _(dve):
            dve.memset(up[:], 0.0).then_inc(cleared, 1)
            dve.wait_ge(up_in, 16 * 3)
            butterfly(dve, up, up_same, up_cross, w_up, range(STAGES), False, up_parts, up_steps)
            dve.wait_ge(bias_loaded, 16 * 3)
            dve.wait_ge(bias_turned, 1)
            dve.tensor_tensor(shared.up_bias[:], bias_ps[:, 0:HCH], bias_in[:, 0:HCH], ALU.add).then_inc(done, 1)
            dve.tensor_tensor(shared.down_bias[:], bias_in[:, HCH:HCH + 1], bias_in[:, HCH + 1:HCH + 2], ALU.add).then_inc(done, 1)

        @block.gpsimd
        def _(pool):
            pool.wait_ge(down_in, 32)
            pool.wait_ge(con_out, 1)
            butterfly(pool, down, dn_same, dn_cross, w_down, range(STAGES - 1, -1, -1), True, dn_parts, dn_steps)


def rwkv_ffn(nc, shared, ins):
    with ExitStack() as ctx:
        mem = Memory(nc, ctx, "rwkv")
        K_CLAMP, K_EPS = 60.0, 1e-8
        w_kvr = mem.sb("w_kvr", [P, 3, HIDDEN])
        w_o = mem.sb("w_o", [P, HCH, P])
        c_k, c_v, c_r = mem.sb("c_k", [P, HIDDEN]), mem.sb("c_v", [P, HCH, P]), mem.sb("c_r", [P, P])
        row_g, row_b = mem.sb("row_g", [P, 1, P]), mem.sb("row_b", [P, 1, P])
        VEC = ("pre_g", "pre_b", "post_g", "post_b", "tm_mix_k", "tm_mix_v", "tm_mix_r", "cm_mix_k", "cm_mix_r")
        vec = mem.sb("vec", [P, len(VEC)])
        rest = mem.sb("rest", [P, 5])
        time = mem.sb("time", [P, 2, HCH])
        timed = mem.sb("timed", [P, 2, HCH])
        growth = mem.sb("growth", [P, HCH])
        rows = mem.sb("rows", [P, TILES, P])
        z1, z2, z3 = (mem.sb(n, [P, TILES, P]) for n in ("z1", "z2", "z3"))
        x0T = mem.sb("x0T", [P, T])
        xa = mem.sb("xa", [P, T])
        xb, xb_in = mem.sb("xb", [P, T]), mem.sb("xb_in", [P, T])
        xc = mem.sb("xc", [P, T])
        xd = mem.sb("xd", [P, T])
        xn, xn_c = mem.sb("xn", [P, 1 + T]), mem.sb("xn_c", [P, 1 + T])
        late, late_c = mem.sb("late", [P, 3, T]), mem.sb("late_c", [P, 2, T])
        mixed_in, mixed_c = mem.sb("mixed_in", [P, 3, T]), mem.sb("mixed_c", [P, 2, T])
        low = mem.sb("low", [P, 2, T])
        key, kv = mem.sb("key", [P, 2, T]), mem.sb("kv", [P, 2, T])
        gate = mem.sb("gate", [P, 2, T])
        gate1, numer = mem.sb("gate1", [P, T]), mem.sb("numer", [P, T])
        sk, skv = mem.sb("sk", [P, 1 + T]), mem.sb("skv", [P, 1 + T])
        wk, wkv, den, rden = (mem.sb(n, [P, T]) for n in ("wk", "wkv", "den", "rden"))
        out_c = mem.sb("out_c", [P, HCH, T])
        hid = mem.sb("hid", [P, HCH, T])
        sig = mem.sb("sig", [P, T])
        xnf = mem.sb("xnf", [P, T])
        k_ps, v_ps, r_ps, o_ps = mem.bank("k"), mem.bank("v"), mem.bank("r"), mem.bank("o")
        tok_ps, up_ps, y_ps = mem.bank("tok"), [mem.bank("up0"), mem.bank("up1")], mem.bank("y")
        lns = LayerNorm(mem, shared, tok_ps, r_ps)
        mem.prefix = "rwkvf"
        lnf = LayerNorm(mem, shared, tok_ps, up_ps[1])
        mem.prefix = "rwkv"

        s = mem.sem
        w_in, x_in = s("w_in"), s("x_in")
        prep = s("prep")
        time_exp = s("time_exp")
        scaled, xa_tok = s("scaled"), s("xa_tok")
        x_turned, z_turned = s("x_turned"), s("z_turned")
        x0_out, xa_out = s("x0_out"), s("xa_out")
        xn_out, late_out, blended = s("xn_out"), s("late_out"), s("blended")
        kvr = s("kvr")
        lowed, keyed, gated, gated1 = s("lowed"), s("keyed"), s("gated"), s("gated1")
        kv_done, scanned, firsts = s("kv_done"), s("scanned"), s("firsts")
        den_done, rden_done = s("den_done"), s("rden_done")
        numerated, out_done = s("numerated"), s("out_done")
        o_done, xb_done, xb_in_done = s("o_done"), s("xb_done"), s("xb_in_done")
        xn_c_out, late_c_out, blended_c = s("xn_c_out"), s("late_c_out"), s("blended_c")
        up_done, hid_done = s("up_done"), s("hid_done")
        cr_done, sig_done, y_done = s("cr_done"), s("sig_done"), s("y_done")
        xc_done, xd_done, xnf_out, xs_out = s("xc_done"), s("xd_done"), s("xnf_out"), s("xs_out")
        WLOADS = 3 + 1 + 3 + 2 + len(VEC) + 2
        block = ctx.enter_context(nc.Block())

        def rounds(engine, both):
            both(0, None)
            with engine.Fori(0, B - 1) as b:
                both(b + 1, b)
            both(None, B - 1)

        @block.sync
        def _(sp):
            name = lambda n: ins["L0_attn_" + n]
            sp.dma_start(rows[:], ins["L0_attn_x"][0].rearrange("(t p) d -> p t d", p=P)).then_inc(x_in, 16)
            for k, v in enumerate(VEC):
                sp.dma_start(vec[:, k:k + 1], name(v).rearrange("(p o) -> p o", o=1)).then_inc(w_in, 16)
            for k, v in enumerate(("tm_decay", "tm_first")):
                sp.dma_start(time[:, k, :], name(v).rearrange("(c p) -> p c", p=P), allow_slow_non_contiguous=True).then_inc(w_in, 16)
            for dst, v in ((row_g, "ln0_g"), (row_b, "ln0_b")):
                sp.dma_start(dst[:, 0, :], name(v).rearrange("(o d) -> o d", o=1).to_broadcast([P, D])).then_inc(w_in, 16)
            for k, v in enumerate(("tm_Wk", "tm_Wv", "tm_Wr")):
                sp.dma_start(w_kvr[:, k, :], name(v)).then_inc(w_in, 16)
            sp.dma_start(w_o[:], name("tm_Wo").rearrange("(c p) d -> p c d", p=P)).then_inc(w_in, 16)
            sp.dma_start(c_k[:], name("cm_Wk")).then_inc(w_in, 16)
            sp.dma_start(c_v[:], name("cm_Wv").rearrange("(c p) d -> p c d", p=P)).then_inc(w_in, 16)
            sp.dma_start(c_r[:], name("cm_Wr")).then_inc(w_in, 16)
            with sp.Fori(1, B) as b:
                sp.wait_ge(lns.back, b)
                src = ins["L0_attn_x"][bass.ds(b, 1)].rearrange("o (t p) d -> p (o t) d", p=P)
                sp.dma_start(rows[:], src).then_inc(x_in, 16)

        @block.tensor
        def _(pe):
            def turn_input(a):
                pe.wait_ge(x_in, 16 * a + 16)
                pe.wait_ge(lowed, HCH * a)
                for t in range(TILES):
                    turn = pe.transpose(k_ps[:, t * P:(t + 1) * P], rows[:, t, :], shared.ident[:])
                turn.then_inc(x_turned, 1)

            def turn_stream(a):
                pe.wait_ge(xa_tok, a + 1)
                pe.wait_ge(kv_done, HCH * a)
                for t in range(TILES):
                    turn = pe.transpose(v_ps[:, t * P:(t + 1) * P], z3[:, t, :], shared.ident[:])
                turn.then_inc(z_turned, 1)

            def turn_normalised(a):
                pe.wait_ge(gated, HCH * a)
                lns.turn_back(pe, 3 * a + 2)

            def project_chunk(a, c):
                if c == 0:
                    pe.wait_ge(x0_out, a + 1)
                    pe.wait_ge(xa_out, a + 1)
                for j, (bank, read) in enumerate(((k_ps, lowed), (v_ps, kv_done), (r_ps, gated))):
                    if c == 0:
                        pe.wait_ge(blended, 3 * a + j + 1)
                    else:
                        pe.wait_ge(read, HCH * a + c)
                    pe.matmul(bank[:], w_kvr[:, j, c * P:(c + 1) * P], mixed_in[:, j, :],
                              start=True, stop=True).then_inc(kvr, 1)

            def project_time(a):
                pe.wait_ge(xb_done, a)
                for c in range(HCH):
                    pe.wait_ge(out_done, HCH * a + c + 1)
                    mm = pe.matmul(o_ps[:], w_o[:, c, :], out_c[:, c, :], start=(c == 0), stop=(c == HCH - 1))
                mm.then_inc(o_done, 1)

            def turn_xb_in(b):
                pe.wait_ge(xb_done, b + 1)
                lnf.turn_in(pe, 2 * b, xb)

            def turn_xb_back(b):
                pe.wait_ge(hid_done, 8 * b)
                lnf.turn_back(pe, 2 * b)

            def channel_up(b):
                pe.wait_ge(blended_c, 2 * b + 2)
                pe.matmul(tok_ps[:], c_r[:], mixed_c[:, 1, :], start=True, stop=True).then_inc(cr_done, 1)
                for c in range(HCH):
                    if c >= 2:
                        pe.wait_ge(hid_done, 8 * b + c - 1)
                    pe.matmul(up_ps[c % 2][:], c_k[:, c * P:(c + 1) * P], mixed_c[:, 0, :], start=True, stop=True).then_inc(up_done, 1)

            def channel_down(b):
                pe.wait_ge(xs_out, b)
                for c in range(HCH):
                    pe.wait_ge(hid_done, 8 * b + c + 1)
                    mm = pe.matmul(y_ps[:], c_v[:, c, :], hid[:, c, :], start=(c == 0), stop=(c == HCH - 1))
                mm.then_inc(y_done, 1)

            def turn_xd_in(b):
                pe.wait_ge(xd_done, b + 1)
                pe.wait_ge(sig_done, b + 1)
                lnf.turn_in(pe, 2 * b + 1, xd)

            def ffn_up(b):
                pe.wait_ge(hid_done, 8 * b + 4)
                lnf.turn_back(pe, 2 * b + 1)
                pe.wait_ge(xnf_out, b + 1)
                for c in range(HCH):
                    if c >= 2:
                        pe.wait_ge(hid_done, 8 * b + 4 + c - 1)
                    pe.matmul(up_ps[c % 2][:], shared.w_up[:, c * P:(c + 1) * P], xnf[:], start=True, stop=True).then_inc(up_done, 1)

            def ffn_down(b):
                pe.wait_ge(xd_done, b + 1)
                for c in range(HCH):
                    pe.wait_ge(hid_done, 8 * b + 4 + c + 1)
                    mm = pe.matmul(y_ps[:], shared.w_down[:, c, :], hid[:, c, :], start=(c == 0), stop=(c == HCH - 1))
                mm.then_inc(y_done, 1)

            def both(a, b):
                if a is not None:
                    turn_input(a)
                if b is not None:
                    turn_xb_in(b)
                    turn_xb_back(b)
                if a is not None:
                    turn_stream(a)
                if b is not None:
                    channel_up(b)
                if a is not None:
                    turn_normalised(a)
                    project_chunk(a, 0)
                if b is not None:
                    channel_down(b)
                if a is not None:
                    project_chunk(a, 1)
                if b is not None:
                    turn_xd_in(b)
                if a is not None:
                    project_chunk(a, 2)
                if b is not None:
                    ffn_up(b)
                if a is not None:
                    project_chunk(a, 3)
                if b is not None:
                    ffn_down(b)
                if a is not None:
                    project_time(a)

            pe.wait_ge(w_in, 16 * WLOADS)
            rounds(pe, both)

        @block.scalar
        def _(act):
            def spread(bank, g, out, shifted, first_rest, out_sem, shifted_sem, n, used):
                count = shifted.shape[1]
                act.wait_ge(used, count * n)
                act.activation(out[:, 1:], bank[:], ACT.Identity, bias=vec[:, g + 1:g + 2],
                               scale=vec[:, g:g + 1]).then_inc(out_sem, 1)
                act.wait_ge(out_sem, n + 1)
                for j in range(count):
                    k = first_rest + j
                    act.activation(shifted[:, j, :], out[:, 0:T], ACT.Copy, scale=rest[:, k:k + 1]).then_inc(shifted_sem, 1)

            def input_out(a):
                act.wait_ge(x_turned, a + 1)
                act.wait_ge(xb_in_done, a)
                act.copy(x0T[:], k_ps[:]).then_inc(x0_out, 1)

            def stream_out(a):
                act.wait_ge(z_turned, a + 1)
                act.wait_ge(xb_done, a)
                act.copy(xa[:], v_ps[:]).then_inc(xa_out, 1)

            def time_inputs(a):
                act.wait_ge(lns.back, a + 1)
                spread(lns.feat, 0, xn, late, 0, xn_out, late_out, a, blended)

            def chunk(a, c):
                act.wait_ge(lowed, HCH * a + c + 1)
                if c >= 2:
                    act.wait_ge(firsts, 8 * a + 2 * c - 2)
                    act.wait_ge(gated1, HCH * a + c - 1)
                act.activation(key[:, c % 2, :], low[:, c % 2, :], ACT.Exp).then_inc(keyed, 1)
                act.wait_ge(kvr, 12 * a + 3 * c + 3)
                act.activation(gate[:, c % 2, :], r_ps[:], ACT.Tanh, scale=0.5).then_inc(gated, 1)

            def channel_inputs(b):
                act.wait_ge(lnf.back, 2 * b + 1)
                spread(lnf.feat, 2, xn_c, late_c, 3, xn_c_out, late_c_out, b, blended_c)

            def channel_hidden(b):
                act.wait_ge(y_done, 2 * b)
                for c in range(HCH):
                    act.wait_ge(up_done, 8 * b + c + 1)
                    act.activation(hid[:, c, :], up_ps[c % 2][:], ACT.Silu).then_inc(hid_done, 1)
                act.wait_ge(cr_done, b + 1)
                act.wait_ge(xc_done, b)
                act.activation(sig[:], tok_ps[:], ACT.Tanh, scale=0.5).then_inc(sig_done, 1)

            def ffn_input(b):
                act.wait_ge(lnf.back, 2 * b + 2)
                act.copy(xnf[:], lnf.feat[:]).then_inc(xnf_out, 1)

            def ffn_hidden(b):
                act.wait_ge(y_done, 2 * b + 1)
                for c in range(HCH):
                    act.wait_ge(up_done, 8 * b + 4 + c + 1)
                    act.activation(hid[:, c, :], up_ps[c % 2][:], ACT.Gelu, bias=shared.up_bias[:, c:c + 1]).then_inc(hid_done, 1)

            def both(a, b):
                if a is not None:
                    input_out(a)
                if b is not None:
                    channel_inputs(b)
                if a is not None:
                    stream_out(a)
                if b is not None:
                    channel_hidden(b)
                if a is not None:
                    time_inputs(a)
                    for c in range(3):
                        chunk(a, c)
                if b is not None:
                    ffn_input(b)
                    ffn_hidden(b)
                if a is not None:
                    chunk(a, 3)

            act.wait_ge(w_in, 16 * WLOADS)
            act.activation(growth[:], time[:, 0, :], ACT.Exp).then_inc(time_exp, 1)
            act.activation(timed[:, 1, :], time[:, 1, :], ACT.Exp).then_inc(time_exp, 1)
            act.wait_ge(time_exp, 2)
            act.activation(timed[:, 0, :], growth[:], ACT.Exp, scale=-1.0).then_inc(time_exp, 1)
            act.wait_ge(prep, 5)
            rounds(act, both)

        @block.vector
        def _(dve):
            def blend(stream, shifted, out, first_mix, shifted_sem, out_sem, n):
                count = shifted.shape[1]
                for j in range(count):
                    k = 4 + first_mix + j
                    dve.wait_ge(shifted_sem, count * n + j + 1)
                    dve.scalar_tensor_tensor(out[:, j, :], stream[:, 1:], vec[:, k:k + 1], shifted[:, j, :],
                                             ALU.mult, ALU.add).then_inc(out_sem, 1)

            def chunk(a, c):
                n = HCH * a + c
                dve.wait_ge(kvr, 12 * a + 3 * c + 1)
                if c >= 2:
                    dve.wait_ge(keyed, HCH * a + c - 1)
                dve.tensor_scalar(low[:, c % 2, :], k_ps[:], K_CLAMP, None, ALU.min).then_inc(lowed, 1)
                dve.wait_ge(keyed, n + 1)
                dve.wait_ge(kvr, 12 * a + 3 * c + 2)
                dve.wait_ge(firsts, 2 * n)
                dve.tensor_tensor(kv[:, c % 2, :], key[:, c % 2, :], v_ps[:], ALU.mult).then_inc(kv_done, 1)
                decay = timed[:, 0, c:c + 1].to_broadcast([P, T])
                dve.tensor_tensor_scan(sk[:, 1:], decay, key[:, c % 2, :], 0.0, ALU.mult, ALU.add).then_inc(scanned, 1)
                dve.wait_ge(kv_done, n + 1)
                dve.tensor_tensor_scan(skv[:, 1:], decay, kv[:, c % 2, :], 0.0, ALU.mult, ALU.add).then_inc(scanned, 1)
                dve.wait_ge(scanned, 2 * n + 1)
                dve.wait_ge(den_done, n)
                dve.scalar_tensor_tensor(wk[:], key[:, c % 2, :], timed[:, 1, c:c + 1], sk[:, 0:T],
                                         ALU.mult, ALU.add).then_inc(firsts, 1)
                dve.wait_ge(scanned, 2 * n + 2)
                dve.wait_ge(numerated, n)
                dve.scalar_tensor_tensor(wkv[:], kv[:, c % 2, :], timed[:, 1, c:c + 1], skv[:, 0:T],
                                         ALU.mult, ALU.add).then_inc(firsts, 1)
                dve.wait_ge(firsts, 2 * n + 1)
                dve.wait_ge(rden_done, n)
                dve.tensor_scalar(den[:], wk[:], K_EPS, 2.0, ALU.add, ALU.mult).then_inc(den_done, 1)
                dve.wait_ge(den_done, n + 1)
                dve.wait_ge(out_done, n)
                dve.reciprocal(rden[:], den[:]).then_inc(rden_done, 1)

            def both(a, b):
                u = None if a is None else 3 * a
                if a is not None:
                    dve.wait_ge(x_in, 16 * a + 16)
                    lns.statistics(dve, u, rows)
                if b is not None:
                    lnf.statistics(dve, 2 * b)
                if a is not None:
                    dve.wait_ge(xa_tok, a)
                    lns.normalise(dve, u, rows, z1)
                if b is not None:
                    dve.wait_ge(lnf.back, 2 * b)
                    lnf.normalise(dve, 2 * b)
                if a is not None:
                    dve.wait_ge(lns.hat_done, TILES * u + TILES)
                    lns.statistics(dve, u + 1, z1)
                    lns.normalise(dve, u + 1, z1, z2)
                    dve.wait_ge(lns.hat_done, TILES * u + 2 * TILES)
                    dve.wait_ge(z_turned, a)
                    dve.tensor_tensor(z1[:], z2[:], row_g[:].to_broadcast([P, TILES, P]), ALU.mult).then_inc(scaled, 1)
                    dve.wait_ge(scaled, a + 1)
                    dve.tensor_tensor(z3[:], z1[:], row_b[:].to_broadcast([P, TILES, P]), ALU.add).then_inc(xa_tok, 1)
                if b is not None:
                    dve.wait_ge(up_done, 8 * b)
                    dve.wait_ge(cr_done, b)
                    blend(xn_c, late_c, mixed_c, 3, late_c_out, blended_c, b)
                if a is not None:
                    dve.wait_ge(xa_tok, a + 1)
                    lns.statistics(dve, u + 2, z3)
                    dve.wait_ge(lns.back, a)
                    lns.normalise(dve, u + 2, z3)
                    dve.wait_ge(kvr, 12 * a)
                    blend(xn, late, mixed_in, 0, late_out, blended, a)
                    chunk(a, 0)
                if b is not None:
                    dve.wait_ge(sig_done, b + 1)
                    dve.wait_ge(xd_done, b)
                    dve.scalar_tensor_tensor(xc[:], sig[:], 0.5, xb_in[:], ALU.mult, ALU.add).then_inc(xc_done, 1)
                    dve.wait_ge(xc_done, b + 1)
                    dve.wait_ge(y_done, 2 * b + 1)
                    dve.scalar_tensor_tensor(xd[:], xc[:], 0.5, y_ps[:], ALU.add, ALU.add).then_inc(xd_done, 1)
                    lnf.statistics(dve, 2 * b + 1)
                if a is not None:
                    chunk(a, 1)
                if b is not None:
                    dve.wait_ge(lnf.back, 2 * b + 1)
                    lnf.normalise(dve, 2 * b + 1)
                if a is not None:
                    chunk(a, 2)
                    chunk(a, 3)
                if b is not None:
                    dve.wait_ge(y_done, 2 * b + 2)
                    dve.scalar_tensor_tensor(shared.xs[:, bass.ds(b * T, T)], y_ps[:], shared.down_bias[:], xd[:],
                                             ALU.add, ALU.add).then_inc(xs_out, 1)
                if a is not None:
                    dve.wait_ge(o_done, a + 1)
                    dve.wait_ge(lnf.turned, 2 * a)
                    dve.tensor_tensor(xb[:], xa[:], o_ps[:], ALU.add).then_inc(xb_done, 1)
                    dve.wait_ge(xb_done, a + 1)
                    dve.wait_ge(xc_done, a)
                    dve.tensor_tensor(xb_in[:], xb[:], x0T[:], ALU.add).then_inc(xb_in_done, 1)

            for at in (xn, xn_c, sk, skv):
                dve.memset(at[:, 0:1], 0.0).then_inc(prep, 1)
            dve.wait_ge(w_in, 16 * WLOADS)
            dve.tensor_scalar(rest[:], vec[:, 4:9], -1.0, 1.0, ALU.mult, ALU.add).then_inc(prep, 1)
            dve.wait_ge(prep, 5)
            dve.wait_ge(time_exp, 3)
            rounds(dve, both)

        @block.gpsimd
        def _(pool):
            def chunk(a, c):
                n = HCH * a + c
                pool.wait_ge(gated, n + 1)
                pool.wait_ge(numerated, n)
                pool.tensor_tensor(gate1[:], gate[:, c % 2, :], shared.ones[:].to_broadcast([P, T]), ALU.add).then_inc(gated1, 1)
                pool.wait_ge(gated1, n + 1)
                pool.wait_ge(firsts, 2 * n + 2)
                pool.wait_ge(out_done, n)
                pool.tensor_tensor(numer[:], wkv[:], gate1[:], ALU.mult).then_inc(numerated, 1)
                pool.wait_ge(numerated, n + 1)
                pool.wait_ge(rden_done, n + 1)
                pool.wait_ge(o_done, a)
                pool.tensor_tensor(out_c[:, c, :], numer[:], rden[:], ALU.mult).then_inc(out_done, 1)

            def both(a, b):
                if a is not None:
                    lns.reciprocal_deviation(pool, 3 * a)
                if b is not None:
                    lnf.reciprocal_deviation(pool, 2 * b)
                if a is not None:
                    lns.reciprocal_deviation(pool, 3 * a + 1)
                    lns.reciprocal_deviation(pool, 3 * a + 2)
                    chunk(a, 0)
                if b is not None:
                    lnf.reciprocal_deviation(pool, 2 * b + 1)
                if a is not None:
                    for c in range(1, HCH):
                        chunk(a, c)

            rounds(pool, both)


def constants(nc, shared, ins):
    with ExitStack() as ctx:
        mem = Memory(nc, ctx, "const")
        loaded, set_ = mem.sem("loaded"), mem.sem("set")
        block = ctx.enter_context(nc.Block())

        @block.sync
        def _(sp):
            sp.dma_start(shared.ident[:], ins["c_ident"]).then_inc(loaded, 16)

        @block.vector
        def _(dve):
            dve.wait_ge(loaded, 16)
            dve.tensor_copy(shared.identb[:], shared.ident[:]).then_inc(set_, 1)

        @block.gpsimd
        def _(pool):
            for dst, value in ((shared.minus_half, -0.5), (shared.ones, 1.0)):
                pool.memset(dst[:], value).then_inc(set_, 1)
            pool.wait_ge(set_, 3)


def store(nc, shared, out):
    with ExitStack() as ctx:
        mem = Memory(nc, ctx, "out")
        total = [mem.sb(f"total{k}", [P, T]) for k in range(2)]
        rows = [mem.sb(f"rows{k}", [P, TILES, D]) for k in range(2)]
        ps = [mem.bank(f"ps{k}") for k in range(2)]
        added, turned, copied = mem.sem("added"), mem.sem("turned"), mem.sem("copied")
        stored = [mem.sem(f"stored{k}") for k in range(2)]
        block = ctx.enter_context(nc.Block())

        @block.vector
        def _(dve):
            for b in range(B):
                if b >= 2:
                    dve.wait_ge(turned, b - 1)
                at = LEAD + 1 + b * SEQ
                dve.tensor_tensor(total[b % 2][:], shared.xs[:, b * T:(b + 1) * T], shared.x0[:, at:at + T],
                                  ALU.add).then_inc(added, 1)

        @block.tensor
        def _(pe):
            for b in range(B):
                pe.wait_ge(added, b + 1)
                if b >= 2:
                    pe.wait_ge(copied, b - 1)
                for t in range(TILES):
                    turn = pe.transpose(ps[b % 2][:, t * P:(t + 1) * P], total[b % 2][:, t * P:(t + 1) * P], shared.ident[:])
                turn.then_inc(turned, 1)

        @block.scalar
        def _(act):
            for b in range(B):
                act.wait_ge(turned, b + 1)
                if b >= 2:
                    act.wait_ge(stored[b % 2], 16 * (b // 2))
                act.copy(rows[b % 2][:].rearrange("p t d -> p (t d)"), ps[b % 2][:]).then_inc(copied, 1)

        @block.sync
        def _(sp):
            for b in range(B):
                sp.wait_ge(copied, b + 1)
                sp.dma_start(out[b].rearrange("(t p) d -> p t d", p=P), rows[b % 2][:]).then_inc(stored[b % 2], 16)
            for k in range(2):
                sp.wait_ge(stored[k], 16 * (B // 2))


def build(nc, ins, out):
    with ExitStack() as ctx:
        shared = Shared(Memory(nc, ctx, "all"))
        constants(nc, shared, ins)
        fold_butterflies(nc, shared, ins)
        fold_heads(nc, shared, ins)
        rwkv_ffn(nc, shared, ins)
        causal(nc, shared, ins)
        layers(nc, shared, ins)
        store(nc, shared, out)


def _constants():
    ident = np.eye(P, dtype=np.float32)
    p = np.arange(P)[:, None] % WIN
    c = np.arange(2 * WIN)[None, :]
    seen = (c <= p + WIN) & (c >= p)
    mask = np.where(seen, 0.0, MASKED)[:, None, :].repeat(TILES, 1)
    mask[:WIN, 0, :WIN] = MASKED
    diag = np.where(np.arange(P)[None, :] <= np.arange(P)[:, None], 0.0, MASKED)
    half = np.arange(0, DH, 2, dtype=np.float32)
    inv_freq = (1.0 / 10000.0 ** (half / DH)).astype(np.float32)
    t = np.arange(T, dtype=np.float32)
    freqs = np.tile(t[:, None] * inv_freq[None, :], (1, 2)).astype(np.float64)
    base = (half + np.float32(0.4 * DH)) / np.float32(1.4 * DH)
    power = (t - T // 2) / (WIN // 2)
    scale = np.tile(base[None, :].astype(np.float64) ** power[:, None], (1, 2))
    sign = np.where(np.arange(DH) < DH // 2, -1.0, 1.0)
    trig = np.stack([np.stack([np.cos(freqs) * scale, np.cos(freqs) / scale]),
                     np.stack([np.sin(freqs) * scale * sign, np.sin(freqs) / scale * sign])])
    trig = trig.reshape(2, 2, TILES, P, DH).transpose(3, 0, 1, 2, 4)
    return {"c_ident": ident, "c_mask": mask.astype(np.float32), "c_diag": diag.astype(np.float32),
            "c_trig": np.ascontiguousarray(trig, dtype=np.float32)}


def kernel(**inputs):
    import concourse.bacc as bacc
    from concourse.bass_utils import run_bass_kernel_spmd

    nc = bacc.Bacc("TRN2", target_bir_lowering=False, num_devices=1)
    arrays = {name: np.ascontiguousarray(a) for name, a in inputs.items()}
    arrays.update(_constants())
    ins = {name: nc.dram_tensor(name, a.shape, mybir.dt.from_np(a.dtype), kind="ExternalInput").ap()
           for name, a in arrays.items()}
    out = nc.dram_tensor("out", (B, T, D), F32, kind="ExternalOutput").ap()
    build(nc, ins, out)
    return run_bass_kernel_spmd(nc, [arrays], core_ids=[0]).results[0]["out"]
```

```python
from contextlib import ExitStack

import numpy as np

import concourse.bass as bass
from concourse import mybir
from concourse.alu_op_type import AluOpType as ALU

ACT = mybir.ActivationFunctionType
AX = mybir.AxisListType
F32 = mybir.dt.float32
BF16 = mybir.dt.bfloat16

P = 128
B, T, D = 8, 512, 128
TILES = T // P
NT = B * TILES
BANK = 512
HEADS, DH = 16, 64
PAIRS = HEADS // 2
INNER = HEADS * DH
WIN = 32
LAYERS = 6
GATED = 341
CHUNKS = [(0, 128), (128, 128), (256, GATED - 256)]
LN_EPS = 1e-5
NORM_FLOOR = 1e-24
QK_SCALE = 8.0
MASKED = -1e30
LEAD = WIN
SEQ = T + 1
XW = LEAD + B * SEQ


class Memory:

    def __init__(self, nc, ctx, prefix):
        self.nc, self.ctx, self.prefix, self.sems = nc, ctx, prefix, []
        ctx.callback(self.clear)

    def clear(self):
        for sem in self.sems:
            self.nc.gpsimd.sem_clear(sem)
            self.nc.release_semaphore(sem)

    def sb(self, name, shape, dt=F32):
        return self.ctx.enter_context(self.nc.sbuf_tensor(f"{self.prefix}_{name}", shape, dt))

    def bank(self, name):
        return self.ctx.enter_context(self.nc.psum_tensor(f"{self.prefix}_{name}", [P, BANK], F32))

    def sem(self, name):
        self.sems.append(self.nc.alloc_semaphore(f"{self.prefix}_{name}"))
        return self.sems[-1]


class LayerNorm:

    def __init__(self, mem, shared, tok, feat):
        self.tok, self.feat, self.shared = tok, feat, shared
        self.stats = mem.sb("ln_stats", [P, TILES, 6])
        self.both = mem.sb("ln_both", [P, TILES, 3])
        self.gap = mem.sb("ln_gap", [P, TILES])
        self.gap2, self.gap_eps = mem.sb("ln_gap2", [P, TILES]), mem.sb("ln_gap_eps", [P, TILES])
        self.mean = mem.sb("ln_mean", [P, TILES])
        self.vareps = mem.sb("ln_vareps", [P, TILES])
        self.rstd = mem.sb("ln_rstd", [P, TILES])
        self.hat = mem.sb("ln_hat", [P, TILES, P])
        self.turned = mem.sem("ln_turned")
        self.stats_done = mem.sem("ln_stats_done")
        self.steps = mem.sem("ln_steps")
        self.rstd_done = mem.sem("ln_rstd_done")
        self.hat_done = mem.sem("ln_hat_done")
        self.back = mem.sem("ln_back")

    def turn_in(self, pe, m, src):
        pe.wait_ge(self.hat_done, TILES * m)
        for t in range(TILES):
            turn = pe.transpose(self.tok[:, t * P:(t + 1) * P], src[:, t * P:(t + 1) * P], self.shared.ident[:])
        turn.then_inc(self.turned, 1)

    def statistics(self, dve, m, tok=None):
        if tok is None:
            dve.wait_ge(self.turned, m + 1)
            tok = self.tok[:].rearrange("p (t f) -> p t f", t=TILES)
        dve.wait_ge(self.steps, 6 * m)
        for t in range(TILES):
            dve.bn_stats(self.stats[:, t, :], tok[:, t, :]).then_inc(self.stats_done, 1)
        dve.wait_ge(self.stats_done, TILES * m + TILES)
        even, odd = self.stats[:, :, 0:3], self.stats[:, :, 3:6]
        dve.tensor_tensor(self.gap[:], even[:, :, 1], odd[:, :, 1], ALU.subtract).then_inc(self.steps, 1)
        dve.tensor_tensor(self.both[:], even, odd, ALU.add).then_inc(self.steps, 1)
        dve.wait_ge(self.steps, 6 * m + 1)
        dve.tensor_tensor(self.gap2[:], self.gap[:], self.gap[:], ALU.mult).then_inc(self.steps, 1)
        dve.wait_ge(self.steps, 6 * m + 2)
        dve.wait_ge(self.hat_done, TILES * m)
        dve.tensor_scalar(self.mean[:], self.both[:, :, 1], 0.5, None, ALU.mult).then_inc(self.steps, 1)
        dve.wait_ge(self.steps, 6 * m + 3)
        dve.tensor_scalar(self.gap_eps[:], self.gap2[:], 0.25, LN_EPS, ALU.mult, ALU.add).then_inc(self.steps, 1)
        dve.wait_ge(self.steps, 6 * m + 5)
        dve.wait_ge(self.rstd_done, m)
        dve.scalar_tensor_tensor(self.vareps[:], self.both[:, :, 2], 1.0 / P, self.gap_eps[:],
                                 ALU.mult, ALU.add).then_inc(self.steps, 1)

    def reciprocal_deviation(self, pool, m):
        pool.wait_ge(self.steps, 6 * m + 6)
        pool.wait_ge(self.hat_done, TILES * m)
        pool.tensor_tensor(self.rstd[:], self.vareps[:], self.shared.minus_half[:, 0:TILES],
                           ALU.pow).then_inc(self.rstd_done, 1)

    def normalise(self, dve, m, tok=None, out=None):
        if tok is None:
            tok = self.tok[:].rearrange("p (t f) -> p t f", t=TILES)
        if out is None:
            out = self.hat
        dve.wait_ge(self.rstd_done, m + 1)
        for t in range(TILES):
            dve.tensor_scalar(out[:, t, :], tok[:, t, :], self.mean[:, t:t + 1], self.rstd[:, t:t + 1],
                              ALU.subtract, ALU.mult).then_inc(self.hat_done, 1)

    def turn_back(self, pe, m):
        pe.wait_ge(self.hat_done, TILES * m + TILES)
        for t in range(TILES):
            turn = pe.transpose(self.feat[:, t * P:(t + 1) * P], self.hat[:, t, :], self.shared.ident[:])
        turn.then_inc(self.back, 1)


class Shared:

    def __init__(self, mem):
        self.ident = mem.sb("ident", [P, P])
        self.identb = mem.sb("identb", [P, P], BF16)
        self.minus_half = mem.sb("minus_half", [P, 2 * HEADS])
        self.ones = mem.sb("ones", [P, 1])
        self.w_score = mem.sb("w_score", [P, HEADS, P])
        self.w_value = mem.sb("w_value", [P, HEADS, P])
        self.w_up = mem.sb("w_up", [P, 4 * D])
        self.w_down = mem.sb("w_down", [P, 4, D])
        self.up_bias = mem.sb("up_bias", [P, 4])
        self.down_bias = mem.sb("down_bias", [P, 1])
        self.x0 = mem.sb("x0", [P, XW])
        self.xs = mem.sb("xs", [P, B * T])


def column(tile):
    return tile * P + tile // TILES + (LEAD + 1)


def layers(nc, shared, ins):
    with ExitStack() as ctx:
        mem = Memory(nc, ctx, "lay")
        x0 = shared.x0
        x1 = mem.sb("x1", [P, XW])
        w_qk = mem.sb("w_qk", [P, 2 * INNER])
        w_v = mem.sb("w_v", [P, 2, PAIRS * DH])
        w_o = mem.sb("w_o", [P, PAIRS, P])
        w_1 = mem.sb("w_1", [P, 2 * GATED])
        w_2 = mem.sb("w_2", [P, len(CHUNKS), P])
        vecs = mem.sb("vecs", [P, 9])
        trig = mem.sb("trig", [P, 2, 2, TILES, DH])
        gains = mem.sb("gains", [P, 2, 2, DH])
        cos = mem.sb("cos", [P, 2, TILES, DH])
        sin = mem.sb("sin", [P, 2, TILES, DH])
        mask = mem.sb("mask", [P, TILES, 2 * WIN])
        mask8 = mem.sb("mask8", [P, TILES, PAIRS * 2 * WIN], BF16)
        xt = mem.sb("xt", [P, P])
        xv = mem.sb("xv", [P, P])
        sq = mem.sb("sq", [P, 2, INNER])
        n2 = mem.sb("n2", [P, 2 * HEADS])
        n2c = mem.sb("n2c", [P, 2 * HEADS])
        rn = mem.sb("rn", [P, 2 * HEADS])
        qkn = mem.sb("qkn", [P, 2, INNER])
        qkr = mem.sb("qkr", [P, 2, INNER])
        qks = mem.sb("qks", [P, 2, INNER])
        qT = mem.sb("qT", [P, PAIRS, P])
        kT = mem.sb("kT", [P, PAIRS, WIN + P])
        probs = mem.sb("probs", [P, PAIRS, 2, 2 * WIN])
        top = mem.sb("top", [P, 2, PAIRS])
        total = mem.sb("total", [P, 2, PAIRS])
        rtotal = mem.sb("rtotal", [P, 2, PAIRS])
        pT = mem.sb("pT", [P, PAIRS, P])
        val = mem.sb("val", [P, TILES + 1, PAIRS * DH])
        att = mem.sb("att", [P, PAIRS, 2, DH])
        aT = mem.sb("aT", [P, PAIRS, P])
        xf = mem.sb("xf", [P, T])
        xn = mem.sb("xn", [P, T])
        gate = mem.sb("gate", [P, len(CHUNKS), T])
        act = mem.sb("act", [P, len(CHUNKS), T])
        qk_ps = [mem.bank(f"qk{j}") for j in range(4)]
        ring = [mem.bank(f"ring{j}") for j in range(4)]
        ln = LayerNorm(mem, shared, ring[0], ring[1])

        s = mem.sem
        const_in = s("const_in")
        qk_in, v_in, o_in, ffn_in, gains_in = s("qk_in"), s("v_in"), s("o_in"), s("ffn_in"), s("gains_in")
        mask_done = s("mask_done")
        kT_clear = s("kT_clear")
        pads_done = s("pads_done")
        tables = s("tables")
        xt_ready, xv_ready = s("xt_ready"), s("xv_ready")
        qk_proj = s("qk_proj")
        squared = s("squared")
        norms = s("norms")
        floored, rnorm = s("floored"), s("rnorm")
        normed = s("normed")
        cosed = s("cosed")
        sined_q, sined_k = s("sined_q"), s("sined_k")
        rotated = s("rotated")
        qk_turned = s("qk_turned")
        qT_out, kT_out = s("qT_out"), s("kT_out")
        k_kept = s("k_kept")
        scores = s("scores")
        topped, shifted, summed, inverted = s("topped"), s("shifted"), s("summed"), s("inverted")
        exped = s("exped")
        v_proj, v_out, v_kept = s("v_proj"), s("v_out"), s("v_kept")
        p_turned, p_out0, p_out1 = s("p_turned"), s("p_out0"), s("p_out1")
        mixed, att_out = s("mixed"), s("att_out")
        a_turned, aT_out = s("a_turned"), s("aT_out")
        projected, x1_out = s("projected"), s("x1_out")
        xf_ready, xn_ready = s("xf_ready"), s("xn_ready")
        gates, vals = s("gates"), s("vals")
        gelued, gated = s("gelued"), s("gated")
        ffn_out = s("ffn_out")
        x0_out = s("x0_out")

        def half_table(w, i, half):
            place = slice(i % TILES, i % TILES + 1) if isinstance(i, int) else bass.ds(i % TILES, 1)
            return sin[:, w, place, 32 * half:32 * half + 32]

        K_FIRST = (2, 3, 0, 1)
        tokens = lambda a, h: a[64 * h:64 * h + 64]
        heads = lambda a: a.rearrange("p (h d) -> p h d", d=DH)
        block = ctx.enter_context(nc.Block())

        @block.sync
        def _(sp):
            sp.dma_start(trig[:], ins["c_trig"]).then_inc(const_in, 16)
            sp.dma_start(mask[:], ins["c_mask"]).then_inc(const_in, 16)
            w_qkv, w_out, w1, w2 = ins["L1_ffn_Wqkv"], ins["L1_ffn_Wo"], ins["L1_ffn_W1"], ins["L1_ffn_W2"]
            with sp.Fori(0, LAYERS) as l:
                one = bass.ds(l, 1)
                sp.wait_ge(tables, 4 * l)
                for side in range(2):
                    for which, name in enumerate(("L1_ffn_q_scale", "L1_ffn_k_scale")):
                        for half in range(2):
                            src = ins[name][one, bass.ds(32 * (half ^ side), 32)]
                            sp.dma_start(gains[:, side, which, 32 * half:32 * half + 32],
                                         src.to_broadcast([P, 32])).then_inc(gains_in, 16)
                sp.wait_ge(qk_proj, 4 * NT * l)
                sp.dma_start(w_qk[:], w_qkv[one, :, 0:2 * INNER].rearrange("o d n -> (o d) n")).then_inc(qk_in, 16)
                sp.wait_ge(v_proj, 2 * NT * l)
                for h in range(2):
                    src = w_qkv[one, :, 2 * INNER:3 * INNER].rearrange("o d (q h v) -> (o d) h q v", h=2, v=DH)
                    sp.dma_start(w_v[:, h, :].rearrange("p (q v) -> p q v", v=DH), src[:, h, :, :]).then_inc(v_in, 16)
                sp.wait_ge(projected, NT * l)
                sp.dma_start(w_o[:], w_out[one].rearrange("o (q p) n -> (o p) q n", p=P)).then_inc(o_in, 16)
                sp.wait_ge(x0_out, B * l + B)
                sp.dma_start(w_1[:], w1[one].rearrange("o d n -> (o d) n")).then_inc(ffn_in, 16)
                for c, (r0, rows) in enumerate(CHUNKS):
                    sp.dma_start(w_2[0:rows, c, :], w2[one, r0:r0 + rows, :].rearrange("o r n -> (o r) n")).then_inc(ffn_in, 16)
                    for side in range(2):
                        src = ins["L1_ffn_b1"][one, side * GATED + r0:side * GATED + r0 + rows]
                        sp.dma_start(vecs[0:rows, 3 * side + c:3 * side + c + 1], src.rearrange("o r -> r o")).then_inc(ffn_in, 16)
                for c, name in enumerate(("L1_ffn_b2", "L1_ffn_ln_g", "L1_ffn_ln_b")):
                    sp.dma_start(vecs[:, 6 + c:7 + c], ins[name][one, :].rearrange("o r -> r o")).then_inc(ffn_in, 16)

        FFN_LOADS = 1 + 3 * len(CHUNKS) + 3

        @block.tensor
        def _(pe):
            def project_qk(n, places):
                pe.wait_ge(xt_ready, 2 * n + 2)
                pe.wait_ge(normed, 4 * n)
                for j in (K_FIRST[place] for place in places):
                    pe.matmul(qk_ps[j][:], xt[:], w_qk[:, j * BANK:(j + 1) * BANK], start=True, stop=True).then_inc(qk_proj, 1)

            def turn(n, w, j):
                for q in range(4 * j, 4 * j + 4):
                    turn = pe.transpose(ring[2 * w + j][:, q % 4 * P:q % 4 * P + P],
                                        qkr[:, w, q * P:(q + 1) * P], shared.ident[:])
                turn.then_inc(qk_turned, 1)

            def turn_k(n, j, att_halves):
                pe.wait_ge(rotated, 2 * n + 1)
                pe.wait_ge(att_out, att_halves)
                turn(n, 1, j)

            def project_v(n, h):
                pe.wait_ge(xv_ready, 2 * n + 2)
                pe.wait_ge(kT_out, 2 * n + h + 1)
                pe.matmul(ring[2 + h][:], xv[:], w_v[:, h, :], start=True, stop=True).then_inc(v_proj, 1)

            def turn_q_project_v(n):
                pe.wait_ge(rotated, 2 * n + 2)
                pe.wait_ge(aT_out, 2 * n)
                turn(n, 0, 1)
                project_v(n, 0)
                pe.wait_ge(x1_out, n)
                turn(n, 0, 0)
                project_v(n, 1)

            def score(n, i):
                pe.wait_ge(qT_out, 2 * n + 2)
                pe.wait_ge(kT_out, 2 * n + 2)
                pe.wait_ge(k_kept, n + 1)
                for h in range(2):
                    pe.matmul(ring[h][:], shared.identb[:], mask8[:, bass.ds(i % TILES, 1), :] if not isinstance(i, int)
                              else mask8[:, i % TILES, :], start=True, stop=False, skip_group_check=True)
                    for q in range(PAIRS):
                        for g in range(TILES):
                            mm = pe.matmul(ring[h][WIN * g:WIN * g + WIN, q * 64:q * 64 + 64],
                                           tokens(qT, h)[:, q, WIN * g:WIN * g + WIN],
                                           tokens(kT, h)[:, q, WIN * g:WIN * g + 2 * WIN],
                                           start=False, stop=True, skip_group_check=True)
                    mm.then_inc(scores, 1)

            def turn_probs(n):
                pe.wait_ge(exped, 2 * n + 2)
                for q in range(PAIRS):
                    turn = pe.transpose(ring[q // 4][:, q % 4 * P:q % 4 * P + P],
                                        probs[:, q, :, :].rearrange("p h k -> p (h k)"), shared.ident[:])
                    if q % 4 == 3:
                        turn.then_inc(p_turned, 1)

            def mix(n):
                pe.wait_ge(v_out, 12 * n + 12)
                pe.wait_ge(p_out0, n + 1)
                pe.wait_ge(p_out1, n + 1)
                pe.matmul(ring[2][:, 0:1], shared.identb[:], mask8[:, 0, 0:1], start=True, stop=True, skip_group_check=True)
                for h in range(2):
                    for q in range(PAIRS):
                        for g in range(TILES):
                            mm = pe.matmul(ring[2 + h][WIN * g:WIN * g + WIN, q * DH:q * DH + DH],
                                           tokens(pT, h)[:, q, WIN * g:WIN * g + WIN],
                                           tokens(val, h)[:, g, q * DH:q * DH + DH],
                                           start=True, stop=True, skip_group_check=True)
                    mm.then_inc(mixed, 1)

            def turn_att(n):
                pe.wait_ge(att_out, 2 * n + 2)
                for q in range(PAIRS):
                    turn = pe.transpose(ring[q // 4][:, q % 4 * P:q % 4 * P + P],
                                        att[:, q, :, :].rearrange("p h v -> p (h v)"), shared.ident[:])
                    if q % 4 == 3:
                        turn.then_inc(a_turned, 1)

            def project_out(n):
                pe.wait_ge(aT_out, 2 * n + 2)
                for q in range(PAIRS):
                    mm = pe.matmul(ring[0][:, 0:P], w_o[:, q, :], aT[:, q, :], start=(q == 0), stop=(q == PAIRS - 1))
                mm.then_inc(projected, 1)

            def rest(n, i, ahead):
                score(n, i)
                if ahead == 2:
                    project_qk(n + 2, (0, 1, 2))
                turn_probs(n)
                if ahead == 2:
                    project_qk(n + 2, (3,))
                mix(n)
                if ahead:
                    turn_k(n + 1, 0, 2 * n + 1)
                turn_att(n)
                if ahead:
                    turn_k(n + 1, 1, 2 * n + 2)
                project_out(n)
                if ahead:
                    turn_q_project_v(n + 1)

            def ffn_up(m):
                pe.wait_ge(xn_ready, m + 1)
                for c, (r0, rows) in enumerate(CHUNKS):
                    g_ps, v_ps = qk_ps[c % 2], qk_ps[2 + c % 2]
                    if c == 2:
                        pe.wait_ge(gelued, 3 * m + 1)
                        pe.wait_ge(gated, 3 * m + 1)
                    elif c == 0:
                        pe.wait_ge(gated, 3 * m)
                    pe.matmul(g_ps[0:rows, :], w_1[:, GATED + r0:GATED + r0 + rows], xn[:], start=True, stop=True).then_inc(gates, 1)
                    pe.matmul(v_ps[0:rows, :], w_1[:, r0:r0 + rows], xn[:], start=True, stop=True).then_inc(vals, 1)

            def ffn_down(m):
                pe.wait_ge(x0_out, m + B)
                for c, (r0, rows) in enumerate(CHUNKS):
                    pe.wait_ge(gated, 3 * m + c + 1)
                    mm = pe.matmul(ring[2][:], w_2[0:rows, c, :], act[0:rows, c, :], start=(c == 0), stop=(c == 2))
                mm.then_inc(ffn_out, 1)

            with pe.Fori(0, B) as b:
                pe.wait_ge(xf_ready, 2 * b + 2)
                ln.turn_in(pe, b, xf)
                pe.wait_ge(x0_out, b)
                ln.turn_back(pe, b)
            pe.wait_ge(mask_done, TILES)
            pe.wait_ge(x0_out, B)
            with pe.Fori(0, LAYERS) as l:
                pe.wait_ge(qk_in, 16 * l + 16)
                pe.wait_ge(v_in, 32 * l + 32)
                pe.wait_ge(o_in, 16 * l + 16)
                pe.wait_ge(gated, 3 * B * l)
                tile0 = l * NT
                project_qk(tile0, range(4))
                pe.wait_ge(x0_out, B * l + B)
                project_qk(tile0 + 1, range(4))
                for j in range(2):
                    turn_k(tile0, j, 2 * tile0)
                turn_q_project_v(tile0)
                with pe.Fori(0, NT - 2) as i:
                    rest(tile0 + i, i, 2)
                rest(tile0 + NT - 2, NT - 2, 1)
                rest(tile0 + NT - 1, NT - 1, 0)
                pe.wait_ge(ffn_in, 16 * FFN_LOADS * l + 16 * FFN_LOADS)
                pe.wait_ge(x1_out, NT * l + NT)
                first = B * l
                pe.wait_ge(xf_ready, 2 * (first + B) + 2)
                ln.turn_in(pe, first + B, xf)
                ln.turn_back(pe, first + B)
                with pe.Fori(0, B - 1) as b:
                    m = first + b
                    pe.wait_ge(xf_ready, 2 * (m + B) + 4)
                    ln.turn_in(pe, m + B + 1, xf)
                    ffn_up(m)
                    ln.turn_back(pe, m + B + 1)
                    ffn_down(m)
                ffn_up(first + B - 1)
                ffn_down(first + B - 1)

        @block.scalar
        def _(eng):
            def shifted_copy(dst, width, src, col, done):
                eng.copy(dst[0:64, 0:width], src[0:64, bass.ds(col, width)]).then_inc(done, 1)
                eng.copy(dst[64:128, 0:width], src[64:128, bass.ds(col - 1, width)]).then_inc(done, 1)

            def take_qk(n, i):
                eng.wait_ge(qk_proj, 4 * n)
                shifted_copy(xt, P, x0, column(i), xt_ready)

            def square(n):
                for place, j in enumerate(K_FIRST):
                    eng.wait_ge(qk_proj, 4 * n + place + 1)
                    if place == 0:
                        eng.wait_ge(norms, 2 * n)
                    eng.activation(sq[:, j // 2, j % 2 * BANK:(j % 2 + 1) * BANK], qk_ps[j][:], ACT.Square).then_inc(squared, 1)

            def take_v(n, i):
                eng.wait_ge(v_proj, 2 * n)
                shifted_copy(xv, P, x0, column(i), xv_ready)

            def rest(n, i, ahead):
                eng.wait_ge(scores, 2 * n)
                for j in (1, 0):
                    eng.wait_ge(qk_turned, 4 * n + 4 - j)
                    eng.copy(qT[:, 4 * j:4 * j + 4, :].rearrange("p q t -> p (q t)"), ring[j][:]).then_inc(qT_out, 1)

                def exp(h):
                    eng.wait_ge(shifted, 2 * n + h + 1)
                    eng.activation(probs[:, :, h, :], probs[:, :, h, :], ACT.Exp, scale=QK_SCALE).then_inc(exped, 1)

                def value(h, g, to, rows, source):
                    to += 64 * h
                    eng.copy(val[to:to + rows, g, :], ring[2 + h][source:source + rows, :]).then_inc(v_out, 1)

                if ahead == 2:
                    take_qk(n + 2, i + 2)
                eng.wait_ge(mixed, 2 * n)
                eng.wait_ge(v_proj, 2 * n + 1)
                value(0, 1, 0, 64, 0)
                value(0, 3, 0, 64, 64)
                value(0, 2, 0, 32, 32)
                value(0, 2, 32, 32, 64)
                eng.wait_ge(v_kept, n)
                value(0, 0, 32, 32, 0)
                value(0, TILES, 0, 32, 96)
                eng.wait_ge(v_proj, 2 * n + 2)
                value(1, 1, 0, 64, 0)
                value(1, 3, 0, 64, 64)
                exp(0)
                value(1, 2, 0, 32, 32)
                exp(1)
                value(1, 2, 32, 32, 64)
                value(1, 0, 32, 32, 0)
                value(1, TILES, 0, 32, 96)
                eng.wait_ge(p_turned, 2 * n + 2)
                eng.copy(pT[:, 4:8, :].rearrange("p q t -> p (q t)"), ring[1][:]).then_inc(p_out1, 1)
                if ahead:
                    take_v(n + 1, i + 1)
                if ahead == 2:
                    square(n + 2)
                eng.wait_ge(projected, n)
                for j in range(2):
                    eng.wait_ge(a_turned, 2 * n + j + 1)
                    eng.copy(aT[:, 4 * j:4 * j + 4, :].rearrange("p q t -> p (q t)"), ring[j][:]).then_inc(aT_out, 1)

            def affine(m):
                eng.wait_ge(ln.back, m + B + 1)
                eng.wait_ge(vals, 3 * m)
                eng.activation(xn[:], ring[1][:], ACT.Identity, bias=vecs[:, 8:9], scale=vecs[:, 7:8]).then_inc(xn_ready, 1)

            def gelu(m):
                for c, (r0, rows) in enumerate(CHUNKS):
                    eng.wait_ge(gates, 3 * m + c + 1)
                    eng.wait_ge(gated, 3 * m)
                    eng.activation(gate[0:rows, c, :], qk_ps[c % 2][0:rows, :], ACT.Gelu,
                                   bias=vecs[0:rows, 3 + c:4 + c]).then_inc(gelued, 1)

            eng.wait_ge(pads_done, 5)
            with eng.Fori(0, B) as b:
                eng.wait_ge(ln.turned, b)
                eng.copy(xf[0:64, :], shared.xs[0:64, bass.ds(b * T, T)]).then_inc(xf_ready, 1)
                eng.copy(xf[64:128, :], shared.xs[64:128, bass.ds(b * T, T)]).then_inc(xf_ready, 1)
                eng.wait_ge(ln.back, b + 1)
                eng.copy(x0[:, bass.ds(b * SEQ + LEAD + 1, T)], ring[1][:]).then_inc(x0_out, 1)
            eng.wait_ge(x0_out, B)
            with eng.Fori(0, LAYERS) as l:
                eng.wait_ge(x0_out, B * l + 1)
                first = l * NT
                take_qk(first, 0)
                take_v(first, 0)
                square(first)
                take_qk(first + 1, 1)
                square(first + 1)
                eng.wait_ge(x0_out, B * l + B)
                with eng.Fori(0, NT - 2) as i:
                    rest(first + i, i, 2)
                rest(first + NT - 2, NT - 2, 1)
                rest(first + NT - 1, NT - 1, 0)
                eng.wait_ge(x1_out, first + NT)
                eng.wait_ge(ffn_in, 16 * FFN_LOADS * l + 16 * FFN_LOADS)
                m0 = B * l
                affine(m0)
                gelu(m0)
                affine(m0 + 1)
                with eng.Fori(1, B - 1) as b:
                    gelu(m0 + b)
                    affine(m0 + b + 1)
                gelu(m0 + B - 1)

        @block.vector
        def _(dve):
            def squared_norms(n, w):
                place = 1 - w
                dve.wait_ge(squared, 4 * n + 2 * place + 2)
                dve.wait_ge(floored, 2 * n)
                part = slice(HEADS * w, HEADS * w + HEADS)
                dve.tensor_reduce(n2[:, part], heads(sq[:, w, :]), AX.X, ALU.add).then_inc(norms, 1)
                dve.wait_ge(norms, 2 * n + place + 1)
                dve.wait_ge(rnorm, 2 * n)
                dve.tensor_scalar(n2c[:, part], n2[:, part], NORM_FLOOR, None, ALU.max).then_inc(floored, 1)

            def scale_to_one(n):
                dve.wait_ge(cosed, 2 * n)
                dve.wait_ge(sined_q, 2 * n)
                dve.wait_ge(sined_k, 2 * n)
                for place, j in enumerate(K_FIRST):
                    dve.wait_ge(rnorm, 2 * n + place // 2 + 1)
                    dve.tensor_tensor(heads(qkn[:, j // 2, j % 2 * BANK:(j % 2 + 1) * BANK]), heads(qk_ps[j][:]),
                                      rn[:, 8 * j:8 * j + 8].unsqueeze(2).to_broadcast([P, 8, DH]),
                                      ALU.mult).then_inc(normed, 1)

            def table(a, w, i):
                row = a[:, w, bass.ds(i % TILES, 1), :] if not isinstance(i, int) else a[:, w, i % TILES:i % TILES + 1, :]
                return row.to_broadcast([P, HEADS, DH])

            def cosine(n, i):
                dve.wait_ge(qk_turned, 4 * n)
                for k, w in enumerate((1, 0)):
                    dve.wait_ge(normed, 4 * n + 2 * k + 2)
                    dve.tensor_tensor(heads(qkr[:, w, :]), heads(qkn[:, w, :]), table(cos, w, i), ALU.mult).then_inc(cosed, 1)

            def sine_q(n, i):
                dve.wait_ge(rotated, 2 * n)
                for half in range(2):
                    dve.tensor_tensor(heads(qks[:, 0, :])[:, :, 32 * half:32 * half + 32],
                                      heads(qkn[:, 0, :])[:, :, 32 - 32 * half:64 - 32 * half],
                                      half_table(0, i, half).to_broadcast([P, HEADS, 32]), ALU.mult).then_inc(sined_q, 1)

            def keys(n):
                dve.wait_ge(scores, 2 * n)
                dve.wait_ge(kT_out, 2 * n)
                dve.tensor_copy(kT[:, :, 0:WIN], kT[:, :, P:P + WIN]).then_inc(k_kept, 1)
                dve.wait_ge(k_kept, n + 1)
                for j in range(2):
                    dve.wait_ge(qk_turned, 4 * n + j + 1)
                    dve.tensor_copy(kT[:, 4 * j:4 * j + 4, WIN:WIN + P],
                                    ring[2 + j][:].rearrange("p (q t) -> p q t", t=P)).then_inc(kT_out, 1)

            def rest(n, i, ahead):
                if ahead:
                    scale_to_one(n + 1)
                dve.wait_ge(shifted, 2 * n)
                dve.wait_ge(p_turned, 2 * n)
                dve.wait_ge(summed, 2 * n)
                for h in range(2):
                    dve.wait_ge(scores, 2 * n + h + 1)
                    dve.tensor_reduce(top[:, h, :], heads(ring[h][:]), AX.X, ALU.max).then_inc(topped, 1)
                    dve.wait_ge(topped, 2 * n + h + 1)
                    dve.tensor_tensor(probs[:, :, h, :], heads(ring[h][:]),
                                      top[:, h, :].unsqueeze(2).to_broadcast([P, PAIRS, 2 * WIN]),
                                      ALU.subtract).then_inc(shifted, 1)
                if ahead:
                    cosine(n + 1, i + 1)
                dve.wait_ge(p_turned, 2 * n + 1)
                dve.wait_ge(mixed, 2 * n)
                dve.tensor_copy(pT[:, 0:4, :].rearrange("p q t -> p (q t)"), ring[0][:]).then_inc(p_out0, 1)
                if ahead:
                    sine_q(n + 1, i + 1)
                dve.wait_ge(inverted, n)
                for h in range(2):
                    dve.wait_ge(exped, 2 * n + h + 1)
                    dve.tensor_reduce(total[:, h, :], probs[:, :, h, :], AX.X, ALU.add).then_inc(summed, 1)
                dve.wait_ge(summed, 2 * n + 2)
                dve.wait_ge(att_out, 2 * n)
                dve.reciprocal(rtotal[:].rearrange("p h q -> p (h q)"), total[:].rearrange("p h q -> p (h q)")).then_inc(inverted, 1)
                dve.wait_ge(inverted, n + 1)
                dve.wait_ge(a_turned, 2 * n)
                for h in range(2):
                    dve.wait_ge(mixed, 2 * n + h + 1)
                    dve.tensor_tensor(att[:, :, h, :], heads(ring[2 + h][:]),
                                      rtotal[:, h, :].unsqueeze(2).to_broadcast([P, PAIRS, DH]),
                                      ALU.mult).then_inc(att_out, 1)
                if ahead == 2:
                    squared_norms(n + 2, 1)
                    squared_norms(n + 2, 0)
                if ahead:
                    keys(n + 1)
                dve.wait_ge(projected, n + 1)
                at = column(i)
                dve.tensor_tensor(x1[:, bass.ds(at, P)], ring[0][:, 0:P], x0[:, bass.ds(at, P)], ALU.add).then_inc(x1_out, 1)

            def take_ffn(m, b):
                col = b * SEQ + (LEAD + 1)
                dve.wait_ge(ln.turned, m + B)
                dve.tensor_copy(xf[0:64, :], x1[0:64, bass.ds(col, T)]).then_inc(xf_ready, 1)
                dve.tensor_copy(xf[64:128, :], x1[64:128, bass.ds(col - 1, T)]).then_inc(xf_ready, 1)

            def gated_product(m, chunks):
                dve.wait_ge(ffn_out, m)
                for c in chunks:
                    rows = CHUNKS[c][1]
                    dve.wait_ge(vals, 3 * m + c + 1)
                    dve.wait_ge(gelued, 3 * m + c + 1)
                    dve.scalar_tensor_tensor(act[0:rows, c, :], qk_ps[2 + c % 2][0:rows, :], vecs[0:rows, c:c + 1],
                                             gate[0:rows, c, :], ALU.add, ALU.mult).then_inc(gated, 1)

            def ffn_add(m, col):
                dve.wait_ge(ffn_out, m + 1)
                dve.scalar_tensor_tensor(x0[:, bass.ds(col, T)], ring[2][:], vecs[:, 6:7], x1[:, bass.ds(col, T)],
                                         ALU.add, ALU.add).then_inc(x0_out, 1)

            for a in (x0, x1):
                dve.memset(a[:, 0:LEAD], 0.0).then_inc(pads_done, 1)
                dve.memset(a[:, LEAD:].rearrange("p (b t) -> p b t", t=SEQ)[:, :, 0:1], 0.0).then_inc(pads_done, 1)
            dve.memset(val[:], 0.0).then_inc(pads_done, 1)
            dve.memset(kT[:], 0.0).then_inc(kT_clear, 1)
            dve.wait_ge(kT_clear, 1)
            with dve.Fori(0, B) as b:
                ln.statistics(dve, b)
                dve.wait_ge(ln.back, b)
                ln.normalise(dve, b)
            dve.wait_ge(const_in, 32)
            with dve.Fori(0, LAYERS) as l:
                first = l * NT
                dve.wait_ge(gains_in, 16 * 8 * l + 16 * 8)
                dve.wait_ge(rotated, 2 * first)
                dve.wait_ge(cosed, 2 * first)
                dve.wait_ge(sined_q, 2 * first)
                for side, tab in enumerate((cos, sin)):
                    for w in range(2):
                        dve.tensor_tensor(tab[:, w, :, :], trig[:, side, w, :, :],
                                          gains[:, side, w, :].unsqueeze(1).to_broadcast([P, TILES, DH]),
                                          ALU.mult).then_inc(tables, 1)
                dve.wait_ge(tables, 4 * l + 4)
                for w in (1, 0):
                    squared_norms(first, w)
                scale_to_one(first)
                cosine(first, 0)
                sine_q(first, 0)
                keys(first)
                for w in (1, 0):
                    squared_norms(first + 1, w)
                with dve.Fori(0, NT - 2) as i:
                    rest(first + i, i, 2)
                rest(first + NT - 2, NT - 2, 1)
                rest(first + NT - 1, NT - 1, 0)
                dve.wait_ge(ffn_in, 16 * FFN_LOADS * l + 16 * FFN_LOADS)
                m0 = B * l
                dve.wait_ge(x1_out, first + NT)
                take_ffn(m0, 0)
                ln.statistics(dve, m0 + B)
                take_ffn(m0 + 1, 1)
                dve.wait_ge(ln.back, m0 + B)
                ln.normalise(dve, m0 + B)

                def ffn(m, b, more):
                    ln.statistics(dve, m + B + 1)
                    gated_product(m, (0,))
                    if more:
                        take_ffn(m + 2, b + 2)
                    dve.wait_ge(ln.back, m + B + 1)
                    ln.normalise(dve, m + B + 1)
                    gated_product(m, (1, 2))
                    ffn_add(m, b * SEQ + (LEAD + 1))

                with dve.Fori(0, B - 2) as b:
                    ffn(m0 + b, b, True)
                ffn(m0 + B - 2, B - 2, False)
                gated_product(m0 + B - 1, range(len(CHUNKS)))
                ffn_add(m0 + B - 1, (B - 1) * SEQ + (LEAD + 1))

        @block.gpsimd
        def _(pool):
            def reciprocal_norms(n, w):
                part = slice(HEADS * w, HEADS * w + HEADS)
                pool.wait_ge(floored, 2 * n + 2 - w)
                pool.wait_ge(normed, 4 * n)
                pool.tensor_tensor(rn[:, part], n2c[:, part], shared.minus_half[:, part], ALU.pow).then_inc(rnorm, 1)

            def rotate(n, i):
                pool.wait_ge(rotated, 2 * n)
                pool.wait_ge(normed, 4 * n + 2)
                for half in range(2):
                    pool.tensor_tensor(heads(qks[:, 1, :])[:, :, 32 * half:32 * half + 32],
                                       heads(qkn[:, 1, :])[:, :, 32 - 32 * half:64 - 32 * half],
                                       half_table(1, i, half).to_broadcast([P, HEADS, 32]), ALU.mult).then_inc(sined_k, 1)
                pool.wait_ge(cosed, 2 * n + 1)
                pool.wait_ge(sined_k, 2 * n + 2)
                pool.tensor_tensor(qkr[:, 1, :], qkr[:, 1, :], qks[:, 1, :], ALU.add).then_inc(rotated, 1)
                pool.wait_ge(cosed, 2 * n + 2)
                pool.wait_ge(sined_q, 2 * n + 2)
                pool.tensor_tensor(qkr[:, 0, :], qkr[:, 0, :], qks[:, 0, :], ALU.add).then_inc(rotated, 1)

            def keep_values(n):
                pool.wait_ge(mixed, 2 * n + 2)
                pool.wait_ge(v_out, 12 * n + 12)
                pool.tensor_tensor(val[:, 0, :], val[:, TILES, :], shared.ones[:].to_broadcast([P, PAIRS * DH]),
                                   ALU.mult).then_inc(v_kept, 1)

            pool.wait_ge(const_in, 32)
            for t in range(TILES):
                pool.tensor_copy(mask8[:, t, :].rearrange("p (h k) -> p h k", h=PAIRS),
                                 mask[:, t:t + 1, :].to_broadcast([P, PAIRS, 2 * WIN])).then_inc(mask_done, 1)
            with pool.Fori(0, B) as b:
                ln.reciprocal_deviation(pool, b)
            with pool.Fori(0, LAYERS) as l:
                first = l * NT
                pool.wait_ge(tables, 4 * l + 4)
                for w in (1, 0):
                    reciprocal_norms(first, w)
                rotate(first, 0)
                for w in (1, 0):
                    reciprocal_norms(first + 1, w)
                with pool.Fori(0, NT - 2) as i:
                    rotate(first + i + 1, i + 1)
                    keep_values(first + i)
                    for w in (1, 0):
                        reciprocal_norms(first + i + 2, w)
                rotate(first + NT - 1, NT - 1)
                keep_values(first + NT - 2)
                keep_values(first + NT - 1)
                with pool.Fori(0, B) as b:
                    ln.reciprocal_deviation(pool, B * l + b + B)


def causal(nc, shared, ins):
    with ExitStack() as ctx:
        mem = Memory(nc, ctx, "cau")
        scale = float(DH) ** -0.5
        diag_in, diag = mem.sb("diag_in", [P, P]), mem.sb("diag", [P, P], BF16)
        xf = mem.sb("xf", [P, T])
        xn = mem.sb("xn", [P, T])
        w_head = mem.sb("w_head", [P, P])
        xa = mem.sb("xa", [P, T])
        u = mem.sb("u", [P, TILES, P])
        probs = mem.sb("probs", [P, TILES, T])
        pT = mem.sb("pT", [P, TILES, T])
        top = mem.sb("top", [P, TILES])
        bias = mem.sb("bias", [P, TILES])
        total = mem.sb("total", [P, TILES])
        rtotal = mem.sb("rtotal", [P, TILES])
        y = mem.sb("y", [P, TILES, P])
        sc = [mem.bank(f"scores{k}") for k in range(3)]
        tr = [mem.bank(f"turn{k}") for k in range(3)]
        out_ps, in_ps = mem.bank("out"), mem.bank("in")
        ln = LayerNorm(mem, shared, in_ps, in_ps)
        ROW = {3: (0, 0), 0: (1, 0), 2: (1, P), 1: (2, 0)}
        COL = {0: (0, 0), 1: (1, 0), 3: (1, 3 * P), 2: (2, 0)}
        BANK_ROWS = [[3], [0, 2], [1]]
        BANK_COLS = [[0], [1, 3], [2]]

        s = mem.sem
        const_in, diag_done = s("const_in"), s("diag_done")
        xf_ready, xn_ready = s("xf_ready"), s("xn_ready")
        w_ready = s("w_ready")
        xa_done, xa_out = s("xa_done"), s("xa_out")
        u_done, u_out = s("u_done"), s("u_out")
        scored = s("scored")
        topped, biased = s("topped"), s("biased")
        exped = s("exped")
        inverted = s("inverted")
        p_turned = s("p_turned")
        pT0_out, pT12_out = s("pT0_out"), s("pT12_out")
        mixed, added = s("mixed"), s("added")
        cleared = s("cleared")
        y_turned, xs_out = s("y_turned"), s("xs_out")
        block = ctx.enter_context(nc.Block())

        @block.sync
        def _(sp):
            sp.dma_start(diag_in[:], ins["c_diag"]).then_inc(const_in, 16)

        @block.tensor
        def _(pe):
            def query(m, values):
                pe.wait_ge(w_ready, m + 1)
                pe.wait_ge(u_out, values)
                pe.matmul(in_ps[:], w_head[:], xn[:], start=True, stop=True).then_inc(xa_done, 1)

            def score(m):
                pe.wait_ge(xa_out, m + 1)
                pe.wait_ge(exped, 4 * m)
                for k, rows in enumerate(BANK_ROWS):
                    for i in rows:
                        c0, keys = ROW[i][1], (i + 1) * P
                        pe.matmul(sc[k][:, c0:c0 + keys], xa[:, i * P:(i + 1) * P], xn[:, 0:keys],
                                  start=True, stop=False, skip_group_check=True)
                        mm = pe.matmul(sc[k][:, c0 + i * P:c0 + keys], shared.identb[:], diag[:],
                                       start=False, stop=True, skip_group_check=True)
                    mm.then_inc(scored, 1)

            def turn(m):
                pe.wait_ge(exped, 4 * m + 4)
                pe.wait_ge(pT0_out, m)
                pe.wait_ge(pT12_out, 3 * m)
                for k, cols in enumerate(BANK_COLS):
                    for j in cols:
                        for i in range(j, TILES):
                            c0 = COL[j][1] + (i - j) * P
                            tp = pe.transpose(tr[k][:, c0:c0 + P], probs[:, i, j * P:(j + 1) * P], shared.ident[:])
                    tp.then_inc(p_turned, 1)

            def value(m, h):
                for t in range(TILES):
                    w = shared.w_value[:, h, :] if isinstance(h, int) else \
                        shared.w_value[:, bass.ds(h, 1), :].rearrange("p o d -> p (o d)")
                    mm = pe.matmul(in_ps[:, t * P:(t + 1) * P], xn[:, t * P:(t + 1) * P], w,
                                   start=True, stop=True, skip_group_check=True)
                mm.then_inc(u_done, 1)

            def mix(m):
                pe.wait_ge(u_out, m + 1)
                pe.wait_ge(pT0_out, m + 1)
                pe.wait_ge(pT12_out, 3 * m + 3)
                pe.wait_ge(added, 4 * m)
                for i in range(TILES):
                    for j in range(i + 1):
                        mm = pe.matmul(out_ps[:, i * P:(i + 1) * P], pT[:, j, i * P:(i + 1) * P], u[:, j, :],
                                       start=(j == 0), stop=(j == i), skip_group_check=True)
                mm.then_inc(mixed, 1)

            pe.wait_ge(diag_done, 1)
            def head(m, h):
                query(m + 1, m)
                turn(m)
                pe.wait_ge(xa_out, m + 2)
                value(m, h)

            def sequence(b, following):
                m0 = HEADS * b
                with pe.Fori(0, HEADS - 2) as h:
                    head(m0 + h, h)
                    score(m0 + h + 1)
                    mix(m0 + h)
                m = m0 + HEADS - 2
                head(m, HEADS - 2)
                if following:
                    pe.wait_ge(xf_ready, b + 2)
                    pe.wait_ge(u_out, m + 1)
                    ln.turn_in(pe, b + 1, xf)
                score(m + 1)
                mix(m)
                m = m0 + HEADS - 1
                turn(m)
                if following:
                    pe.wait_ge(ln.hat_done, TILES * b + 2 * TILES)
                value(m, HEADS - 1)
                if following:
                    pe.wait_ge(u_out, m + 1)
                    ln.turn_back(pe, b + 1)
                mix(m)
                if following:
                    pe.wait_ge(xn_ready, b + 2)
                    query(m + 1, m + 1)
                pe.wait_ge(added, 4 * m + 4)
                for t in range(TILES):
                    tp = pe.transpose(out_ps[:, t * P:(t + 1) * P], y[:, t, :], shared.ident[:])
                tp.then_inc(y_turned, 1)
                if following:
                    score(m + 1)
                    pe.wait_ge(xs_out, b + 1)

            pe.wait_ge(xf_ready, 1)
            ln.turn_in(pe, 0, xf)
            ln.turn_back(pe, 0)
            pe.wait_ge(xn_ready, 1)
            query(0, 0)
            score(0)
            with pe.Fori(0, B - 1) as b:
                sequence(b, True)
            sequence(B - 1, False)

        @block.scalar
        def _(act):
            def query_out(m):
                act.wait_ge(xa_done, m + 1)
                act.wait_ge(scored, 3 * m)
                act.copy(xa[:], in_ps[:]).then_inc(xa_out, 1)

            def exponentials(m):
                act.wait_ge(biased, m + 1)
                act.wait_ge(p_turned, 3 * m)
                act.wait_ge(inverted, m)
                for k in range(3):
                    for i in BANK_ROWS[k]:
                        c0, keys = ROW[i][1], (i + 1) * P
                        act.activation(probs[:, i, 0:keys], sc[k][:, c0:c0 + keys], ACT.Exp, bias=bias[:, i:i + 1],
                                       scale=scale, accum_out=total[:, i:i + 1]).then_inc(exped, 1)

            def values_out(m):
                act.wait_ge(p_turned, 3 * m + 1)
                act.wait_ge(mixed, m)
                act.copy(pT[:, 0, :], tr[0][:]).then_inc(pT0_out, 1)
                act.wait_ge(u_done, m + 1)
                act.copy(u[:].rearrange("p t d -> p (t d)"), in_ps[:]).then_inc(u_out, 1)

            def take(b, at):
                act.wait_ge(ln.turned, b)
                act.copy(xf[:], shared.xs[:, at]).then_inc(xf_ready, 1)

            def normalised_out(b):
                act.wait_ge(ln.back, b + 1)
                act.wait_ge(u_done, HEADS * b)
                act.wait_ge(scored, 3 * HEADS * b)
                act.copy(xn[:], in_ps[:]).then_inc(xn_ready, 1)

            def sequence(b, following):
                m0 = HEADS * b
                with act.Fori(0, HEADS - 2) as h:
                    query_out(m0 + h + 1)
                    values_out(m0 + h)
                    exponentials(m0 + h + 1)
                m = m0 + HEADS - 2
                if following:
                    take(b + 1, bass.ds(b * T + T, T))
                query_out(m + 1)
                values_out(m)
                exponentials(m + 1)
                values_out(m + 1)
                if following:
                    normalised_out(b + 1)
                    query_out(m + 2)
                    exponentials(m + 2)

            take(0, slice(0, T))
            normalised_out(0)
            query_out(0)
            exponentials(0)
            with act.Fori(0, B - 1) as b:
                sequence(b, True)
            sequence(B - 1, False)

        @block.vector
        def _(dve):
            def maxima(m):
                dve.wait_ge(biased, m)
                for k in range(3):
                    dve.wait_ge(scored, 3 * m + k + 1)
                    for i in BANK_ROWS[k]:
                        c0, keys = ROW[i][1], (i + 1) * P
                        dve.tensor_reduce(top[:, i:i + 1], sc[k][:, c0:c0 + keys], AX.X, ALU.max).then_inc(topped, 1)
                dve.wait_ge(topped, 4 * m + 4)
                dve.wait_ge(exped, 4 * m)
                dve.tensor_scalar(bias[:], top[:], -scale, None, ALU.mult).then_inc(biased, 1)

            def invert(m):
                dve.wait_ge(exped, 4 * m + 4)
                dve.wait_ge(added, 4 * m)
                dve.reciprocal(rtotal[:], total[:]).then_inc(inverted, 1)

            def turned_out(m):
                dve.wait_ge(mixed, m)
                dve.wait_ge(p_turned, 3 * m + 2)
                dve.tensor_copy(pT[:, 1, P:T], tr[1][:, 0:3 * P]).then_inc(pT12_out, 1)
                dve.tensor_copy(pT[:, 3, 3 * P:T], tr[1][:, 3 * P:T]).then_inc(pT12_out, 1)
                dve.wait_ge(p_turned, 3 * m + 3)
                dve.tensor_copy(pT[:, 2, 2 * P:T], tr[2][:, 0:2 * P]).then_inc(pT12_out, 1)

            def add(m):
                dve.wait_ge(mixed, m + 1)
                dve.wait_ge(inverted, m + 1)
                dve.wait_ge(added, 4 * m)
                for t in range(TILES):
                    dve.scalar_tensor_tensor(y[:, t, :], out_ps[:, t * P:(t + 1) * P], rtotal[:, t:t + 1], y[:, t, :],
                                             ALU.mult, ALU.add).then_inc(added, 1)

            dve.wait_ge(const_in, 16)
            dve.tensor_copy(diag[:], diag_in[:]).then_inc(diag_done, 1)
            def clear(b):
                dve.wait_ge(y_turned, b)
                dve.memset(y[:], 0.0).then_inc(cleared, 1)
                dve.wait_ge(cleared, b + 1)

            def sequence(b, following):
                m0 = HEADS * b
                with dve.Fori(0, HEADS - 2) as h:
                    turned_out(m0 + h)
                    maxima(m0 + h + 1)
                    add(m0 + h)
                    invert(m0 + h + 1)
                m = m0 + HEADS - 2
                turned_out(m)
                if following:
                    ln.statistics(dve, b + 1)
                maxima(m + 1)
                if following:
                    dve.wait_ge(ln.back, b + 1)
                    ln.normalise(dve, b + 1)
                add(m)
                invert(m + 1)
                turned_out(m + 1)
                add(m + 1)
                dve.wait_ge(y_turned, b + 1)
                dve.tensor_tensor(shared.xs[:, bass.ds(b * T, T)], shared.xs[:, bass.ds(b * T, T)], out_ps[:],
                                  ALU.add).then_inc(xs_out, 1)
                if following:
                    clear(b + 1)
                    maxima(m + 2)
                    invert(m + 2)

            ln.statistics(dve, 0)
            ln.normalise(dve, 0)
            clear(0)
            maxima(0)
            invert(0)
            with dve.Fori(0, B - 1) as b:
                sequence(b, True)
            sequence(B - 1, False)

        @block.gpsimd
        def _(pool):
            def heads(b):
                with pool.Fori(0, HEADS) as h:
                    pool.wait_ge(xa_done, HEADS * b + h)
                    pool.tensor_copy(w_head[:], shared.w_score[:, bass.ds(h, 1), :].rearrange("p o d -> p (o d)")).then_inc(w_ready, 1)

            ln.reciprocal_deviation(pool, 0)
            with pool.Fori(0, B - 1) as b:
                heads(b)
                ln.reciprocal_deviation(pool, b + 1)
            heads(B - 1)


STAGES = 9
HIDDEN = 4 * D
HCH = HIDDEN // P


def fold_weights(nc, shared, ins):
    with ExitStack() as ctx:
        mem = Memory(nc, ctx, "fly")
        w_up = mem.sb("w_up", [P, STAGES, HIDDEN // 2, 2, 2])
        w_down = mem.sb("w_down", [P, STAGES, HIDDEN // 2, 2, 2])
        up = mem.sb("up", [P, 2, HIDDEN])
        up_same, up_cross = mem.sb("up_same", [P, 2, HIDDEN]), mem.sb("up_cross", [P, 2, HIDDEN])
        w_con = mem.sb("w_con", [P, HCH, P])
        down = mem.sb("down", [P, 1, HIDDEN])
        dn_same, dn_cross = mem.sb("dn_same", [P, 1, HIDDEN]), mem.sb("dn_cross", [P, 1, HIDDEN])
        bias_in = mem.sb("bias_in", [P, HCH + 2])
        raw = mem.sb("raw", [P, 4, HEADS, DH])
        turned_w = mem.sb("turned_w", [P, 4, PAIRS, P])
        ps = [mem.bank(f"ps{k}") for k in range(4)]
        prod = [mem.bank(f"prod{k}") for k in range(4)]
        con_ps, turn_ps, bias_ps = ps[:3]
        s = mem.sem
        loaded = s("loaded")
        head_turned, taken = s("head_turned"), s("taken")
        folded, kept = s("folded"), s("kept")
        up_in, down_in, bias_loaded = s("up_in"), s("down_in"), s("bias_loaded")
        cleared, con_turned, con_out = s("cleared"), s("con_turned"), s("con_out")
        up_parts, up_steps, dn_parts, dn_steps = s("up_parts"), s("up_steps"), s("dn_parts"), s("dn_steps")
        turned, bias_turned, done = s("turned"), s("bias_turned"), s("done")
        block = ctx.enter_context(nc.Block())

        def butterfly(eng, cur, same, cross, w, order, transposed, parts, steps):
            blocks = cur.shape[1]
            for n, stage in enumerate(order):
                st = 2 ** stage
                pair = lambda a, half: a[:].rearrange("p k (n two s) -> p k n two s", two=2, s=st)[:, :, :, half, :]

                def weight(o, i):
                    v = w[:, stage, :, o, i].rearrange("p (k n s) -> p k n s", k=1, s=st)
                    return v.to_broadcast([P, blocks, HIDDEN // 2 // st, st])

                eng.wait_ge(steps, n)
                for o in range(2):
                    i = 1 - o
                    eng.tensor_tensor(pair(same, o), pair(cur, o), weight(o, o), ALU.mult).then_inc(parts, 1)
                    eng.tensor_tensor(pair(cross, o), pair(cur, i), weight(*((i, o) if transposed else (o, i))),
                                      ALU.mult).then_inc(parts, 1)
                eng.wait_ge(parts, 4 * n + 4)
                eng.tensor_tensor(cur[:], same[:], cross[:], ALU.add).then_inc(steps, 1)

        @block.sync
        def _(sp):
            for w, name in enumerate(("L1_attn_P_q", "L1_attn_P_k", "L1_attn_P_v", "L1_attn_P_o")):
                sp.dma_start(raw[:, w, :, :], ins[name].rearrange("h d k -> d h k")).then_inc(loaded, 16)
            def on_every_partition(w, name, done):
                src = ins[name].rearrange("(q s) k a b -> q (s k a b)", q=1)
                sp.dma_start(w[:].rearrange("p s k a b -> p (s k a b)"), src.to_broadcast([P, STAGES * 2 * HIDDEN])).then_inc(done, 16)

            sp.dma_start(w_con[:], ins["L0_ffn_W_con"].rearrange("(c p) d -> p c d", p=P)).then_inc(down_in, 16)
            on_every_partition(w_down, "L0_ffn_down_weights", down_in)
            sp.wait_ge(cleared, 1)
            sp.dma_start(up[:, 0, :], ins["L0_ffn_W_exp"]).then_inc(up_in, 16)
            sp.dma_start(up[0:1, 1, :], ins["L0_ffn_b_exp"].rearrange("(o h) -> o h", o=1)).then_inc(up_in, 16)
            on_every_partition(w_up, "L0_ffn_up_weights", up_in)
            sp.dma_start(bias_in[:, 0:HCH], ins["L0_ffn_up_bias"].rearrange("(c p) -> p c", p=P), allow_slow_non_contiguous=True).then_inc(bias_loaded, 16)
            for k, name in enumerate(("L0_ffn_b_con", "L0_ffn_down_bias")):
                sp.dma_start(bias_in[:, HCH + k:HCH + k + 1], ins[name].rearrange("(p o) -> p o", o=1)).then_inc(bias_loaded, 16)

        @block.tensor
        def _(pe):
            pe.wait_ge(loaded, 16 * 4)
            for n in range(8):
                w, half = n // 2, n % 2
                if n >= 4:
                    pe.wait_ge(taken, n - 3)
                for q in range(4):
                    first = 8 * half + 2 * q
                    turn = pe.transpose(ps[n % 4][:, q * P:(q + 1) * P],
                                        raw[:, w, first:first + 2, :].rearrange("p h k -> p (h k)"), shared.ident[:])
                turn.then_inc(head_turned, 1)
            pe.wait_ge(taken, 8)
            for n in range(HEADS):
                q, h = n // 2, n % 2
                if q >= 2:
                    pe.wait_ge(kept, 4 * (q - 1))
                half = slice(64 * h, 64 * h + 64)
                for w in range(2):
                    mm = pe.matmul(prod[n % 4][:, w * P:(w + 1) * P],
                                   turned_w[half, 2 * w, q, :], turned_w[half, 2 * w + 1, q, :],
                                   start=True, stop=True, skip_group_check=True)
                mm.then_inc(folded, 1)
            pe.wait_ge(down_in, 32)
            for c in range(HCH):
                turn = pe.transpose(con_ps[:, c * P:(c + 1) * P], w_con[:, c, :], shared.ident[:])
            turn.then_inc(con_turned, 1)
            pe.wait_ge(up_steps, STAGES)
            for c in range(HCH):
                mm = pe.matmul(bias_ps[:, c:c + 1], up[0:1, 1, c * P:(c + 1) * P], shared.ident[0:1, 0:1],
                               start=True, stop=True, skip_group_check=True)
            mm.then_inc(bias_turned, 1)
            pe.wait_ge(dn_steps, STAGES)
            for c in range(HCH):
                turn = pe.transpose(turn_ps[:, c * P:(c + 1) * P], down[:, 0, c * P:(c + 1) * P], shared.ident[:])
            turn.then_inc(turned, 1)

        @block.scalar
        def _(act):
            act.wait_ge(con_turned, 1)
            act.copy(down[:, 0, :], con_ps[:]).then_inc(con_out, 1)
            act.wait_ge(turned, 1)
            act.copy(shared.w_down[:].rearrange("p c d -> p (c d)"), turn_ps[:]).then_inc(done, 1)
            act.wait_ge(up_steps, STAGES)
            act.copy(shared.w_up[:], up[:, 0, :]).then_inc(done, 1)

        @block.vector
        def _(dve):
            dve.memset(up[:], 0.0).then_inc(cleared, 1)
            for n in range(8):
                dve.wait_ge(head_turned, n + 1)
                dve.tensor_copy(turned_w[:, n // 2, 4 * (n % 2):4 * (n % 2) + 4, :].rearrange("p q d -> p (q d)"),
                                ps[n % 4][:]).then_inc(taken, 1)
            for n in range(HEADS):
                dve.wait_ge(folded, n + 1)
                for w, dst in enumerate((shared.w_score, shared.w_value)):
                    dve.tensor_copy(dst[:, n, :], prod[n % 4][:, w * P:(w + 1) * P]).then_inc(kept, 1)
            dve.wait_ge(up_in, 16 * 3)
            butterfly(dve, up, up_same, up_cross, w_up, range(STAGES), False, up_parts, up_steps)
            dve.wait_ge(bias_loaded, 16 * 3)
            dve.wait_ge(bias_turned, 1)
            dve.tensor_tensor(shared.up_bias[:], bias_ps[:, 0:HCH], bias_in[:, 0:HCH], ALU.add).then_inc(done, 1)
            dve.tensor_tensor(shared.down_bias[:], bias_in[:, HCH:HCH + 1], bias_in[:, HCH + 1:HCH + 2], ALU.add).then_inc(done, 1)

        @block.gpsimd
        def _(pool):
            pool.wait_ge(down_in, 32)
            pool.wait_ge(con_out, 1)
            butterfly(pool, down, dn_same, dn_cross, w_down, range(STAGES - 1, -1, -1), True, dn_parts, dn_steps)


def rwkv_ffn(nc, shared, ins):
    with ExitStack() as ctx:
        mem = Memory(nc, ctx, "rwkv")
        K_CLAMP, K_EPS = 60.0, 1e-8
        w_kvr = mem.sb("w_kvr", [P, 3, HIDDEN])
        w_o = mem.sb("w_o", [P, HCH, P])
        c_k, c_v, c_r = mem.sb("c_k", [P, HIDDEN]), mem.sb("c_v", [P, HCH, P]), mem.sb("c_r", [P, P])
        row_g, row_b = mem.sb("row_g", [P, 1, P]), mem.sb("row_b", [P, 1, P])
        VEC = ("pre_g", "pre_b", "post_g", "post_b", "tm_mix_k", "tm_mix_v", "tm_mix_r", "cm_mix_k", "cm_mix_r")
        vec = mem.sb("vec", [P, len(VEC)])
        rest = mem.sb("rest", [P, 5])
        time = mem.sb("time", [P, 2, HCH])
        timed = mem.sb("timed", [P, 2, HCH])
        growth = mem.sb("growth", [P, HCH])
        rows = mem.sb("rows", [P, TILES, P])
        z1, z2, z3 = (mem.sb(n, [P, TILES, P]) for n in ("z1", "z2", "z3"))
        x0T = mem.sb("x0T", [P, T])
        xa = mem.sb("xa", [P, T])
        xb, xb_in = mem.sb("xb", [P, T]), mem.sb("xb_in", [P, T])
        xc = mem.sb("xc", [P, T])
        xd = mem.sb("xd", [P, T])
        xn, xn_c = mem.sb("xn", [P, 1 + T]), mem.sb("xn_c", [P, 1 + T])
        late, late_c = mem.sb("late", [P, 3, T]), mem.sb("late_c", [P, 2, T])
        mixed_in, mixed_c = mem.sb("mixed_in", [P, 3, T]), mem.sb("mixed_c", [P, 2, T])
        low = mem.sb("low", [P, 2, T])
        key, kv = mem.sb("key", [P, 2, T]), mem.sb("kv", [P, 2, T])
        gate = mem.sb("gate", [P, 2, T])
        gate1, numer = mem.sb("gate1", [P, T]), mem.sb("numer", [P, T])
        sk, skv = mem.sb("sk", [P, 1 + T]), mem.sb("skv", [P, 1 + T])
        wk, wkv, den, rden = (mem.sb(n, [P, T]) for n in ("wk", "wkv", "den", "rden"))
        out_c = mem.sb("out_c", [P, HCH, T])
        hid = mem.sb("hid", [P, HCH, T])
        sig = mem.sb("sig", [P, T])
        xnf = mem.sb("xnf", [P, T])
        k_ps, v_ps, r_ps, o_ps = mem.bank("k"), mem.bank("v"), mem.bank("r"), mem.bank("o")
        tok_ps, up_ps, y_ps = mem.bank("tok"), [mem.bank("up0"), mem.bank("up1")], mem.bank("y")
        lns = LayerNorm(mem, shared, tok_ps, r_ps)
        mem.prefix = "rwkvf"
        lnf = LayerNorm(mem, shared, tok_ps, up_ps[1])
        mem.prefix = "rwkv"

        s = mem.sem
        w_in, x_in = s("w_in"), s("x_in")
        prep = s("prep")
        time_exp = s("time_exp")
        scaled, xa_tok = s("scaled"), s("xa_tok")
        x_turned, z_turned = s("x_turned"), s("z_turned")
        x0_out, xa_out = s("x0_out"), s("xa_out")
        xn_out, late_out, blended = s("xn_out"), s("late_out"), s("blended")
        kvr = s("kvr")
        lowed, keyed, gated, gated1 = s("lowed"), s("keyed"), s("gated"), s("gated1")
        kv_done, scanned, firsts = s("kv_done"), s("scanned"), s("firsts")
        den_done, rden_done = s("den_done"), s("rden_done")
        numerated, out_done = s("numerated"), s("out_done")
        o_done, xb_done, xb_in_done = s("o_done"), s("xb_done"), s("xb_in_done")
        xn_c_out, late_c_out, blended_c = s("xn_c_out"), s("late_c_out"), s("blended_c")
        up_done, hid_done = s("up_done"), s("hid_done")
        cr_done, sig_done, y_done = s("cr_done"), s("sig_done"), s("y_done")
        xc_done, xd_done, xnf_out, xs_out = s("xc_done"), s("xd_done"), s("xnf_out"), s("xs_out")
        WLOADS = 3 + 1 + 3 + 2 + len(VEC) + 2
        block = ctx.enter_context(nc.Block())

        def rounds(engine, both):
            both(0, None)
            with engine.Fori(0, B - 1) as b:
                both(b + 1, b)
            both(None, B - 1)

        @block.sync
        def _(sp):
            name = lambda n: ins["L0_attn_" + n]
            sp.dma_start(rows[:], ins["L0_attn_x"][0].rearrange("(t p) d -> p t d", p=P)).then_inc(x_in, 16)
            for k, v in enumerate(("tm_decay", "tm_first")):
                sp.dma_start(time[:, k, :], name(v).rearrange("(c p) -> p c", p=P), allow_slow_non_contiguous=True).then_inc(w_in, 16)
            for dst, v in ((row_g, "ln0_g"), (row_b, "ln0_b")):
                sp.dma_start(dst[:, 0, :], name(v).rearrange("(o d) -> o d", o=1).to_broadcast([P, D])).then_inc(w_in, 16)
            for k, v in enumerate(("tm_Wk", "tm_Wv", "tm_Wr")):
                sp.dma_start(w_kvr[:, k, :], name(v)).then_inc(w_in, 16)
            sp.dma_start(w_o[:], name("tm_Wo").rearrange("(c p) d -> p c d", p=P)).then_inc(w_in, 16)
            sp.dma_start(c_k[:], name("cm_Wk")).then_inc(w_in, 16)
            sp.dma_start(c_v[:], name("cm_Wv").rearrange("(c p) d -> p c d", p=P)).then_inc(w_in, 16)
            sp.dma_start(c_r[:], name("cm_Wr")).then_inc(w_in, 16)
            with sp.Fori(1, B) as b:
                sp.wait_ge(lns.back, b)
                src = ins["L0_attn_x"][bass.ds(b, 1)].rearrange("o (t p) d -> p (o t) d", p=P)
                sp.dma_start(rows[:], src).then_inc(x_in, 16)

        @block.tensor
        def _(pe):
            def turn_input(a):
                pe.wait_ge(x_in, 16 * a + 16)
                pe.wait_ge(lowed, HCH * a)
                for t in range(TILES):
                    turn = pe.transpose(k_ps[:, t * P:(t + 1) * P], rows[:, t, :], shared.ident[:])
                turn.then_inc(x_turned, 1)

            def turn_stream(a):
                pe.wait_ge(xa_tok, a + 1)
                pe.wait_ge(kv_done, HCH * a)
                for t in range(TILES):
                    turn = pe.transpose(v_ps[:, t * P:(t + 1) * P], z3[:, t, :], shared.ident[:])
                turn.then_inc(z_turned, 1)

            def turn_normalised(a):
                pe.wait_ge(gated, HCH * a)
                lns.turn_back(pe, 3 * a + 2)

            def project_chunk(a, c):
                if c == 0:
                    pe.wait_ge(x0_out, a + 1)
                    pe.wait_ge(xa_out, a + 1)
                for j, (bank, read) in enumerate(((k_ps, lowed), (v_ps, kv_done), (r_ps, gated))):
                    if c == 0:
                        pe.wait_ge(blended, 3 * a + j + 1)
                    else:
                        pe.wait_ge(read, HCH * a + c)
                    pe.matmul(bank[:], w_kvr[:, j, c * P:(c + 1) * P], mixed_in[:, j, :],
                              start=True, stop=True).then_inc(kvr, 1)

            def project_time(a):
                pe.wait_ge(xb_done, a)
                for c in range(HCH):
                    pe.wait_ge(out_done, HCH * a + c + 1)
                    mm = pe.matmul(o_ps[:], w_o[:, c, :], out_c[:, c, :], start=(c == 0), stop=(c == HCH - 1))
                mm.then_inc(o_done, 1)

            def turn_xb_in(b):
                pe.wait_ge(xb_done, b + 1)
                lnf.turn_in(pe, 2 * b, xb)

            def turn_xb_back(b):
                pe.wait_ge(hid_done, 8 * b)
                lnf.turn_back(pe, 2 * b)

            def channel_up(b, chunks):
                if 0 in chunks:
                    pe.wait_ge(blended_c, 2 * b + 2)
                    pe.matmul(tok_ps[:], c_r[:], mixed_c[:, 1, :], start=True, stop=True).then_inc(cr_done, 1)
                for c in chunks:
                    if c >= 2:
                        pe.wait_ge(hid_done, 8 * b + c - 1)
                    pe.matmul(up_ps[c % 2][:], c_k[:, c * P:(c + 1) * P], mixed_c[:, 0, :], start=True, stop=True).then_inc(up_done, 1)

            def channel_down(b):
                pe.wait_ge(xs_out, b)
                for c in range(HCH):
                    pe.wait_ge(hid_done, 8 * b + c + 1)
                    mm = pe.matmul(y_ps[:], c_v[:, c, :], hid[:, c, :], start=(c == 0), stop=(c == HCH - 1))
                mm.then_inc(y_done, 1)

            def turn_xd_in(b):
                pe.wait_ge(xd_done, b + 1)
                pe.wait_ge(sig_done, b + 1)
                lnf.turn_in(pe, 2 * b + 1, xd)

            def ffn_up(b):
                pe.wait_ge(hid_done, 8 * b + 4)
                lnf.turn_back(pe, 2 * b + 1)
                pe.wait_ge(xnf_out, b + 1)
                for c in range(HCH):
                    if c >= 2:
                        pe.wait_ge(hid_done, 8 * b + 4 + c - 1)
                    pe.matmul(up_ps[c % 2][:], shared.w_up[:, c * P:(c + 1) * P], xnf[:], start=True, stop=True).then_inc(up_done, 1)

            def ffn_down(b):
                pe.wait_ge(xd_done, b + 1)
                for c in range(HCH):
                    pe.wait_ge(hid_done, 8 * b + 4 + c + 1)
                    mm = pe.matmul(y_ps[:], shared.w_down[:, c, :], hid[:, c, :], start=(c == 0), stop=(c == HCH - 1))
                mm.then_inc(y_done, 1)

            def both(a, b):
                if a is not None:
                    turn_input(a)
                if b is not None:
                    turn_xb_in(b)
                    turn_xb_back(b)
                if a is not None:
                    turn_stream(a)
                if b is not None:
                    channel_up(b, (0, 1))
                if a is not None:
                    turn_normalised(a)
                if b is not None:
                    channel_up(b, (2, 3))
                if a is not None:
                    project_chunk(a, 0)
                if b is not None:
                    channel_down(b)
                if a is not None:
                    project_chunk(a, 1)
                if b is not None:
                    turn_xd_in(b)
                if a is not None:
                    project_chunk(a, 2)
                    project_chunk(a, 3)
                if b is not None:
                    ffn_up(b)
                if a is not None:
                    project_time(a)
                if b is not None:
                    ffn_down(b)

            pe.wait_ge(w_in, 16 * WLOADS)
            rounds(pe, both)

        @block.scalar
        def _(act):
            def spread(bank, g, out, shifted, first_rest, out_sem, shifted_sem, n, used):
                count = shifted.shape[1]
                act.wait_ge(used, count * n)
                act.activation(out[:, 1:], bank[:], ACT.Identity, bias=vec[:, g + 1:g + 2],
                               scale=vec[:, g:g + 1]).then_inc(out_sem, 1)
                act.wait_ge(out_sem, n + 1)
                for j in range(count):
                    k = first_rest + j
                    act.activation(shifted[:, j, :], out[:, 0:T], ACT.Copy, scale=rest[:, k:k + 1]).then_inc(shifted_sem, 1)

            def input_out(a):
                act.wait_ge(x_turned, a + 1)
                act.wait_ge(xb_in_done, a)
                act.copy(x0T[:], k_ps[:]).then_inc(x0_out, 1)

            def stream_out(a):
                act.wait_ge(z_turned, a + 1)
                act.wait_ge(xb_done, a)
                act.copy(xa[:], v_ps[:]).then_inc(xa_out, 1)

            def time_inputs(a):
                act.wait_ge(lns.back, a + 1)
                spread(lns.feat, 0, xn, late, 0, xn_out, late_out, a, blended)

            def chunk(a, c):
                act.wait_ge(lowed, HCH * a + c + 1)
                if c >= 2:
                    act.wait_ge(firsts, 8 * a + 2 * c - 2)
                    act.wait_ge(gated1, HCH * a + c - 1)
                act.activation(key[:, c % 2, :], low[:, c % 2, :], ACT.Exp).then_inc(keyed, 1)
                act.wait_ge(kvr, 12 * a + 3 * c + 3)
                act.activation(gate[:, c % 2, :], r_ps[:], ACT.Tanh, scale=0.5).then_inc(gated, 1)

            def channel_inputs(b):
                act.wait_ge(lnf.back, 2 * b + 1)
                spread(lnf.feat, 2, xn_c, late_c, 3, xn_c_out, late_c_out, b, blended_c)

            def channel_hidden(b, chunks):
                act.wait_ge(y_done, 2 * b)
                for c in chunks:
                    act.wait_ge(up_done, 8 * b + c + 1)
                    act.activation(hid[:, c, :], up_ps[c % 2][:], ACT.Silu).then_inc(hid_done, 1)

            def channel_gate(b):
                act.wait_ge(cr_done, b + 1)
                act.wait_ge(xc_done, b)
                act.activation(sig[:], tok_ps[:], ACT.Tanh, scale=0.5).then_inc(sig_done, 1)

            def ffn_input(b):
                act.wait_ge(lnf.back, 2 * b + 2)
                act.copy(xnf[:], lnf.feat[:]).then_inc(xnf_out, 1)

            def ffn_hidden(b):
                act.wait_ge(y_done, 2 * b + 1)
                for c in range(HCH):
                    act.wait_ge(up_done, 8 * b + 4 + c + 1)
                    act.activation(hid[:, c, :], up_ps[c % 2][:], ACT.Gelu, bias=shared.up_bias[:, c:c + 1]).then_inc(hid_done, 1)

            def both(a, b):
                if a is not None:
                    input_out(a)
                if b is not None:
                    channel_inputs(b)
                if a is not None:
                    stream_out(a)
                if b is not None:
                    channel_gate(b)
                    channel_hidden(b, (0, 1))
                if a is not None:
                    time_inputs(a)
                if b is not None:
                    channel_hidden(b, (2, 3))
                if a is not None:
                    for c in range(HCH):
                        chunk(a, c)
                if b is not None:
                    ffn_input(b)
                    ffn_hidden(b)

            for k, v in enumerate(VEC):
                act.dma_start(vec[:, k:k + 1], ins["L0_attn_" + v].rearrange("(p o) -> p o", o=1)).then_inc(w_in, 16)
            act.wait_ge(w_in, 16 * WLOADS)
            act.activation(growth[:], time[:, 0, :], ACT.Exp).then_inc(time_exp, 1)
            act.activation(timed[:, 1, :], time[:, 1, :], ACT.Exp).then_inc(time_exp, 1)
            act.wait_ge(time_exp, 2)
            act.activation(timed[:, 0, :], growth[:], ACT.Exp, scale=-1.0).then_inc(time_exp, 1)
            act.wait_ge(prep, 5)
            rounds(act, both)

        @block.vector
        def _(dve):
            def blend(stream, shifted, out, first_mix, shifted_sem, out_sem, n):
                count = shifted.shape[1]
                for j in range(count):
                    k = 4 + first_mix + j
                    dve.wait_ge(shifted_sem, count * n + j + 1)
                    dve.scalar_tensor_tensor(out[:, j, :], stream[:, 1:], vec[:, k:k + 1], shifted[:, j, :],
                                             ALU.mult, ALU.add).then_inc(out_sem, 1)

            def chunk(a, c):
                n = HCH * a + c
                dve.wait_ge(kvr, 12 * a + 3 * c + 1)
                if c >= 2:
                    dve.wait_ge(keyed, HCH * a + c - 1)
                dve.tensor_scalar(low[:, c % 2, :], k_ps[:], K_CLAMP, None, ALU.min).then_inc(lowed, 1)
                dve.wait_ge(keyed, n + 1)
                dve.wait_ge(kvr, 12 * a + 3 * c + 2)
                dve.wait_ge(firsts, 2 * n)
                dve.tensor_tensor(kv[:, c % 2, :], key[:, c % 2, :], v_ps[:], ALU.mult).then_inc(kv_done, 1)
                decay = timed[:, 0, c:c + 1].to_broadcast([P, T])
                dve.tensor_tensor_scan(sk[:, 1:], decay, key[:, c % 2, :], 0.0, ALU.mult, ALU.add).then_inc(scanned, 1)
                dve.wait_ge(kv_done, n + 1)
                dve.tensor_tensor_scan(skv[:, 1:], decay, kv[:, c % 2, :], 0.0, ALU.mult, ALU.add).then_inc(scanned, 1)
                dve.wait_ge(scanned, 2 * n + 1)
                dve.wait_ge(den_done, n)
                dve.scalar_tensor_tensor(wk[:], key[:, c % 2, :], timed[:, 1, c:c + 1], sk[:, 0:T],
                                         ALU.mult, ALU.add).then_inc(firsts, 1)
                dve.wait_ge(scanned, 2 * n + 2)
                dve.wait_ge(numerated, n)
                dve.scalar_tensor_tensor(wkv[:], kv[:, c % 2, :], timed[:, 1, c:c + 1], skv[:, 0:T],
                                         ALU.mult, ALU.add).then_inc(firsts, 1)
                dve.wait_ge(firsts, 2 * n + 1)
                dve.wait_ge(rden_done, n)
                dve.tensor_scalar(den[:], wk[:], K_EPS, 2.0, ALU.add, ALU.mult).then_inc(den_done, 1)
                dve.wait_ge(den_done, n + 1)
                dve.wait_ge(out_done, n)
                dve.reciprocal(rden[:], den[:]).then_inc(rden_done, 1)

            def add_ffn(b):
                dve.wait_ge(y_done, 2 * b + 2)
                dve.scalar_tensor_tensor(shared.xs[:, bass.ds(b * T, T)], y_ps[:], shared.down_bias[:], xd[:],
                                         ALU.add, ALU.add).then_inc(xs_out, 1)

            def both(a, b, before):
                u = None if a is None else 3 * a
                if a is not None:
                    dve.wait_ge(x_in, 16 * a + 16)
                    lns.statistics(dve, u, rows)
                if b is not None:
                    dve.wait_ge(o_done, b + 1)
                    dve.wait_ge(lnf.turned, 2 * b)
                    dve.tensor_tensor(xb[:], xa[:], o_ps[:], ALU.add).then_inc(xb_done, 1)
                    dve.wait_ge(xb_done, b + 1)
                    dve.wait_ge(xc_done, b)
                    dve.tensor_tensor(xb_in[:], xb[:], x0T[:], ALU.add).then_inc(xb_in_done, 1)
                    lnf.statistics(dve, 2 * b)
                if before is not None:
                    add_ffn(before)
                if a is not None:
                    dve.wait_ge(xa_tok, a)
                    lns.normalise(dve, u, rows, z1)
                if b is not None:
                    dve.wait_ge(lnf.back, 2 * b)
                    lnf.normalise(dve, 2 * b)
                if a is not None:
                    dve.wait_ge(lns.hat_done, TILES * u + TILES)
                    lns.statistics(dve, u + 1, z1)
                    lns.normalise(dve, u + 1, z1, z2)
                    dve.wait_ge(lns.hat_done, TILES * u + 2 * TILES)
                    dve.wait_ge(z_turned, a)
                    dve.tensor_tensor(z1[:], z2[:], row_g[:].to_broadcast([P, TILES, P]), ALU.mult).then_inc(scaled, 1)
                    dve.wait_ge(scaled, a + 1)
                    dve.tensor_tensor(z3[:], z1[:], row_b[:].to_broadcast([P, TILES, P]), ALU.add).then_inc(xa_tok, 1)
                if b is not None:
                    dve.wait_ge(up_done, 8 * b)
                    dve.wait_ge(cr_done, b)
                    blend(xn_c, late_c, mixed_c, 3, late_c_out, blended_c, b)
                if a is not None:
                    dve.wait_ge(xa_tok, a + 1)
                    lns.statistics(dve, u + 2, z3)
                    dve.wait_ge(lns.back, a)
                    lns.normalise(dve, u + 2, z3)
                    dve.wait_ge(kvr, 12 * a)
                    blend(xn, late, mixed_in, 0, late_out, blended, a)
                    chunk(a, 0)
                if b is not None:
                    dve.wait_ge(sig_done, b + 1)
                    dve.wait_ge(xd_done, b)
                    dve.scalar_tensor_tensor(xc[:], sig[:], 0.5, xb_in[:], ALU.mult, ALU.add).then_inc(xc_done, 1)
                    dve.wait_ge(xc_done, b + 1)
                    dve.wait_ge(y_done, 2 * b + 1)
                    dve.wait_ge(xs_out, b)
                    dve.scalar_tensor_tensor(xd[:], xc[:], 0.5, y_ps[:], ALU.add, ALU.add).then_inc(xd_done, 1)
                    lnf.statistics(dve, 2 * b + 1)
                if a is not None:
                    chunk(a, 1)
                if b is not None:
                    dve.wait_ge(lnf.back, 2 * b + 1)
                    lnf.normalise(dve, 2 * b + 1)
                if a is not None:
                    chunk(a, 2)
                    chunk(a, 3)

            for at in (xn, xn_c, sk, skv):
                dve.memset(at[:, 0:1], 0.0).then_inc(prep, 1)
            dve.wait_ge(w_in, 16 * WLOADS)
            dve.tensor_scalar(rest[:], vec[:, 4:9], -1.0, 1.0, ALU.mult, ALU.add).then_inc(prep, 1)
            dve.wait_ge(prep, 5)
            dve.wait_ge(time_exp, 3)
            both(0, None, None)
            both(1, 0, None)
            with dve.Fori(0, B - 2) as before:
                both(before + 2, before + 1, before)
            both(None, B - 1, B - 2)
            add_ffn(B - 1)

        @block.gpsimd
        def _(pool):
            def chunk(a, c):
                n = HCH * a + c
                pool.wait_ge(gated, n + 1)
                pool.wait_ge(numerated, n)
                pool.tensor_tensor(gate1[:], gate[:, c % 2, :], shared.ones[:].to_broadcast([P, T]), ALU.add).then_inc(gated1, 1)
                pool.wait_ge(gated1, n + 1)
                pool.wait_ge(firsts, 2 * n + 2)
                pool.wait_ge(out_done, n)
                pool.tensor_tensor(numer[:], wkv[:], gate1[:], ALU.mult).then_inc(numerated, 1)
                pool.wait_ge(numerated, n + 1)
                pool.wait_ge(rden_done, n + 1)
                pool.wait_ge(o_done, a)
                pool.tensor_tensor(out_c[:, c, :], numer[:], rden[:], ALU.mult).then_inc(out_done, 1)

            def both(a, b):
                if a is not None:
                    lns.reciprocal_deviation(pool, 3 * a)
                if b is not None:
                    lnf.reciprocal_deviation(pool, 2 * b)
                if a is not None:
                    lns.reciprocal_deviation(pool, 3 * a + 1)
                    lns.reciprocal_deviation(pool, 3 * a + 2)
                    chunk(a, 0)
                if b is not None:
                    lnf.reciprocal_deviation(pool, 2 * b + 1)
                if a is not None:
                    for c in range(1, HCH):
                        chunk(a, c)

            rounds(pool, both)


def constants(nc, shared, ins):
    with ExitStack() as ctx:
        mem = Memory(nc, ctx, "const")
        loaded, set_ = mem.sem("loaded"), mem.sem("set")
        block = ctx.enter_context(nc.Block())

        @block.sync
        def _(sp):
            sp.dma_start(shared.ident[:], ins["c_ident"]).then_inc(loaded, 16)

        @block.vector
        def _(dve):
            dve.wait_ge(loaded, 16)
            dve.tensor_copy(shared.identb[:], shared.ident[:]).then_inc(set_, 1)

        @block.gpsimd
        def _(pool):
            for dst, value in ((shared.minus_half, -0.5), (shared.ones, 1.0)):
                pool.memset(dst[:], value).then_inc(set_, 1)
            pool.wait_ge(set_, 3)


def store(nc, shared, out):
    with ExitStack() as ctx:
        mem = Memory(nc, ctx, "out")
        total = [mem.sb(f"total{k}", [P, T]) for k in range(2)]
        rows = [mem.sb(f"rows{k}", [P, TILES, D]) for k in range(2)]
        ps = [mem.bank(f"ps{k}") for k in range(2)]
        added, turned, copied = mem.sem("added"), mem.sem("turned"), mem.sem("copied")
        stored = [mem.sem(f"stored{k}") for k in range(2)]
        block = ctx.enter_context(nc.Block())

        @block.vector
        def _(dve):
            for b in range(B):
                if b >= 2:
                    dve.wait_ge(turned, b - 1)
                at = LEAD + 1 + b * SEQ
                dve.tensor_tensor(total[b % 2][:], shared.xs[:, b * T:(b + 1) * T], shared.x0[:, at:at + T],
                                  ALU.add).then_inc(added, 1)

        @block.tensor
        def _(pe):
            for b in range(B):
                pe.wait_ge(added, b + 1)
                if b >= 2:
                    pe.wait_ge(copied, b - 1)
                for t in range(TILES):
                    turn = pe.transpose(ps[b % 2][:, t * P:(t + 1) * P], total[b % 2][:, t * P:(t + 1) * P], shared.ident[:])
                turn.then_inc(turned, 1)

        @block.scalar
        def _(act):
            for b in range(B):
                act.wait_ge(turned, b + 1)
                if b >= 2:
                    act.wait_ge(stored[b % 2], 16 * (b // 2))
                act.copy(rows[b % 2][:].rearrange("p t d -> p (t d)"), ps[b % 2][:]).then_inc(copied, 1)

        @block.sync
        def _(sp):
            for b in range(B):
                sp.wait_ge(copied, b + 1)
                sp.dma_start(out[b].rearrange("(t p) d -> p t d", p=P), rows[b % 2][:]).then_inc(stored[b % 2], 16)
            for k in range(2):
                sp.wait_ge(stored[k], 16 * (B // 2))


def build(nc, ins, out):
    with ExitStack() as ctx:
        shared = Shared(Memory(nc, ctx, "all"))
        constants(nc, shared, ins)
        fold_weights(nc, shared, ins)
        rwkv_ffn(nc, shared, ins)
        causal(nc, shared, ins)
        layers(nc, shared, ins)
        store(nc, shared, out)


def _constants():
    ident = np.eye(P, dtype=np.float32)
    p = np.arange(P)[:, None] % WIN
    c = np.arange(2 * WIN)[None, :]
    seen = (c <= p + WIN) & (c >= p)
    mask = np.where(seen, 0.0, MASKED)[:, None, :].repeat(TILES, 1)
    mask[:WIN, 0, :WIN] = MASKED
    diag = np.where(np.arange(P)[None, :] <= np.arange(P)[:, None], 0.0, MASKED)
    half = np.arange(0, DH, 2, dtype=np.float32)
    inv_freq = (1.0 / 10000.0 ** (half / DH)).astype(np.float32)
    t = np.arange(T, dtype=np.float32)
    freqs = np.tile(t[:, None] * inv_freq[None, :], (1, 2)).astype(np.float64)
    base = (half + np.float32(0.4 * DH)) / np.float32(1.4 * DH)
    power = (t - T // 2) / (WIN // 2)
    scale = np.tile(base[None, :].astype(np.float64) ** power[:, None], (1, 2))
    sign = np.where(np.arange(DH) < DH // 2, -1.0, 1.0)
    trig = np.stack([np.stack([np.cos(freqs) * scale, np.cos(freqs) / scale]),
                     np.stack([np.sin(freqs) * scale * sign, np.sin(freqs) / scale * sign])])
    trig = trig.reshape(2, 2, TILES, P, DH).transpose(3, 0, 1, 2, 4)
    return {"c_ident": ident, "c_mask": mask.astype(np.float32), "c_diag": diag.astype(np.float32),
            "c_trig": np.ascontiguousarray(trig, dtype=np.float32)}


def kernel(**inputs):
    import concourse.bacc as bacc
    from concourse.bass_utils import run_bass_kernel_spmd

    nc = bacc.Bacc("TRN2", target_bir_lowering=False, num_devices=1)
    arrays = {name: np.ascontiguousarray(a) for name, a in inputs.items()}
    arrays.update(_constants())
    ins = {name: nc.dram_tensor(name, a.shape, mybir.dt.from_np(a.dtype), kind="ExternalInput").ap()
           for name, a in arrays.items()}
    out = nc.dram_tensor("out", (B, T, D), F32, kind="ExternalOutput").ap()
    build(nc, ins, out)
    return run_bass_kernel_spmd(nc, [arrays], core_ids=[0]).results[0]["out"]
```
